# Optimizing a Trainium2 kernel written in Bass

```python
import numpy as np
import jax
import jax.numpy as jnp

def _softmax(x, axis=-1):
    return jax.nn.softmax(x, axis=axis)

def _gelu(x):
    return jax.nn.gelu(x, approximate=True)

def _silu(x):
    return jax.nn.silu(x)

def _sigmoid(x):
    return jax.nn.sigmoid(x)

def _layernorm(x, axis=-1, eps=1e-05):
    m = jnp.mean(x, axis=axis, keepdims=True)
    v = jnp.var(x, axis=axis, keepdims=True)
    return (x - m) / jnp.sqrt(v + eps)

def _scatter_add(tgt, idx, src, axis=0):
    return tgt.at[idx].add(src)

def _segment_sum(src, seg, n):
    return jax.ops.segment_sum(src, seg, n)
kernel_name = 'mk_decoder_preln_d1_seqx_r2_cd33be'

def setup_inputs(seed: int=0):
    np.random.seed(seed)
    _w = jnp.asarray

    def _rec_inputs():
        import jax
        import jax.numpy as jnp
        _rk = jax.random.key(seed)
        x = -0.0005207 + 1.001 * jax.random.normal(jax.random.fold_in(_rk, 1), (4, 1024, 512), jnp.float32)
        _lenS = 1024 - jax.random.randint(jax.random.fold_in(_rk, 7), (4,), 0, max(1, 1024 // 4) + 1, jnp.int32)
        _lenS2 = 64 - jax.random.randint(jax.random.fold_in(_rk, 8), (4,), 0, max(1, 64 // 4) + 1, jnp.int32)
        _ctx_1024P = jax.random.normal(jax.random.fold_in(_rk, 11), (4, 16, 512), jnp.float32)
        _ctx_1024c = jax.random.dirichlet(jax.random.fold_in(_rk, 511), 0.3 * jnp.ones((16,), jnp.float32), (4, 64))
        _ctx_1024t = jnp.einsum('bsk,bkd->bsd', _ctx_1024c, _ctx_1024P)
        _ctx_1024t = _ctx_1024t * jax.lax.rsqrt(jnp.mean(jnp.square(_ctx_1024t)) + 1e-12) * 0.953939
        ctx_1024 = 2.81802e-05 + 1.00001 * (_ctx_1024t + 0.3 * jax.random.normal(jax.random.fold_in(_rk, 611), (4, 64, 512), jnp.float32))
        _validS = jnp.arange(1024)[None, :] < _lenS[:, None]
        _validS2 = jnp.arange(64)[None, :] < _lenS2[:, None]
        _causal = jnp.tril(jnp.ones((1024, 1024), dtype=bool))
        mask_BxSxS2_bk0 = jnp.logical_not(jnp.broadcast_to(_validS2[:, None, :], (4, 1024, 64)))
        return (x, ctx_1024, mask_BxSxS2_bk0)
    x, ctx_1024, mask_BxSxS2_bk0 = _rec_inputs()

    def _L0_attn_setup():
        import jax, jax.numpy as jnp
        import numpy as np
        B, L, H, I, K, G = (2, 2048, 512, 1024, 4, 8)
        EPS = 1e-05

        def _layernorm(x, g, b):
            m = x.mean(-1, keepdims=True)
            v = jnp.var(x, axis=-1, keepdims=True)
            return (x - m) * jax.lax.rsqrt(v + EPS) * g + b
        key = jax.random.key(seed)
        ks = jax.random.split(key, 8)
        s = 0.02
        return {'hidden_states': jax.random.normal(ks[0], (B, L, H), jnp.float32), 'in_proj_w': jax.random.normal(ks[1], (2 * I, H), jnp.float32) * s, 'conv_w': jax.random.normal(ks[2], (I, I // G, K), jnp.float32) * s, 'conv_b': jax.random.normal(ks[3], (I,), jnp.float32) * s, 'ln_g': jnp.ones((I,), jnp.float32), 'ln_b': jnp.zeros((I,), jnp.float32), 'fc_w': jax.random.normal(ks[4], (H, I), jnp.float32) * s, 'fc_b': jnp.zeros((H,), jnp.float32), 'cproj_w': jax.random.normal(ks[5], (I, H), jnp.float32) * s, 'cproj_b': jnp.zeros((I,), jnp.float32), 'out_w': jax.random.normal(ks[6], (H, I), jnp.float32) * s}
    _L0_attn_all = _L0_attn_setup()
    _L0_attn_in = {k: v for k, v in _L0_attn_all.items() if k in ('in_proj_w', 'conv_w', 'conv_b', 'ln_g', 'ln_b', 'fc_w', 'fc_b', 'cproj_w', 'cproj_b', 'out_w')}
    del _L0_attn_all

    def _L0_xattn_setup():
        import jax, jax.numpy as jnp
        import numpy as np
        B, TQ, TKV, D, H = (4, 256, 2048, 512, 8)
        HEAD_DIM = D // H

        def _split_heads(x, h):
            b, t, c = x.shape
            return x.reshape(b, t, h, c // h).transpose(0, 2, 1, 3)
        key = jax.random.key(seed)
        ks = jax.random.split(key, 8)
        s = 0.02
        inputs_q = jax.random.normal(ks[0], (B, TQ, D), jnp.float32)
        inputs_kv = jax.random.normal(ks[1], (B, TKV, D), jnp.float32)
        attention_mask = jax.random.randint(ks[2], (B, TQ, TKV), 0, 2).astype(bool)
        Wq = jax.random.normal(ks[3], (D, D), jnp.float32) * s
        Wk = jax.random.normal(ks[4], (D, D), jnp.float32) * s
        Wv = jax.random.normal(ks[5], (D, D), jnp.float32) * s
        Wo = jax.random.normal(ks[6], (D, D), jnp.float32) * s
        zb = jnp.zeros((D,), jnp.float32)
        return {'inputs_q': inputs_q, 'inputs_kv': inputs_kv, 'attention_mask': attention_mask, 'Wq': Wq, 'bq': zb, 'Wk': Wk, 'bk': zb, 'Wv': Wv, 'bv': zb, 'Wo': Wo, 'bo': zb}
    _L0_xattn_all = _L0_xattn_setup()
    _L0_xattn_in = {k: v for k, v in _L0_xattn_all.items() if k in ('Wq', 'bq', 'Wk', 'bk', 'Wv', 'bv', 'Wo', 'bo')}
    del _L0_xattn_all

    def _L0_ffn_setup():
        import jax, jax.numpy as jnp
        import numpy as np
        B, S, D = (4, 1024, 512)
        E = 8
        CF = 1
        key = jax.random.key(seed)
        k_x, k_g, k_w, k_b = jax.random.split(key, 4)
        x = jax.random.normal(k_x, (B, S, D), dtype=jnp.float32)
        Wg = jax.random.normal(k_g, (D, E), dtype=jnp.float32) * (1.0 / np.sqrt(D))
        We = jax.random.normal(k_w, (D, D), dtype=jnp.float32) * (1.0 / np.sqrt(D))
        be = jax.random.normal(k_b, (D,), dtype=jnp.float32) * 0.01
        return {'x': x, 'Wg': Wg, 'We': We, 'be': be}
    _L0_ffn_all = _L0_ffn_setup()
    _L0_ffn_in = {k: v for k, v in _L0_ffn_all.items() if k in ('Wg', 'We', 'be')}
    del _L0_ffn_all
    return {'x': x, 'ctx_1024': ctx_1024, 'mask_BxSxS2_bk0': mask_BxSxS2_bk0, 'L0_attn_in_proj_w': _L0_attn_in['in_proj_w'], 'L0_attn_conv_w': _L0_attn_in['conv_w'], 'L0_attn_conv_b': _L0_attn_in['conv_b'], 'L0_attn_ln_g': _L0_attn_in['ln_g'], 'L0_attn_ln_b': _L0_attn_in['ln_b'], 'L0_attn_fc_w': _L0_attn_in['fc_w'], 'L0_attn_fc_b': _L0_attn_in['fc_b'], 'L0_attn_cproj_w': _L0_attn_in['cproj_w'], 'L0_attn_cproj_b': _L0_attn_in['cproj_b'], 'L0_attn_out_w': _L0_attn_in['out_w'], 'L0_xattn_Wq': _L0_xattn_in['Wq'], 'L0_xattn_bq': _L0_xattn_in['bq'], 'L0_xattn_Wk': _L0_xattn_in['Wk'], 'L0_xattn_bk': _L0_xattn_in['bk'], 'L0_xattn_Wv': _L0_xattn_in['Wv'], 'L0_xattn_bv': _L0_xattn_in['bv'], 'L0_xattn_Wo': _L0_xattn_in['Wo'], 'L0_xattn_bo': _L0_xattn_in['bo'], 'L0_ffn_Wg': _L0_ffn_in['Wg'], 'L0_ffn_We': _L0_ffn_in['We'], 'L0_ffn_be': _L0_ffn_in['be']}

def reference(x, ctx_1024, mask_BxSxS2_bk0, L0_attn_in_proj_w, L0_attn_conv_w, L0_attn_conv_b, L0_attn_ln_g, L0_attn_ln_b, L0_attn_fc_w, L0_attn_fc_b, L0_attn_cproj_w, L0_attn_cproj_b, L0_attn_out_w, L0_xattn_Wq, L0_xattn_bq, L0_xattn_Wk, L0_xattn_bk, L0_xattn_Wv, L0_xattn_bv, L0_xattn_Wo, L0_xattn_bo, L0_ffn_Wg, L0_ffn_We, L0_ffn_be):
    import jax
    import jax.numpy as jnp

    def _L0_attn_ref(hidden_states, in_proj_w, conv_w, conv_b, ln_g, ln_b, fc_w, fc_b, cproj_w, cproj_b, out_w):
        import jax, jax.numpy as jnp
        import numpy as np
        B, L, H, I, K, G = (2, 2048, 512, 1024, 4, 8)
        EPS = 1e-05

        def _layernorm(x, g, b):
            m = x.mean(-1, keepdims=True)
            v = jnp.var(x, axis=-1, keepdims=True)
            return (x - m) * jax.lax.rsqrt(v + EPS) * g + b
        p = hidden_states @ in_proj_w.T
        h, gate = (p[..., :I], p[..., I:])
        gate = jax.nn.silu(gate)
        hc = jnp.transpose(h, (0, 2, 1))
        conv = jax.lax.conv_general_dilated(hc, conv_w, window_strides=(1,), padding=[(K - 1, 0)], feature_group_count=G, dimension_numbers=('NCH', 'OIH', 'NCH'))
        conv = conv + conv_b[None, :, None]
        h = jnp.transpose(conv, (0, 2, 1)) * gate
        residual = h
        hn = _layernorm(h, ln_g, ln_b)
        m = jax.nn.silu(hn @ fc_w.T + fc_b) @ cproj_w.T + cproj_b
        h = m + residual
        return h @ out_w.T

    def _L0_xattn_ref(inputs_q, inputs_kv, attention_mask, Wq, bq, Wk, bk, Wv, bv, Wo, bo):
        import jax, jax.numpy as jnp
        import numpy as np
        B, TQ, TKV, D, H = (4, 256, 2048, 512, 8)
        HEAD_DIM = D // H

        def _split_heads(x, h):
            b, t, c = x.shape
            return x.reshape(b, t, h, c // h).transpose(0, 2, 1, 3)
        q = _split_heads(inputs_q @ Wq + bq, H)
        k = _split_heads(inputs_kv @ Wk + bk, H)
        v = _split_heads(inputs_kv @ Wv + bv, H)
        scale = 1.0 / np.sqrt(HEAD_DIM).astype(np.float32)
        scores = jnp.einsum('bhtd,bhTd->bhtT', q, k) * scale
        large_k = jnp.asarray(1e+30, scores.dtype)
        scores = jnp.where(attention_mask[:, None, :, :], scores, -large_k)
        probs = jax.nn.softmax(scores, axis=-1)
        summed = jnp.einsum('bhtT,bhTd->bhtd', probs, v)
        b, h, t, d = summed.shape
        summed = summed.transpose(0, 2, 1, 3).reshape(b, t, h * d)
        wipe = jnp.all(~attention_mask, axis=-1, keepdims=True)
        summed = jnp.where(wipe, jnp.zeros_like(summed), summed)
        return summed @ Wo + bo

    def _L0_ffn_ref(x, Wg, We, be):
        import jax, jax.numpy as jnp
        import numpy as np
        B, S, D = (4, 1024, 512)
        E = 8
        CF = 1
        b, s, d = x.shape
        n = b * s
        cap = n // E * CF
        h = x.reshape(n, d)
        router_logits = h @ Wg
        probs = jax.nn.softmax(router_logits, axis=1)
        best = jnp.argmax(probs, axis=1)
        mask = jax.nn.one_hot(best, E, dtype=probs.dtype)
        gate = jnp.sum(probs * mask, axis=1)
        locations = jnp.cumsum(mask, axis=0) - 1.0
        mask = mask * (locations < cap).astype(mask.dtype)
        loc_idx = jnp.sum(locations * mask, axis=1).astype(jnp.int32)
        new_gate = gate[:, None] * mask
        loc_oh = jax.nn.one_hot(loc_idx, cap, dtype=new_gate.dtype)
        combine = new_gate[:, :, None] * loc_oh[:, None, :]
        dispatch = (combine != 0).astype(h.dtype)
        dispatched = jnp.einsum('nec,nd->ecd', dispatch, h).reshape(E * cap, d)
        expert_out = dispatched @ We + be
        out = combine.reshape(n, E * cap) @ expert_out
        return out.reshape(b, s, d)
    x = x + _L0_attn_ref(_layernorm(x, axis=-1), L0_attn_in_proj_w, L0_attn_conv_w, L0_attn_conv_b, L0_attn_ln_g, L0_attn_ln_b, L0_attn_fc_w, L0_attn_fc_b, L0_attn_cproj_w, L0_attn_cproj_b, L0_attn_out_w)
    x = x + _L0_xattn_ref(_layernorm(x, axis=-1), ctx_1024, mask_BxSxS2_bk0, L0_xattn_Wq, L0_xattn_bq, L0_xattn_Wk, L0_xattn_bk, L0_xattn_Wv, L0_xattn_bv, L0_xattn_Wo, L0_xattn_bo)
    x = x + _L0_ffn_ref(_layernorm(x, axis=-1), L0_ffn_Wg, L0_ffn_We, L0_ffn_be)
    return x

_drawn_inputs = setup_inputs


def setup_inputs(seed=0):
    import zlib

    import numpy as np

    out = dict(_drawn_inputs(seed))
    spreads = {'L0_attn_ln_g': (1.0, 0.544),
     'L0_attn_ln_b': (0.0, 0.277),
     'L0_attn_fc_b': (0.0, 0.1),
     'L0_attn_cproj_b': (0.0, 0.1),
     'L0_xattn_bq': (0.0, 0.595),
     'L0_xattn_bk': (0.0, 2.0),
     'L0_xattn_bv': (0.0, 0.1),
     'L0_xattn_bo': (0.0, 0.1)}
    factors = {'L0_attn_conv_b': 2.696, 'L0_ffn_be': 8.0, 'L0_xattn_Wq': 2.807}
    for name, (base, spread) in spreads.items():
        noise = np.random.default_rng([zlib.crc32(name.encode()), seed]).standard_normal(out[name].shape)
        drawn = base * np.exp(spread * noise) if base else spread * noise
        out[name] = jnp.asarray(drawn.astype(out[name].dtype))
    for name, factor in factors.items():
        out[name] = (out[name] * factor).astype(out[name].dtype)
    return out
```

```python
from contextlib import ExitStack

import concourse.bass as bass
from concourse import mybir

ALU = mybir.AluOpType
ACT = mybir.ActivationFunctionType
AX = mybir.AxisListType
F32 = mybir.dt.float32
F16 = mybir.dt.float16
BF16 = mybir.dt.bfloat16

P = 128
B, S, D = 4, 1024, 512
I = 1024
MID = 512
TAPS, GROUPS = 4, 8
KEYS, HEADS = 64, 8
E = 8
CAP = B * S // E
EPS = 1e-5
TILE = 512
SUBS = TILE // P
HALVES = S // TILE
KD = D // P
KI = I // P
HALO = TAPS - 1
BSUBS = S // P
NSUB = B * BSUBS
PAIRS = HEADS // 2
BIG = 1e30

W_SCALE = 2.0 ** 8
LN_SCALE = 2.0 ** 8
P_SCALE = 2.0 ** 6
H_SCALE = 2.0 ** 7
MID_SCALE = 2.0 ** 6
W2_SCALE = H_SCALE * W_SCALE / MID_SCALE
PROB_SCALE = 2.0 ** 12


def carry(dve, pad, *waits):
    for s, v in waits:
        at_least(dve, s, v)
    dve.memset(pad, 0.0)


def at_least(eng, sem, value):
    if isinstance(value, int) and value <= 0:
        return
    eng.wait_ge(sem, value)


def product3(pe, out, chunks, start=True, stop=True):
    last = len(chunks) - 1
    for n, (l_hi, l_lo, r_hi, r_lo) in enumerate(chunks):
        pe.matmul(out, l_hi, r_hi, start=start and n == 0, stop=False)
        pe.matmul(out, l_hi, r_lo, start=False, stop=False)
        mm = pe.matmul(out, l_lo, r_hi, start=False, stop=stop and n == last)
    return mm


def bass_decoder_kernel(
    nc, x, ctxT, mask, in_wT, conv_wT, conv_b, ln_g, ln_b, fc_wT, fc_b, cproj_w, cproj_b, out_wT,
    WqT, bq, Wk, bk, Wv, bv, Wo, bo, Wg, We, be, ident_in, tri_in, prio_in, out,
):
    x_v = x.rearrange("b (h s p) d -> b h p s d", h=HALVES, p=P)
    x1_dram = nc.dram_tensor("x1_scratch", (B * HALVES, P, SUBS, D), F32).ap()
    out_v = out.rearrange("b (s p) d -> (b s) p d", p=P)
    m_dram = nc.dram_tensor("m_scratch", (B, P, 2, KD, HEADS * KEYS), F16).ap()
    vw_dram = nc.dram_tensor("vw_scratch", (B, P, 2, PAIRS, D), F16).ap()

    top = ExitStack()
    with top:
        def sem(name):
            return top.enter_context(nc.semaphore(name))

        def sb_in(stack):
            return lambda name, shape, dt=F32: stack.enter_context(nc.sbuf_tensor(name, shape, dt))

        bank = [top.enter_context(nc.psum_tensor(f"bank{n}", [P, 512], F32)) for n in range(8)]

        sb = sb_in(top)
        ident = sb("ident", [P, P])
        hbias = sb("hbias", [P, B, HEADS * KEYS])
        masku = sb("masku", [P, NSUB, KEYS], mybir.dt.uint8)
        tri = sb("tri", [P, P], BF16)
        ones_b = sb("ones_b", [P, P], BF16)
        prio = sb("prio", [P, E])
        mhalf = sb("mhalf", [P, SUBS])
        pad_dve = sb("pad_dve", [P, 1])

        mid_stack = ExitStack()
        with mid_stack:
            mb = sb_in(mid_stack)
            in_w = mb("in_w", [P, 2, KD, 2 * I], F16)
            conv_w = mb("conv_w", [P, 2, GROUPS, TAPS, P], F16)
            fc_w = mb("fc_w", [P, 2, KI, MID], F16)
            out_w = mb("out_w", [P, 2, KI, D], F16)
            w2 = mb("w2", [P, 2, KD, D], F16)
            fc_g_row = mb("fc_g_row", [P, MID])
            fc_b_row = mb("fc_b_row", [P, MID])
            out_b_row = mb("out_b_row", [P, D])
            conv_bs = mb("conv_bs", [P, GROUPS])

            prep = ExitStack()
            with prep:
                pb = sb_in(prep)
                raw0 = pb("raw0", [P, KD * 2 * I])
                raw1 = pb("raw1", [P, 4 * KD * D])
                ctx = pb("ctx", [P, KD, B * KEYS])
                kbd = pb("kbd", [P, PAIRS, B, P])
                vbd = pb("vbd", [P, PAIRS, B, P])
                vw_stage = pb("vw_stage", [P, 2, 2, D], F16)
                vec = pb("vec", [P, 4 * KI + 3 * KD])
                g256 = pb("g256", [P, KI])
                tri_f = pb("tri_f", [P, P])

                conv_bv, ln_gv, ln_bv, cproj_bv = [vec[:, n * KI:(n + 1) * KI] for n in range(4)]
                bqv, bkv, bvv = [vec[:, 4 * KI + n * KD:4 * KI + (n + 1) * KD] for n in range(3)]
                raw_in = raw0[:, :].rearrange("p (k n) -> p k n", k=KD)
                raw_conv = raw0[:, 0:GROUPS * TAPS * P]
                raw_fc = raw0[:, KD * I:2 * KD * I].rearrange("p (k n) -> p k n", k=KI)
                wk_r, wv_r, wq_r, wo_r = [raw1[:, n * KD * D:(n + 1) * KD * D].rearrange("p (k n) -> p k n", k=KD)
                                          for n in range(4)]
                m_stage = [raw1[:, n * KD * D:(n + 1) * KD * D].bitcast(F16).rearrange(
                    "p (b t n) -> p b t n", b=B, t=2) for n in range(2)]
                raw_out = raw1[:, 0:KI * D].rearrange("p (k n) -> p k n", k=KI)
                raw_cproj = raw1[:, KI * D:2 * KI * D].rearrange("p (k n) -> p k n", k=KI)

                names = ["small", "ctx", "wk", "wv", "wq", "wo", "in", "conv", "fc", "outw", "cproj"]
                landed = {n: sem(f"landed_{n}") for n in names}
                SMALL = 12
                p_const = sem("p_const")
                p_job = sem("p_job")
                p_hi = sem("p_hi")
                p_evac = sem("p_evac")
                p_whi = sem("p_whi")
                p_wlo = sem("p_wlo")
                p_vec = sem("p_vec")
                m_stored = [sem(f"m_stored{n}") for n in range(2)]
                vw_stored = [sem(f"vw_stored{n}") for n in range(2)]

                K_JOB, V_JOB, HB_JOB, M_JOB = 0, KD, 2 * KD, 2 * KD + PAIRS
                VW_JOB = M_JOB + KD * PAIRS
                GB_JOB = VW_JOB + B * PAIRS
                W2_JOB = GB_JOB + 3

                def m_out(n):
                    m, c = n // PAIRS, n % PAIRS
                    return m_stage[m % 2][:, :, :, c * P:(c + 1) * P]

                def vw_out(n):
                    return vw_stage[:, n % 2, :, :]

                def conv_piece(t, n):
                    return conv_w[:, t, 4 * n:4 * n + 4, :, :].rearrange("p g k o -> p (g k o)")

                def out_piece(t, n):
                    return out_w[:, t, 4 * n:4 * n + 4, :].rearrange("p k n -> p (k n)")

                def raw_out_piece(n):
                    return raw_out[:, 4 * n:4 * n + 4, :].rearrange("p k n -> p (k n)")

                IN_N, CONV_N, FC_N, OUT_N = KD, 2, KI, 2

                with nc.Block() as block:
                    @block.sync
                    def _(sp):
                        kn = "(k p) n -> p k n"
                        sp.dma_start(ctx[:, :, :], ctxT.rearrange(kn, p=P)).then_inc(landed["ctx"], 16)
                        sp.dma_start(wk_r, Wk.rearrange(kn, p=P)).then_inc(landed["wk"], 16)
                        for n, v in enumerate([conv_b, ln_g, ln_b, cproj_b]):
                            sp.dma_start(vec[:, n * KI:(n + 1) * KI], v).then_inc(landed["small"], 16)
                        for n, v in enumerate([bq, bk, bv]):
                            sp.dma_start(vec[:, 4 * KI + n * KD:4 * KI + (n + 1) * KD], v).then_inc(landed["small"], 16)
                        sp.dma_start(ident[:, :], ident_in).then_inc(landed["small"], 16)
                        sp.dma_start(tri_f[:, :], tri_in).then_inc(landed["small"], 16)
                        sp.dma_start(prio[:, :], prio_in).then_inc(landed["small"], 16)
                        sp.dma_start(masku[:, :, :], mask).then_inc(landed["small"], 16)
                        sp.dma_start(fc_b_row[:, :], fc_b.partition_broadcast(P)).then_inc(landed["small"], 16)
                        sp.dma_start(wv_r, Wv.rearrange(kn, p=P)).then_inc(landed["wv"], 16)
                        sp.dma_start(wq_r, WqT.rearrange(kn, p=P)).then_inc(landed["wq"], 16)
                        sp.dma_start(raw_in, in_wT.rearrange(kn, p=P)).then_inc(landed["in"], 16)
                        sp.dma_start(wo_r, Wo.rearrange(kn, p=P)).then_inc(landed["wo"], 16)
                        for m in range(KD):
                            sp.wait_ge(p_evac, M_JOB + PAIRS * (m + 1))
                            for b in range(B):
                                sp.dma_start(m_dram[b, :, :, m, :], m_stage[m % 2][:, b, :, :])\
                                  .then_inc(m_stored[m % 2], 16)
                        sp.wait_ge(p_whi, IN_N)
                        sp.wait_ge(p_wlo, IN_N)
                        sp.dma_start(raw_conv, conv_wT).then_inc(landed["conv"], 16)
                        sp.dma_start(raw_fc, fc_wT.rearrange(kn, p=P)).then_inc(landed["fc"], 16)
                        for n in range(B * PAIRS):
                            sp.wait_ge(p_evac, VW_JOB + n + 1)
                            sp.dma_start(vw_dram[n // PAIRS, :, :, n % PAIRS, :], vw_out(n))\
                              .then_inc(vw_stored[n % 2], 16)
                        sp.wait_ge(m_stored[0], 16 * B * KD // 2)
                        sp.wait_ge(m_stored[1], 16 * B * KD // 2)
                        sp.dma_start(raw_out, out_wT.rearrange(kn, p=P)).then_inc(landed["outw"], 16)
                        sp.dma_start(raw_cproj, cproj_w.rearrange(kn, p=P)).then_inc(landed["cproj"], 16)
                        sp.wait_ge(vw_stored[0], 16 * B * PAIRS // 2)
                        sp.wait_ge(vw_stored[1], 16 * B * PAIRS // 2)

                    @block.gpsimd
                    def _(pool):
                        pool.memset(kbd[:, :, :, :], 0.0).then_inc(p_const, 1)
                        pool.memset(vbd[:, :, :, :], 0.0).then_inc(p_const, 1)
                        pool.memset(ones_b[:, :], 1.0).then_inc(p_const, 1)
                        pool.memset(mhalf[:, :], -0.5).then_inc(p_const, 1)

                    @block.tensor
                    def _(pe):
                        def slot(n):
                            at_least(pe, p_evac, n - 7)
                            return bank[n % 8]

                        pe.wait_ge(landed["ctx"], 16)
                        for job, name, w in ((K_JOB, "wk", wk_r), (V_JOB, "wv", wv_r)):
                            pe.wait_ge(landed[name], 16)
                            for m in range(KD):
                                o = slot(job + m)[:, 0:B * KEYS]
                                for k in range(KD):
                                    mm = pe.matmul(o, w[:, k, m * P:(m + 1) * P], ctx[:, k, :],
                                                   start=(k == 0), stop=(k == KD - 1))
                                mm.then_inc(p_job, 1)
                        pe.wait_ge(p_evac, K_JOB + KD)
                        for c in range(PAIRS):
                            o = slot(HB_JOB + c)
                            pe.matmul(o[:, :], bqv[:, c:c + 1].to_broadcast([P, P]),
                                      kbd[:, c, :, :].rearrange("p b n -> p (b n)"),
                                      start=True, stop=True).then_inc(p_job, 1)
                        pe.wait_ge(landed["wq"], 16)
                        for m in range(KD):
                            for c in range(PAIRS):
                                o = slot(M_JOB + PAIRS * m + c)
                                pe.matmul(o[:, :], wq_r[:, c, m * P:(m + 1) * P],
                                          kbd[:, c, :, :].rearrange("p b n -> p (b n)"),
                                          start=True, stop=True).then_inc(p_job, 1)
                        pe.wait_ge(landed["wo"], 16)
                        pe.wait_ge(p_evac, V_JOB + KD)
                        for b in range(B):
                            for c in range(PAIRS):
                                o = slot(VW_JOB + PAIRS * b + c)
                                pe.matmul(o[:, :], vbd[:, c, b, :], wo_r[:, c, :],
                                          start=True, stop=True).then_inc(p_job, 1)
                        for n, (v, w, name) in enumerate(((ln_gv, raw_fc, "fc"), (ln_bv, raw_fc, "fc"),
                                                          (cproj_bv, raw_out, "outw"))):
                            pe.wait_ge(landed[name], 16)
                            o = slot(GB_JOB + n)
                            for k in range(KI):
                                mm = pe.matmul(o[:, :], v[:, k:k + 1].to_broadcast([P, P]), w[:, k, :],
                                               start=(k == 0), stop=(k == KI - 1))
                            mm.then_inc(p_job, 1)
                        pe.wait_ge(landed["cproj"], 16)
                        for m in range(KD):
                            o = slot(W2_JOB + m)
                            for k in range(KI):
                                mm = pe.matmul(o[:, :], raw_cproj[:, k, m * P:(m + 1) * P], raw_out[:, k, :],
                                               start=(k == 0), stop=(k == KI - 1))
                            mm.then_inc(p_job, 1)

                    @block.scalar
                    def _(act):
                        def split(dst, src, scale=W_SCALE):
                            act.activation(dst, src, ACT.Copy, scale=scale).then_inc(p_whi, 1)

                        for m in range(KD):
                            for c in range(PAIRS):
                                n = PAIRS * m + c
                                act.wait_ge(p_job, M_JOB + n + 1)
                                if m < 2:
                                    act.wait_ge(p_evac, V_JOB + KD)
                                else:
                                    act.wait_ge(m_stored[m % 2], 16 * B)
                                act.activation(m_out(n)[:, :, 0, :],
                                               bank[(M_JOB + n) % 8][:, :].rearrange("p (b n) -> p b n", b=B),
                                               ACT.Copy, scale=W_SCALE).then_inc(p_hi, 1)
                            if m == 0:
                                act.wait_ge(landed["in"], 16)
                            split(in_w[:, 0, m, :], raw_in[:, m, :])
                        for n in range(B * PAIRS):
                            act.wait_ge(p_job, VW_JOB + n + 1)
                            if n >= 2:
                                act.wait_ge(vw_stored[n % 2], 16 * (n // 2))
                            act.activation(vw_out(n)[:, 0, :], bank[(VW_JOB + n) % 8][:, :],
                                           ACT.Copy, scale=W_SCALE).then_inc(p_hi, 1)
                        act.wait_ge(landed["conv"], 16)
                        for n in range(CONV_N):
                            split(conv_piece(0, n), raw_conv[:, n * 2048:(n + 1) * 2048])
                        act.wait_ge(landed["fc"], 16)
                        act.wait_ge(p_vec, 2)
                        for k in range(KI):
                            split(fc_w[:, 0, k, :], raw_fc[:, k, :], g256[:, k:k + 1])
                        act.wait_ge(landed["outw"], 16)
                        for n in range(OUT_N):
                            split(out_piece(0, n), raw_out_piece(n))
                        for m in range(KD):
                            act.wait_ge(p_job, W2_JOB + m + 1)
                            act.activation(w2[:, 0, m, :], bank[(W2_JOB + m) % 8][:, :],
                                           ACT.Copy, scale=W2_SCALE).then_inc(p_hi, 1)

                    @block.vector
                    def _(dve):
                        def split(n, dst, src, hi, scale=W_SCALE):
                            dve.wait_ge(p_whi, n + 1)
                            dve.scalar_tensor_tensor(dst, src, scale, hi, ALU.mult, ALU.subtract).then_inc(p_wlo, 1)

                        dve.wait_ge(landed["small"], 16 * SMALL)
                        dve.tensor_scalar(conv_bs[:, :], conv_bv, P_SCALE * W_SCALE, None, ALU.mult).then_inc(p_vec, 1)
                        dve.tensor_scalar(g256[:, :], ln_gv, W_SCALE, None, ALU.mult).then_inc(p_vec, 1)
                        dve.tensor_copy(tri[:, :], tri_f[:, :]).then_inc(p_vec, 1)
                        for job, bd, bias, scale, const in ((K_JOB, kbd, bkv, 0.125, 1), (V_JOB, vbd, bvv, 1.0, 2)):
                            dve.wait_ge(p_const, const)
                            for m in range(KD):
                                dve.wait_ge(p_job, job + m + 1)
                                for q in range(2):
                                    r = slice(64 * q, 64 * q + 64)
                                    ins = dve.tensor_scalar(
                                        bd[r, m, :, r],
                                        bank[(job + m) % 8][r, 0:B * KEYS].rearrange("p (b n) -> p b n", b=B),
                                        bias[r, m:m + 1], scale, ALU.add, ALU.mult)
                                ins.then_inc(p_evac, 1)
                        for c in range(PAIRS):
                            dve.wait_ge(p_job, HB_JOB + c + 1)
                            dve.tensor_copy(hbias[:, :, c * P:(c + 1) * P],
                                            bank[(HB_JOB + c) % 8][:, :].rearrange("p (b n) -> p b n", b=B))\
                               .then_inc(p_evac, 1)
                        for m in range(KD):
                            for c in range(PAIRS):
                                n = PAIRS * m + c
                                dve.wait_ge(p_hi, n + 1)
                                for b in range(B):
                                    ins = dve.scalar_tensor_tensor(
                                        m_out(n)[:, b, 1, :], bank[(M_JOB + n) % 8][:, b * P:(b + 1) * P],
                                        W_SCALE, m_out(n)[:, b, 0, :], ALU.mult, ALU.subtract)
                                ins.then_inc(p_evac, 1)
                            split(m, in_w[:, 1, m, :], raw_in[:, m, :], in_w[:, 0, m, :])
                        for n in range(B * PAIRS):
                            dve.wait_ge(p_hi, KD * PAIRS + n + 1)
                            dve.scalar_tensor_tensor(vw_out(n)[:, 1, :], bank[(VW_JOB + n) % 8][:, :], W_SCALE,
                                                     vw_out(n)[:, 0, :], ALU.mult, ALU.subtract).then_inc(p_evac, 1)
                        for n in range(CONV_N):
                            split(IN_N + n, conv_piece(1, n), raw_conv[:, n * 2048:(n + 1) * 2048], conv_piece(0, n))
                        for k in range(KI):
                            split(IN_N + CONV_N + k, fc_w[:, 1, k, :], raw_fc[:, k, :], fc_w[:, 0, k, :],
                                  g256[:, k:k + 1])
                        dve.wait_ge(p_job, GB_JOB + 1)
                        dve.tensor_scalar(fc_g_row[:, :], bank[GB_JOB % 8][:, :], H_SCALE * W_SCALE, None, ALU.mult)\
                           .then_inc(p_evac, 1)
                        dve.wait_ge(p_job, GB_JOB + 2)
                        dve.tensor_tensor(fc_b_row[:, :], bank[(GB_JOB + 1) % 8][:, :], fc_b_row[:, :], ALU.add)\
                           .then_inc(p_evac, 1)
                        for n in range(OUT_N):
                            split(IN_N + CONV_N + FC_N + n, out_piece(1, n), raw_out_piece(n), out_piece(0, n))
                        dve.wait_ge(p_job, GB_JOB + 3)
                        dve.tensor_copy(out_b_row[:, :], bank[(GB_JOB + 2) % 8][:, :]).then_inc(p_evac, 1)
                        for m in range(KD):
                            dve.wait_ge(p_hi, (KD + B) * PAIRS + m + 1)
                            dve.scalar_tensor_tensor(w2[:, 1, m, :], bank[(W2_JOB + m) % 8][:, :], W2_SCALE,
                                                     w2[:, 0, m, :], ALU.mult, ALU.subtract).then_inc(p_evac, 1)

            pha = ExitStack()
            with pha:
                ab = sb_in(pha)
                xs = ab("xs", [P, HALVES, SUBS, D])
                xn = ab("xn", [P, SUBS, D])
                bn = ab("bn", [P, SUBS, 6])
                mv = ab("mv", [P, SUBS, 2])
                va = ab("va", [P, SUBS])
                rs = ab("rs", [P, SUBS])
                nm = ab("nm", [P, SUBS])
                nb = ab("nb", [P, SUBS])
                xT = ab("xT", [P, 2, KD, TILE], F16)
                pp = ab("pp", [P, 2, 2, HALO + TILE + 1], F16)
                tails = ab("tails", [P, GROUPS, 2, HALO], F16)
                gate = ab("gate", [P, 2, TILE])
                hh = ab("hh", [P, 2, TILE])
                sq = ab("sq", [P, 2, TILE])
                hsum = ab("hsum", [P, TILE])
                qsum = ab("qsum", [P, TILE])
                zero = ab("zero", [P, TILE])
                hT = ab("hT", [P, 2, KI, TILE], F16)
                ones1 = ab("ones1", [P, 1])
                mneg = ab("mneg", [P, SUBS])
                msq = ab("msq", [P, SUBS])
                e2 = ab("e2", [P, SUBS])
                v2 = ab("v2", [P, SUBS])
                r2 = ab("r2", [P, SUBS])
                tb = ab("tb", [P, 2, MID])
                ub = ab("ub", [P, 2, MID])
                mm_s = ab("mm_s", [P, SUBS, MID])
                mT = ab("mT", [P, 2, 2, KD, P], F16)
                x1o = ab("x1o", [P, SUBS, D])

                x_landed = [sem(f"x_landed{h}") for h in range(HALVES)]
                a_one = sem("a_one")
                a_zero = sem("a_zero")
                bn_done, mv_done, va_done, rs_done = sem("bn_done"), sem("mv_done"), sem("va_done"), sem("rs_done")
                nm_done, nb_done = sem("nm_done"), sem("nb_done")
                xn_done = sem("xn_done")
                resid_done = sem("resid_done")
                xt_tr, xt_hi, xt_lo = sem("xt_tr"), sem("xt_hi"), sem("xt_lo")
                iph, ipg = sem("iph"), sem("ipg")
                p_hi_done, p_lo_done, p_halo, p_ready = sem("p_hi_done"), sem("p_lo_done"), sem("p_halo"), sem("p_ready")
                gate_done = sem("gate_done")
                conv_done = sem("conv_done")
                h_done = sem("h_done")
                h_hi, h_lo, h_sq, h_sum, q_sum = sem("h_hi"), sem("h_lo"), sem("h_sq"), sem("h_sum"), sem("q_sum")
                stats_done = sem("stats_done")
                ln2_mneg, ln2_e2, ln2_msq, ln2_v, ln2_r = (sem("ln2_mneg"), sem("ln2_e2"), sem("ln2_msq"),
                                                           sem("ln2_v"), sem("ln2_r"))
                fc_done, t_done, u_done, silu_done = sem("fc_done"), sem("t_done"), sem("u_done"), sem("silu_done")
                mt_tr, mt_hi, mt_lo = sem("mt_tr"), sem("mt_hi"), sem("mt_lo")
                h_used = sem("h_used")
                out_done, x1_done, x1_stored = sem("out_done"), sem("x1_done"), sem("x1_stored")

                OUT_BANK = [6, 7, 2, 3]
                FC_SQ = (H_SCALE * W_SCALE) ** 2
                XT_B, MT_B, ST_B = bank[4], bank[5], bank[7]

                with nc.Block() as block:

                    @block.sync
                    def _(sp):
                        for h in range(HALVES):
                            sp.dma_start(xs[:, h, :, :], x_v[0, h]).then_inc(x_landed[h], 16)

                        def tile(b, half, more):
                            t = HALVES * b + half
                            sp.wait_ge(x1_done, SUBS * t + SUBS)
                            sp.dma_start(x1_dram[t], x1o[:, :, :]).then_inc(x1_stored, 16)
                            if more:
                                sp.dma_start(xs[:, half, :, :], x_v[b + 1, half]).then_inc(x_landed[half], 16)

                        for half in range(HALVES):
                            tile(0, half, True)
                        with sp.Fori(1, B - 1) as b:
                            for half in range(HALVES):
                                tile(b, half, True)
                        for half in range(HALVES):
                            tile(B - 1, half, False)
                        sp.wait_ge(x1_stored, 16 * B * HALVES)

                    @block.tensor
                    def _(pe):
                        def transpose_x(t, s):
                            pe.wait_ge(xn_done, SUBS * t + s + 1)
                            at_least(pe, xt_lo, SUBS * t + s)
                            for k in range(KD):
                                tr = pe.transpose(XT_B[:, k * P:(k + 1) * P], xn[:, s, k * P:(k + 1) * P], ident[:, :])
                            tr.then_inc(xt_tr, 1)

                        def in_proj(t, g, gate_half):
                            o = bank[1 if gate_half else 0]
                            if g == 0:
                                at_least(pe, t_done, SUBS * t)
                                if not gate_half:
                                    pe.wait_ge(xt_lo, SUBS * t + SUBS)
                            elif gate_half:
                                pe.wait_ge(gate_done, GROUPS * t + g)
                            else:
                                pe.wait_ge(p_lo_done, GROUPS * t + g)
                            c = (I if gate_half else 0) + g * P
                            product3(pe, o[:, :], [(in_w[:, 0, k, c:c + P], in_w[:, 1, k, c:c + P],
                                                    xT[:, 0, k, :], xT[:, 1, k, :]) for k in range(KD)])\
                                .then_inc(ipg if gate_half else iph, 1)

                        def conv(t, g):
                            o = bank[2 + g % 2]
                            if g < 2:
                                at_least(pe, x1_done, SUBS * t)
                            else:
                                pe.wait_ge(h_done, GROUPS * t + g - 1)
                            pe.wait_ge(p_halo, GROUPS * t + g + 1)
                            pe.wait_ge(p_ready, GROUPS * t + g + 1)
                            product3(pe, o[:, :], [(conv_w[:, 0, g, k, :], conv_w[:, 1, g, k, :],
                                                    pp[:, g % 2, 0, k:k + TILE], pp[:, g % 2, 1, k:k + TILE])
                                                   for k in range(TAPS)]).then_inc(conv_done, 1)

                        def fc(t, s):
                            if s == 0:
                                pe.wait_ge(p_lo_done, GROUPS * t + GROUPS)
                            elif s == 1:
                                pe.wait_ge(gate_done, GROUPS * t + GROUPS)
                            else:
                                pe.wait_ge(h_done, GROUPS * t + GROUPS - 3 + s)
                            r = slice(s * P, (s + 1) * P)
                            for g in range(KI):
                                if s == 0:
                                    pe.wait_ge(h_lo, GROUPS * t + g + 1)
                                mm = product3(pe, bank[s][:, :], [(hT[:, 0, g, r], hT[:, 1, g, r],
                                                                   fc_w[:, 0, g, :], fc_w[:, 1, g, :])],
                                              start=(g == 0), stop=(g == KI - 1))
                            mm.then_inc(fc_done, 1)

                        def stats(t):
                            pe.wait_ge(h_sum, GROUPS * t + GROUPS)
                            pe.wait_ge(q_sum, GROUPS * t + GROUPS)
                            for n, v in enumerate((hsum, qsum)):
                                for s in range(SUBS):
                                    c = n * SUBS + s
                                    mm = pe.matmul(ST_B[:, c:c + 1], v[:, s * P:(s + 1) * P], ones1[:, :],
                                                   start=True, stop=True)
                            mm.then_inc(stats_done, 1)

                        def out_h(t, s):
                            if s == 1:
                                pe.wait_ge(ln2_e2, t + 1)
                            elif s >= 2:
                                pe.wait_ge(t_done, SUBS * t + s + 1)
                            r = slice(s * P, (s + 1) * P)
                            mm = product3(pe, bank[OUT_BANK[s]][:, :],
                                          [(hT[:, 0, g, r], hT[:, 1, g, r], out_w[:, 0, g, :], out_w[:, 1, g, :])
                                           for g in range(KI)], stop=False)
                            if s == SUBS - 1:
                                mm.then_inc(h_used, 1)

                        def transpose_m(t, s):
                            pe.wait_ge(silu_done, SUBS * t + s + 1)
                            pe.wait_ge(mt_lo, SUBS * t + s)
                            for k in range(KD):
                                tr = pe.transpose(MT_B[:, k * P:(k + 1) * P], mm_s[:, s, k * P:(k + 1) * P], ident[:, :])
                            tr.then_inc(mt_tr, 1)

                        def out_m(t, s):
                            pe.wait_ge(mt_lo, SUBS * t + s + 1)
                            product3(pe, bank[OUT_BANK[s]][:, :],
                                     [(mT[:, s % 2, 0, k, :], mT[:, s % 2, 1, k, :], w2[:, 0, k, :], w2[:, 1, k, :])
                                      for k in range(KD)], start=False).then_inc(out_done, 1)

                        def tile(b, half, more):
                            t = HALVES * b + half
                            for g in range(GROUPS + 1):
                                if g < GROUPS:
                                    in_proj(t, g, False)
                                    in_proj(t, g, True)
                                if g >= 1:
                                    conv(t, g - 1)
                            fc(t, 0)
                            fc(t, 1)
                            stats(t)
                            fc(t, 2)
                            fc(t, 3)
                            if more:
                                transpose_x(t + 1, 0)
                            out_h(t, 0)
                            transpose_m(t, 0)
                            out_h(t, 1)
                            if more:
                                transpose_x(t + 1, 1)
                            out_m(t, 0)
                            transpose_m(t, 1)
                            out_h(t, 2)
                            if more:
                                transpose_x(t + 1, 2)
                            out_m(t, 1)
                            transpose_m(t, 2)
                            out_h(t, 3)
                            out_m(t, 2)
                            transpose_m(t, 3)
                            if more:
                                transpose_x(t + 1, 3)
                            out_m(t, 3)

                        pe.wait_ge(a_one, 1)
                        for s in range(SUBS):
                            transpose_x(0, s)
                        for half in range(HALVES):
                            tile(0, half, True)
                        with pe.Fori(1, B - 1) as b:
                            for half in range(HALVES):
                                tile(b, half, True)
                        tile(B - 1, 0, True)
                        tile(B - 1, 1, False)

                    @block.scalar
                    def _(act):
                        def xt_hi_part(t, s):
                            act.wait_ge(xt_tr, SUBS * t + s + 1)
                            at_least(act, ipg, GROUPS * t)
                            act.activation(xT[:, 0, :, s * P:(s + 1) * P],
                                           XT_B[:, :].rearrange("p (k n) -> p k n", k=KD), ACT.Copy)\
                               .then_inc(xt_hi, 1)

                        def mt_hi_part(t, s):
                            act.wait_ge(mt_tr, SUBS * t + s + 1)
                            at_least(act, out_done, SUBS * t + max(s - 1, 0))
                            act.activation(mT[:, s % 2, 0, :, :], MT_B[:, :].rearrange("p (k n) -> p k n", k=KD),
                                           ACT.Copy, scale=MID_SCALE).then_inc(mt_hi, 1)

                        def normalise(t, half, s):
                            if s == 0:
                                act.wait_ge(nb_done, t + 1)
                                at_least(act, xt_tr, SUBS * t)
                            act.activation(xn[:, s, :], xs[:, half, s, :], ACT.Identity, bias=nb[:, s:s + 1],
                                           scale=rs[:, s:s + 1]).then_inc(xn_done, 1)

                        def silu_m(t, s):
                            act.wait_ge(u_done, SUBS * t + s + 1)
                            at_least(act, mt_tr, SUBS * t)
                            act.activation(mm_s[:, s, :], ub[:, s % 2, :], ACT.Silu).then_inc(silu_done, 1)

                        def tile(b, half, more):
                            t = HALVES * b + half
                            for g in range(GROUPS + 1):
                                if g < GROUPS:
                                    before = GROUPS * t + max(g - 1, 0)
                                    act.wait_ge(iph, GROUPS * t + g + 1)
                                    at_least(act, conv_done, before)
                                    act.activation(pp[:, g % 2, 0, HALO:HALO + TILE], bank[0][:, :], ACT.Copy,
                                                   scale=P_SCALE / (W_SCALE * LN_SCALE)).then_inc(p_hi_done, 1)
                                    act.wait_ge(ipg, GROUPS * t + g + 1)
                                    at_least(act, h_done, before)
                                    act.activation(gate[:, g % 2, :], bank[1][:, :], ACT.Silu,
                                                   scale=1.0 / (W_SCALE * LN_SCALE)).then_inc(gate_done, 1)
                                if g >= 1:
                                    q = g - 1
                                    act.wait_ge(h_done, GROUPS * t + q + 1)
                                    if q == 0:
                                        at_least(act, h_used, t)
                                    act.activation(hT[:, 0, q, :], hh[:, q % 2, :], ACT.Copy,
                                                   scale=H_SCALE / (P_SCALE * W_SCALE)).then_inc(h_hi, 1)
                                    at_least(act, q_sum, GROUPS * t + max(q - 1, 0))
                                    act.activation(sq[:, q % 2, :], hh[:, q % 2, :], ACT.Square,
                                                   scale=1.0 / (P_SCALE * W_SCALE)).then_inc(h_sq, 1)
                            if more:
                                for s in range(SUBS):
                                    normalise(t + 1, 1 - half, s)
                            silu_m(t, 0)
                            silu_m(t, 1)
                            silu_m(t, 2)
                            if more:
                                xt_hi_part(t + 1, 0)
                            silu_m(t, 3)
                            mt_hi_part(t, 0)
                            if more:
                                xt_hi_part(t + 1, 1)
                            mt_hi_part(t, 1)
                            if more:
                                xt_hi_part(t + 1, 2)
                            mt_hi_part(t, 2)
                            mt_hi_part(t, 3)
                            if more:
                                xt_hi_part(t + 1, 3)

                        for s in range(SUBS):
                            normalise(0, 0, s)
                        for s in range(SUBS):
                            xt_hi_part(0, s)
                        for half in range(HALVES):
                            tile(0, half, True)
                        with act.Fori(1, B - 1) as b:
                            for half in range(HALVES):
                                tile(b, half, True)
                        tile(B - 1, 0, True)
                        tile(B - 1, 1, False)

                    @block.vector
                    def _(dve):
                        def ln_stats(t, half, s, b_use):
                            if s == 0:
                                dve.wait_ge(x_landed[half], 16 * (b_use + 1))
                            dve.bn_stats(bn[:, s, :], xs[:, half, s, :]).then_inc(bn_done, 1)

                        def ln_var(t):
                            carry(dve, pad_dve[:, :], (bn_done, SUBS * t + SUBS), (xn_done, SUBS * t))
                            for s in range(SUBS):
                                ins = dve.bn_aggr(mv[:, s, :], bn[:, s, :])
                            ins.then_inc(mv_done, 1)
                            dve.wait_ge(mv_done, t + 1)
                            dve.tensor_scalar(nm[:, :], mv[:, :, 0], -1.0, None, ALU.mult).then_inc(nm_done, 1)
                            dve.tensor_scalar(va[:, :], mv[:, :, 1], EPS, LN_SCALE ** -2, ALU.add, ALU.mult)\
                               .then_inc(va_done, 1)

                        def xt_lo_part(t, s):
                            dve.wait_ge(xt_hi, SUBS * t + s + 1)
                            r = slice(s * P, (s + 1) * P)
                            dve.tensor_tensor(xT[:, 1, :, r], XT_B[:, :].rearrange("p (k n) -> p k n", k=KD),
                                              xT[:, 0, :, r], ALU.subtract).then_inc(xt_lo, 1)

                        def p_part(t, half, g):
                            n = GROUPS * t + g + 1
                            sl = g % 2
                            at_least(dve, conv_done, GROUPS * t + max(g - 1, 0))
                            if half == 0:
                                dve.memset(pp[:, sl, :, 0:HALO], 0.0).then_inc(p_halo, 1)
                            else:
                                dve.tensor_copy(pp[:, sl, :, 0:HALO], tails[:, g, :, :]).then_inc(p_halo, 1)
                            dve.wait_ge(p_hi_done, n)
                            dve.scalar_tensor_tensor(pp[:, sl, 1, HALO:HALO + TILE], bank[0][:, :],
                                                     P_SCALE / (W_SCALE * LN_SCALE), pp[:, sl, 0, HALO:HALO + TILE],
                                                     ALU.mult, ALU.subtract).then_inc(p_lo_done, 1)
                            dve.wait_ge(p_lo_done, n)
                            dve.wait_ge(p_halo, n)
                            dve.tensor_copy(tails[:, g, :, :], pp[:, sl, :, TILE:TILE + HALO]).then_inc(p_ready, 1)

                        def h_part(t, g):
                            n = GROUPS * t + g + 1
                            before = GROUPS * t + max(g - 1, 0)
                            dve.wait_ge(conv_done, n)
                            dve.wait_ge(gate_done, n)
                            at_least(dve, h_hi, before)
                            at_least(dve, h_sq, before)
                            at_least(dve, h_sum, before)
                            dve.scalar_tensor_tensor(hh[:, g % 2, :], bank[2 + g % 2][:, :], conv_bs[:, g:g + 1],
                                                     gate[:, g % 2, :], ALU.add, ALU.mult).then_inc(h_done, 1)

                        def h_lo_part(t, g):
                            dve.wait_ge(h_hi, GROUPS * t + g + 1)
                            dve.scalar_tensor_tensor(hT[:, 1, g, :], hh[:, g % 2, :], H_SCALE / (P_SCALE * W_SCALE),
                                                     hT[:, 0, g, :], ALU.mult, ALU.subtract).then_inc(h_lo, 1)

                        def ln2_stats(t):
                            dve.wait_ge(stats_done, t + 1)
                            dve.tensor_scalar(mneg[:, :], ST_B[:, 0:SUBS], -1.0 / (P_SCALE * W_SCALE * I), None, ALU.mult)\
                               .then_inc(ln2_mneg, 1)
                            dve.tensor_scalar(e2[:, :], ST_B[:, SUBS:2 * SUBS], FC_SQ / I, EPS * FC_SQ, ALU.mult, ALU.add)\
                               .then_inc(ln2_e2, 1)
                            dve.wait_ge(ln2_mneg, t + 1)
                            dve.scalar_tensor_tensor(msq[:, :], mneg[:, :], FC_SQ, mneg[:, :], ALU.mult, ALU.mult)\
                               .then_inc(ln2_msq, 1)
                            dve.wait_ge(ln2_msq, t + 1)
                            dve.wait_ge(ln2_e2, t + 1)
                            dve.tensor_tensor(v2[:, :], e2[:, :], msq[:, :], ALU.subtract).then_inc(ln2_v, 1)

                        def tu(t, s):
                            n = SUBS * t + s + 1
                            dve.wait_ge(fc_done, n)
                            dve.scalar_tensor_tensor(tb[:, s % 2, :], fc_g_row[:, :], mneg[:, s:s + 1], bank[s][:, :],
                                                     ALU.mult, ALU.add).then_inc(t_done, 1)
                            if s == 0:
                                dve.wait_ge(ln2_r, t + 1)
                            dve.wait_ge(t_done, n)
                            at_least(dve, silu_done, SUBS * t + max(s - 1, 0))
                            dve.scalar_tensor_tensor(ub[:, s % 2, :], tb[:, s % 2, :], r2[:, s:s + 1], fc_b_row[:, :],
                                                     ALU.mult, ALU.add).then_inc(u_done, 1)

                        def mt_lo_part(t, s):
                            dve.wait_ge(mt_hi, SUBS * t + s + 1)
                            dve.scalar_tensor_tensor(mT[:, s % 2, 1, :, :], MT_B[:, :].rearrange("p (k n) -> p k n", k=KD),
                                                     MID_SCALE, mT[:, s % 2, 0, :, :], ALU.mult, ALU.subtract)\
                               .then_inc(mt_lo, 1)

                        def x1_part(t, half, s):
                            dve.wait_ge(out_done, SUBS * t + s + 1)
                            if s == 0:
                                dve.wait_ge(resid_done, SUBS * t + SUBS)
                                at_least(dve, x1_stored, 16 * t)
                            dve.scalar_tensor_tensor(x1o[:, s, :], bank[OUT_BANK[s]][:, :], 1.0 / (H_SCALE * W_SCALE),
                                                     xs[:, half, s, :], ALU.mult, ALU.add).then_inc(x1_done, 1)

                        def tile(b, half, more):
                            t = HALVES * b + half
                            for g in range(GROUPS + 1):
                                if g < GROUPS:
                                    p_part(t, half, g)
                                if more and 2 <= g < 2 + SUBS:
                                    ln_stats(t + 1, 1 - half, g - 2, b + half)
                                if more and g == 2 + SUBS:
                                    ln_var(t + 1)
                                if g >= 1:
                                    h_part(t, g - 1)
                                    h_lo_part(t, g - 1)
                            ln2_stats(t)
                            for s in range(SUBS):
                                tu(t, s)
                            if more:
                                xt_lo_part(t + 1, 0)
                            mt_lo_part(t, 0)
                            if more:
                                xt_lo_part(t + 1, 1)
                            x1_part(t, half, 0)
                            mt_lo_part(t, 1)
                            if more:
                                xt_lo_part(t + 1, 2)
                            x1_part(t, half, 1)
                            mt_lo_part(t, 2)
                            x1_part(t, half, 2)
                            mt_lo_part(t, 3)
                            if more:
                                xt_lo_part(t + 1, 3)
                            x1_part(t, half, 3)

                        dve.memset(ones1[:, :], 1.0).then_inc(a_one, 1)
                        for s in range(SUBS):
                            ln_stats(0, 0, s, 0)
                        ln_var(0)
                        for s in range(SUBS):
                            xt_lo_part(0, s)
                        for half in range(HALVES):
                            tile(0, half, True)
                        with dve.Fori(1, B - 1) as b:
                            for half in range(HALVES):
                                tile(b, half, True)
                        tile(B - 1, 0, True)
                        tile(B - 1, 1, False)

                    @block.gpsimd
                    def _(pool):
                        def factors(t):
                            pool.wait_ge(va_done, t + 1)
                            pool.wait_ge(nm_done, t + 1)
                            pool.tensor_tensor(rs[:, :], va[:, :], mhalf[:, :], ALU.pow).then_inc(rs_done, 1)
                            at_least(pool, rs_done, t + 1)
                            pool.tensor_tensor(nb[:, :], nm[:, :], rs[:, :], ALU.mult).then_inc(nb_done, 1)

                        def residual(t, half):
                            for s in range(SUBS):
                                pool.wait_ge(xn_done, SUBS * t + s + 1)
                                pool.tensor_tensor(xs[:, half, s, :], xs[:, half, s, :], out_b_row[:, :], ALU.add)\
                                    .then_inc(resid_done, 1)

                        def tile(b, half, more):
                            t = HALVES * b + half
                            for g in range(GROUPS):
                                n = GROUPS * t + g
                                pool.wait_ge(h_done, n + 1)
                                if g == 0:
                                    at_least(pool, stats_done, t)
                                    pool.tensor_tensor(hsum[:, :], zero[:, :], hh[:, 0, :], ALU.add).then_inc(h_sum, 1)
                                    pool.wait_ge(h_sq, n + 1)
                                    pool.tensor_tensor(qsum[:, :], zero[:, :], sq[:, 0, :], ALU.add).then_inc(q_sum, 1)
                                else:
                                    pool.wait_ge(h_sum, n)
                                    pool.tensor_tensor(hsum[:, :], hsum[:, :], hh[:, g % 2, :], ALU.add).then_inc(h_sum, 1)
                                    pool.wait_ge(h_sq, n + 1)
                                    pool.wait_ge(q_sum, n)
                                    pool.tensor_tensor(qsum[:, :], qsum[:, :], sq[:, g % 2, :], ALU.add).then_inc(q_sum, 1)
                                if more and g == GROUPS - 1:
                                    factors(t + 1)
                            pool.wait_ge(ln2_v, t + 1)
                            pool.tensor_tensor(r2[:, :], v2[:, :], mhalf[:, :], ALU.pow).then_inc(ln2_r, 1)
                            if more:
                                residual(t + 1, 1 - half)

                        pool.memset(zero[:, :], 0.0).then_inc(a_zero, 1)
                        pool.wait_ge(a_zero, 1)
                        factors(0)
                        residual(0, 0)
                        for half in range(HALVES):
                            tile(0, half, True)
                        with pool.Fori(1, B - 1) as b:
                            for half in range(HALVES):
                                tile(b, half, True)
                        tile(B - 1, 0, True)
                        tile(B - 1, 1, False)

        phb = ExitStack()
        with phb:
            cb_ = sb_in(phb)
            RING = BSUBS
            xr = cb_("xr", [P, RING, D])
            m_w = cb_("m_w", [P, B, 2, KD, HEADS * KEYS], F16)
            vw_w = cb_("vw_w", [P, B, 2, PAIRS, D], F16)
            we_w = cb_("we_w", [P, 2, KD, D], F16)
            wg_w = cb_("wg_w", [P, 2, KD, E], F16)
            we_raw = cb_("we_raw", [P, KD, D])
            wg_raw = cb_("wg_raw", [P, KD, E])
            be_raw = cb_("be_raw", [P, D])
            be_hi = cb_("be_hi", [P, D], F16)
            be_w = cb_("be_w", [P, D], F16)
            be_one = cb_("be_one", [P, P], F16)
            bo_row = cb_("bo_row", [P, D])
            maskb = cb_("maskb", [P, NSUB, KEYS])
            attends = cb_("attends", [P, NSUB])
            bn2, mv2, va2, rs2 = cb_("bn2", [P, 6]), cb_("mv2", [P, 2, 2]), cb_("va2", [P, 2]), cb_("rs2", [P, 2])
            bn3, mv3, va3, rs3 = cb_("bn3", [P, 6]), cb_("mv3", [P, 2, 2]), cb_("va3", [P, 2]), cb_("rs3", [P, 2])
            nm2, nb2 = cb_("nm2", [P, 2]), cb_("nb2", [P, 2])
            nm3, nb3 = cb_("nm3", [P, 2]), cb_("nb3", [P, 2])
            xn2, xn3 = cb_("xn2", [P, 2, D]), cb_("xn3", [P, 2, D])
            x2T, x3T = cb_("x2T", [P, 2, 2, KD, P], F16), cb_("x3T", [P, 2, 2, KD, P], F16)
            prT = cb_("prT", [P, 2, 2, PAIRS, P], F16)
            bias = cb_("bias", [P, 2, HEADS, KEYS])
            sc = cb_("sc", [P, 2, HEADS, KEYS])
            ex = cb_("ex", [P, 4, HEADS, KEYS])
            mx, su, ri, rw = (cb_("mx", [P, 2, HEADS]), cb_("su", [P, HEADS]), cb_("ri", [P, HEADS]),
                              cb_("rw", [P, 2, HEADS]))
            lm, nl, eqp, pm = cb_("lm", [P, 1]), cb_("nl", [P, 1]), cb_("eqp", [P, E]), cb_("pm", [P, 1])
            oh, seen = cb_("oh", [P, E], BF16), cb_("seen", [P, E], BF16)
            e8, den, rden = cb_("e8", [P, E]), cb_("den", [P, 1]), cb_("rden", [P, 1])
            kv, kept, gk = cb_("kv", [P, E]), cb_("kept", [P, 1]), cb_("gk", [P, 1])

            T2_B, S_B, PT_B, PV_B, T3_B, WE_B, R_B, LOC_B = bank
            S_SCALE = 1.0 / (LN_SCALE * W_SCALE)
            PV_SCALE = 1.0 / (PROB_SCALE * W_SCALE)

            w_landed = {n: sem(f"w_landed_{n}") for n in ("we", "wg", "be", "bo")}
            x1_landed = [sem(f"x1_landed{n}") for n in range(RING)]
            out_stored = [sem(f"out_stored{n}") for n in range(RING)]
            m_landed, vw_landed = [sem(f"m_landed{n}") for n in range(B)], [sem(f"vw_landed{n}") for n in range(B)]
            c_hi, c_lo, c_zero, c_mask = sem("c_hi"), sem("c_lo"), sem("c_zero"), sem("c_mask")
            bn2_done, mv2_done, va2_done, rs2_done, xn2_done = (sem("bn2_done"), sem("mv2_done"), sem("va2_done"),
                                                               sem("rs2_done"), sem("xn2_done"))
            bn3_done, mv3_done, va3_done, rs3_done, xn3_done = (sem("bn3_done"), sem("mv3_done"), sem("va3_done"),
                                                               sem("rs3_done"), sem("xn3_done"))
            nm2_done, nb2_done, nm3_done, nb3_done = sem("nm2_done"), sem("nb2_done"), sem("nm3_done"), sem("nb3_done")
            t2_tr, t2_hi, t2_lo = sem("t2_tr"), sem("t2_hi"), sem("t2_lo")
            pt_tr, pt_hi, pt_lo = sem("pt_tr"), sem("pt_hi"), sem("pt_lo")
            t3_tr, t3_hi, t3_lo = sem("t3_tr"), sem("t3_hi"), sem("t3_lo")
            s_done, pv_done, r_done, we_done, loc_done = (sem("s_done"), sem("pv_done"), sem("r_done"),
                                                          sem("we_done"), sem("loc_done"))
            bias_done, sc_done, mx_done, sub_done, ex_done = (sem("bias_done"), sem("sc_done"), sem("mx_done"),
                                                              sem("sub_done"), sem("ex_done"))
            su_done, ri_done, rw_done, pr_done, bo_done = (sem("su_done"), sem("ri_done"), sem("rw_done"),
                                                           sem("pr_done"), sem("bo_done"))
            x2_done, lm_done, nl_done, eqp_done, pm_done, oh_done = (sem("x2_done"), sem("lm_done"), sem("nl_done"),
                                                                     sem("eqp_done"), sem("pm_done"), sem("oh_done"))
            seen_done, den_done, rden_done, kept_done, gk_done, y_done = (sem("seen_done"), sem("den_done"),
                                                                          sem("rden_done"), sem("kept_done"),
                                                                          sem("gk_done"), sem("y_done"))

            LN2_AT, T2_AT, S_AT, PV_AT, WE_AT = 2, 3, 4, 6, 7
            STEPS_TAIL = WE_AT

            def real(j):
                return not isinstance(j, int) or 0 <= j < NSUB

            def steps(eng, body, loaded=lambda eng: None):
                for k in range(BSUBS):
                    body(0, k, lambda d: k - d)
                loaded(eng)
                with eng.Fori(1, B) as b:
                    for k in range(BSUBS):
                        body(b, k, lambda d: b * BSUBS + (k - d))
                for k in range(STEPS_TAIL):
                    body(B, k, lambda d: NSUB + k - d)

            with nc.Block() as block:
                @block.sync
                def _(sp):
                    kn = "(k p) n -> p k n"
                    sp.dma_start(wg_raw[:, :, :], Wg.rearrange(kn, p=P)).then_inc(w_landed["wg"], 16)
                    sp.dma_start(bo_row[:, :], bo.partition_broadcast(P)).then_inc(w_landed["bo"], 16)
                    sp.dma_start(be_raw[:, :], be.partition_broadcast(P)).then_inc(w_landed["be"], 16)

                    def step(b, k, j):
                        if real(j(0)):
                            if not isinstance(b, int):
                                sp.wait_ge(out_stored[k], 16 * b)
                            sp.dma_start(xr[:, k, :], x1_dram[b * HALVES + k // SUBS, :, k % SUBS, :])\
                              .then_inc(x1_landed[k], 16)
                        if isinstance(b, int) and b == 0:
                            if k == 1:
                                sp.dma_start(m_w[:, 0], m_dram[0]).then_inc(m_landed[0], 16)
                            elif k == 2:
                                sp.dma_start(vw_w[:, 0], vw_dram[0]).then_inc(vw_landed[0], 16)
                                sp.dma_start(we_raw[:, :, :], We.rearrange(kn, p=P)).then_inc(w_landed["we"], 16)
                            elif 4 <= k < 4 + B - 1:
                                sp.dma_start(m_w[:, k - 3], m_dram[k - 3]).then_inc(m_landed[k - 3], 16)
                                sp.dma_start(vw_w[:, k - 3], vw_dram[k - 3]).then_inc(vw_landed[k - 3], 16)
                        y = j(WE_AT)
                        if real(y):
                            sp.wait_ge(y_done, y + 1)
                            slot = (k - WE_AT) % RING
                            yb = b if k >= WE_AT else b - 1
                            sp.dma_start(out_v[yb * BSUBS + slot], xr[:, slot, :]).then_inc(out_stored[slot], 16)

                    steps(sp, step)
                    for n in range(RING):
                        sp.wait_ge(out_stored[n], 16 * B)

                @block.tensor
                def _(pe):
                    def transpose4(dst, src, done):
                        for c in range(KD):
                            tr = pe.transpose(dst[:, c * P:(c + 1) * P], src[:, c * P:(c + 1) * P], ident[:, :])
                        tr.then_inc(done, 1)

                    def pairs(lhs, rhs, chunks):
                        return [(lhs[:, 0, c, :], lhs[:, 1, c, :], rhs[:, 0, c, :], rhs[:, 1, c, :])
                                for c in range(chunks)]

                    def batch_of(w, b):
                        return w[:, b] if isinstance(b, int) else w[:, bass.ds(b, 1)].rearrange("p b t k n -> p (b t) k n")

                    def step(b, k, j):
                        p, t, s, w = j(PV_AT), j(T2_AT), j(S_AT), j(WE_AT)
                        if real(p):
                            pe.wait_ge(pr_done, p + 1)
                            at_least(pe, pt_lo, p)
                            transpose4(PT_B, ex[:, (k - PV_AT) % 4, :, :].rearrange("p h n -> p (h n)"), pt_tr)
                        if real(t):
                            pe.wait_ge(xn2_done, t + 1)
                            at_least(pe, t2_lo, t)
                            transpose4(T2_B, xn2[:, (k - T2_AT) % 2, :], t2_tr)
                        if real(s):
                            sb_ = b if k >= S_AT else b - 1
                            if isinstance(b, int) and s == 0:
                                pe.wait_ge(m_landed[0], 16)
                            pe.wait_ge(t2_lo, s + 1)
                            at_least(pe, sc_done, s)
                            product3(pe, S_B[:, :], pairs(x2T[:, (k - S_AT) % 2], batch_of(m_w, sb_), KD)).then_inc(s_done, 1)
                        if real(w):
                            pe.wait_ge(xn3_done, w + 1)
                            at_least(pe, t3_lo, w)
                            transpose4(T3_B, xn3[:, (k - WE_AT) % 2, :], t3_tr)
                        if real(p):
                            pb_ = b if k >= PV_AT else b - 1
                            if isinstance(b, int) and p == 0:
                                pe.wait_ge(vw_landed[0], 16)
                                pe.wait_ge(c_lo, 3)
                            pe.wait_ge(pt_lo, p + 1)
                            at_least(pe, x2_done, p)
                            product3(pe, PV_B[:, :], pairs(prT[:, (k - PV_AT) % 2], batch_of(vw_w, pb_), PAIRS)).then_inc(pv_done, 1)
                        if real(w):
                            x3 = x3T[:, (k - WE_AT) % 2]
                            pe.wait_ge(t3_lo, w + 1)
                            at_least(pe, eqp_done, w)
                            at_least(pe, den_done, w)
                            product3(pe, R_B[:, 0:E], pairs(x3, wg_w, KD)).then_inc(r_done, 1)
                            at_least(pe, y_done, w)
                            product3(pe, WE_B[:, :], pairs(x3, we_w, KD), stop=False)
                            pe.matmul(WE_B[:, :], be_one[:, :], be_w[:, :], start=False, stop=True).then_inc(we_done, 1)
                            pe.wait_ge(oh_done, w + 1)
                            at_least(pe, kept_done, w)
                            pe.wait_ge(seen_done, w + 1)
                            pe.matmul(LOC_B[:, 0:E], tri[:, :], oh[:, :], start=True, stop=False)
                            pe.matmul(LOC_B[:, 0:E], ones_b[:, :], seen[:, :], start=False, stop=True)\
                              .then_inc(loc_done, 1)

                    def all_loaded(pe):
                        for n in range(1, B):
                            pe.wait_ge(m_landed[n], 16)
                            pe.wait_ge(vw_landed[n], 16)

                    steps(pe, step, all_loaded)

                @block.scalar
                def _(act):
                    act.wait_ge(w_landed["we"], 16)
                    act.activation(we_w[:, 0, :, :], we_raw[:, :, :], ACT.Copy, scale=W_SCALE).then_inc(c_hi, 1)
                    act.wait_ge(w_landed["wg"], 16)
                    act.activation(wg_w[:, 0, :, :], wg_raw[:, :, :], ACT.Copy, scale=W_SCALE).then_inc(c_hi, 1)
                    act.wait_ge(w_landed["be"], 16)
                    act.activation(be_hi[:, :], be_raw[:, :], ACT.Copy, scale=W_SCALE).then_inc(c_hi, 1)

                    def normalise(n, q, src, xn, rs, nb, nb_done, tr, xn_done):
                        act.wait_ge(nb_done, n + 1)
                        at_least(act, tr, n - 1)
                        act.activation(xn[:, q, :], src, ACT.Identity, bias=nb[:, q:q + 1], scale=rs[:, q:q + 1])\
                           .then_inc(xn_done, 1)

                    def hi_part(n, tr, dst, src, done, scale=1.0):
                        act.wait_ge(tr, n + 1)
                        act.activation(dst, src[:, :].rearrange("p (k n) -> p k n", k=KD), ACT.Copy, scale=scale)\
                           .then_inc(done, 1)

                    def step(b, k, j):
                        l, p, t, s, w = j(LN2_AT), j(PV_AT), j(T2_AT), j(S_AT), j(WE_AT)
                        if real(p):
                            hi_part(p, pt_tr, prT[:, (k - PV_AT) % 2, 0], PT_B, pt_hi, PROB_SCALE)
                        if real(t):
                            hi_part(t, t2_tr, x2T[:, (k - T2_AT) % 2, 0], T2_B, t2_hi)
                        if real(l):
                            normalise(l, k % 2, xr[:, (k - LN2_AT) % RING, :], xn2, rs2, nb2, nb2_done, t2_tr, xn2_done)
                        if real(w):
                            hi_part(w, t3_tr, x3T[:, (k - WE_AT) % 2, 0], T3_B, t3_hi)
                        if real(s):
                            act.wait_ge(sub_done, s + 1)
                            at_least(act, pt_tr, s - 3)
                            act.activation(ex[:, (k - S_AT) % 4, :, :], sc[:, (k - S_AT) % 2, :, :], ACT.Exp)\
                               .then_inc(ex_done, 1)
                        if real(p):
                            normalise(p, k % 2, xr[:, (k - PV_AT) % RING, :], xn3, rs3, nb3, nb3_done, t3_tr, xn3_done)
                        if real(w):
                            act.wait_ge(r_done, w + 1)
                            act.wait_ge(nl_done, w + 1)
                            act.wait_ge(eqp_done, w + 1)
                            at_least(act, rden_done, w)
                            act.activation(e8[:, :], R_B[:, 0:E], ACT.Exp, bias=nl[:, :], scale=S_SCALE,
                                           accum_out=den[:, :]).then_inc(den_done, 1)

                    steps(act, step)

                @block.gpsimd
                def _(pool):
                    pool.memset(be_w[:, :], 0.0).then_inc(c_zero, 1)
                    pool.memset(be_one[:, :], LN_SCALE).then_inc(c_zero, 1)

                    def factors(n, q, va, nm, rs, nb, va_done, nm_done, rs_done, xn_done, nb_done):
                        pool.wait_ge(va_done, n + 1)
                        pool.wait_ge(nm_done, n + 1)
                        at_least(pool, xn_done, n - 1)
                        pool.tensor_tensor(rs[:, q:q + 1], va[:, q:q + 1], mhalf[:, 0:1], ALU.pow).then_inc(rs_done, 1)
                        pool.wait_ge(rs_done, n + 1)
                        pool.tensor_tensor(nb[:, q:q + 1], nm[:, q:q + 1], rs[:, q:q + 1], ALU.mult).then_inc(nb_done, 1)

                    def step(b, k, j):
                        l, t, s, p = j(LN2_AT), j(T2_AT), j(S_AT), j(PV_AT)
                        if real(l):
                            factors(l, k % 2, va2, nm2, rs2, nb2, va2_done, nm2_done, rs2_done, xn2_done, nb2_done)
                        if real(t):
                            q = (k - T2_AT) % 2
                            tb_ = b if k >= T2_AT else b - 1
                            at_least(pool, sc_done, t - 1)
                            pool.tensor_tensor(bias[:, q, :, :],
                                               hbias[:, tb_, :].rearrange("p (h n) -> p h n", h=HEADS),
                                               maskb[:, t, :].unsqueeze(1).to_broadcast([P, HEADS, KEYS]), ALU.add)\
                                .then_inc(bias_done, 1)
                        if real(s):
                            q = (k - S_AT) % 2
                            pool.wait_ge(mx_done, s + 1)
                            pool.tensor_tensor(sc[:, q, :, :], sc[:, q, :, :],
                                               mx[:, q, :].unsqueeze(2).to_broadcast([P, HEADS, KEYS]),
                                               ALU.subtract).then_inc(sub_done, 1)
                        if real(p):
                            factors(p, k % 2, va3, nm3, rs3, nb3, va3_done, nm3_done, rs3_done, xn3_done, nb3_done)
                        if real(s):
                            q = (k - S_AT) % 4
                            pool.wait_ge(rw_done, s + 1)
                            pool.tensor_tensor(ex[:, q, :, :], ex[:, q, :, :],
                                               rw[:, (k - S_AT) % 2, :].unsqueeze(2).to_broadcast([P, HEADS, KEYS]),
                                               ALU.mult).then_inc(pr_done, 1)
                        if real(l):
                            pool.wait_ge(xn2_done, l + 1)
                            r = xr[:, (k - LN2_AT) % RING, :]
                            pool.tensor_tensor(r, r, bo_row[:, :], ALU.add).then_inc(bo_done, 1)

                    pool.wait_ge(c_mask, 1)
                    pool.wait_ge(w_landed["bo"], 16)
                    steps(pool, step)

                @block.vector
                def _(dve):
                    dve.wait_ge(c_hi, 1)
                    dve.scalar_tensor_tensor(we_w[:, 1, :, :].rearrange("p k n -> p (k n)"),
                                             we_raw[:, :, :].rearrange("p k n -> p (k n)"), W_SCALE,
                                             we_w[:, 0, :, :].rearrange("p k n -> p (k n)"),
                                             ALU.mult, ALU.subtract).then_inc(c_lo, 1)
                    dve.wait_ge(c_hi, 2)
                    dve.scalar_tensor_tensor(wg_w[:, 1, :, :], wg_raw[:, :, :], W_SCALE, wg_w[:, 0, :, :],
                                             ALU.mult, ALU.subtract).then_inc(c_lo, 1)
                    dve.wait_ge(c_hi, 3)
                    dve.wait_ge(c_zero, 2)
                    dve.tensor_copy(be_w[0:1, :], be_hi[0:1, :])
                    dve.scalar_tensor_tensor(be_w[32:33, :], be_raw[32:33, :], W_SCALE, be_hi[32:33, :],
                                             ALU.mult, ALU.subtract).then_inc(c_lo, 1)
                    dve.tensor_scalar(maskb[:, :, :], masku[:, :, :], BIG, -BIG, ALU.mult, ALU.add).then_inc(c_mask, 1)
                    dve.tensor_reduce(attends[:, :], masku[:, :, :], AX.X, ALU.max).then_inc(c_mask, 1)
                    dve.memset(seen[:, :], 0.0).then_inc(seen_done, 1)
                    dve.wait_ge(c_mask, 2)

                    def stats(n, q, src, bn_, mv, nm, va, bn_done, mv_done, nm_done, va_done, nb_done):
                        dve.bn_stats(bn_[:, :], src).then_inc(bn_done, 1)
                        carry(dve, pad_dve[:, :], (bn_done, n + 1))
                        dve.bn_aggr(mv[:, q, :], bn_[:, :]).then_inc(mv_done, 1)
                        dve.wait_ge(mv_done, n + 1)
                        at_least(dve, nb_done, n - 1)
                        dve.tensor_scalar(nm[:, q:q + 1], mv[:, q, 0:1], -1.0, None, ALU.mult).then_inc(nm_done, 1)
                        dve.tensor_scalar(va[:, q:q + 1], mv[:, q, 1:2], EPS, LN_SCALE ** -2, ALU.add, ALU.mult)\
                           .then_inc(va_done, 1)

                    def lo_part(n, hi, slot, src, done, scale=1.0):
                        dve.wait_ge(hi, n + 1)
                        dve.scalar_tensor_tensor(slot[:, 1], src[:, :].rearrange("p (k n) -> p k n", k=KD), scale,
                                                 slot[:, 0], ALU.mult, ALU.subtract).then_inc(done, 1)

                    def step(b, k, j):
                        l, t, s, p, w = j(LN2_AT), j(T2_AT), j(S_AT), j(PV_AT), j(WE_AT)
                        if real(p):
                            lo_part(p, pt_hi, prT[:, (k - PV_AT) % 2], PT_B, pt_lo, PROB_SCALE)
                        if real(t):
                            lo_part(t, t2_hi, x2T[:, (k - T2_AT) % 2], T2_B, t2_lo)
                        if real(l):
                            slot = (k - LN2_AT) % RING
                            lb = b if k >= LN2_AT else b - 1
                            dve.wait_ge(x1_landed[slot], 16 * lb + 16)
                            stats(l, k % 2, xr[:, slot, :], bn2, mv2, nm2, va2, bn2_done, mv2_done, nm2_done,
                                  va2_done, nb2_done)
                        if real(s):
                            q = (k - S_AT) % 2
                            dve.wait_ge(s_done, s + 1)
                            dve.wait_ge(bias_done, s + 1)
                            at_least(dve, ex_done, s - 1)
                            dve.scalar_tensor_tensor(sc[:, q, :, :].rearrange("p h n -> p (h n)"), S_B[:, :], S_SCALE,
                                                     bias[:, q, :, :].rearrange("p h n -> p (h n)"),
                                                     ALU.mult, ALU.add).then_inc(sc_done, 1)
                        if real(w):
                            lo_part(w, t3_hi, x3T[:, (k - WE_AT) % 2], T3_B, t3_lo)
                        if real(s):
                            q = (k - S_AT) % 2
                            dve.wait_ge(sc_done, s + 1)
                            at_least(dve, sub_done, s - 1)
                            dve.tensor_reduce(mx[:, q, :], sc[:, q, :, :], AX.X, ALU.max).then_inc(mx_done, 1)
                        if real(p):
                            r = xr[:, (k - PV_AT) % RING, :]
                            dve.wait_ge(pv_done, p + 1)
                            dve.wait_ge(bo_done, p + 1)
                            dve.scalar_tensor_tensor(r, PV_B[:, :], PV_SCALE, r, ALU.mult, ALU.add).then_inc(x2_done, 1)
                            dve.wait_ge(x2_done, p + 1)
                            stats(p, k % 2, r, bn3, mv3, nm3, va3, bn3_done, mv3_done, nm3_done, va3_done, nb3_done)
                        if real(w):
                            dve.wait_ge(r_done, w + 1)
                            dve.tensor_reduce(lm[:, :], R_B[:, 0:E], AX.X, ALU.max).then_inc(lm_done, 1)
                            dve.wait_ge(lm_done, w + 1)
                            at_least(dve, den_done, w)
                            dve.tensor_scalar(nl[:, :], lm[:, :], -S_SCALE, None, ALU.mult).then_inc(nl_done, 1)
                            dve.scalar_tensor_tensor(eqp[:, :], R_B[:, 0:E], lm[:, :], prio[:, :],
                                                     ALU.is_equal, ALU.mult).then_inc(eqp_done, 1)
                            dve.wait_ge(eqp_done, w + 1)
                            dve.tensor_reduce(pm[:, :], eqp[:, :], AX.X, ALU.max).then_inc(pm_done, 1)
                            dve.wait_ge(pm_done, w + 1)
                            at_least(dve, loc_done, w)
                            at_least(dve, kept_done, w)
                            dve.tensor_scalar(oh[:, :], eqp[:, :], pm[:, :], None, ALU.is_equal).then_inc(oh_done, 1)
                        if real(s):
                            dve.wait_ge(ex_done, s + 1)
                            dve.tensor_reduce(su[:, :], ex[:, (k - S_AT) % 4, :, :], AX.X, ALU.add).then_inc(su_done, 1)
                            dve.wait_ge(su_done, s + 1)
                            dve.reciprocal(ri[:, :], su[:, :]).then_inc(ri_done, 1)
                            dve.wait_ge(ri_done, s + 1)
                            at_least(dve, pr_done, s - 1)
                            dve.tensor_scalar(rw[:, (k - S_AT) % 2, :], ri[:, :], attends[:, bass.ds(s, 1)], None,
                                              ALU.mult).then_inc(rw_done, 1)
                        if real(w):
                            dve.wait_ge(den_done, w + 1)
                            dve.reciprocal(rden[:, :], den[:, :]).then_inc(rden_done, 1)
                            dve.wait_ge(loc_done, w + 1)
                            dve.scalar_tensor_tensor(kv[:, :], LOC_B[:, 0:E], float(CAP), oh[:, :], ALU.is_le, ALU.mult,
                                                     accum_out=kept[:, :]).then_inc(kept_done, 1)
                            dve.tensor_tensor(seen[:, :], seen[:, :], oh[:, :], ALU.add).then_inc(seen_done, 1)
                            dve.wait_ge(kept_done, w + 1)
                            dve.wait_ge(rden_done, w + 1)
                            dve.scalar_tensor_tensor(gk[:, :], kept[:, :], S_SCALE, rden[:, :], ALU.mult, ALU.mult)\
                               .then_inc(gk_done, 1)
                            dve.wait_ge(gk_done, w + 1)
                            dve.wait_ge(we_done, w + 1)
                            r = xr[:, (k - WE_AT) % RING, :]
                            dve.scalar_tensor_tensor(r, WE_B[:, :], gk[:, :], r, ALU.mult, ALU.add).then_inc(y_done, 1)

                    steps(dve, step)


def kernel(**inputs):
    import numpy as _np
    import concourse.bacc as _bacc
    from concourse import mybir as _mybir
    from concourse.bass_utils import run_bass_kernel_spmd as _run

    g = {n: _np.asarray(v) for n, v in inputs.items()}

    def columns(v):
        return v.reshape(-1, P).T

    conv = g["L0_attn_conv_w"].reshape(GROUPS, P, P, TAPS)
    layout = {
        "x": g["x"],
        "ctxT": g["ctx_1024"].reshape(B * KEYS, D).T,
        "mask": g["mask_BxSxS2_bk0"].reshape(NSUB, P, KEYS).transpose(1, 0, 2),
        "in_wT": g["L0_attn_in_proj_w"].T,
        "conv_wT": conv.transpose(2, 0, 3, 1).reshape(P, GROUPS * TAPS * P),
        "conv_b": columns(g["L0_attn_conv_b"]),
        "ln_g": columns(g["L0_attn_ln_g"]),
        "ln_b": columns(g["L0_attn_ln_b"]),
        "fc_wT": g["L0_attn_fc_w"].T,
        "fc_b": g["L0_attn_fc_b"],
        "cproj_w": g["L0_attn_cproj_w"],
        "cproj_b": columns(g["L0_attn_cproj_b"]),
        "out_wT": g["L0_attn_out_w"].T,
        "WqT": g["L0_xattn_Wq"].T,
        "bq": columns(g["L0_xattn_bq"]),
        "Wk": g["L0_xattn_Wk"],
        "bk": columns(g["L0_xattn_bk"]),
        "Wv": g["L0_xattn_Wv"],
        "bv": columns(g["L0_xattn_bv"]),
        "Wo": g["L0_xattn_Wo"],
        "bo": g["L0_xattn_bo"],
        "Wg": g["L0_ffn_Wg"],
        "We": g["L0_ffn_We"],
        "be": g["L0_ffn_be"],
        "ident": _np.eye(P, dtype=_np.float32),
        "tri": _np.triu(_np.ones((P, P), _np.float32)),
        "prio": _np.tile(_np.arange(E, 0, -1, dtype=_np.float32), (P, 1)),
    }
    nc = _bacc.Bacc("TRN2", target_bir_lowering=False, num_devices=1)
    arrays, args = {}, []
    for name, a in layout.items():
        a = _np.ascontiguousarray(a)
        arrays[f"in_{name}_dram"] = a
        args.append(nc.dram_tensor(f"in_{name}_dram", a.shape, _mybir.dt.from_np(a.dtype), kind="ExternalInput").ap())
    args.append(nc.dram_tensor("out_0_dram", (B, S, D), F32, kind="ExternalOutput").ap())
    bass_decoder_kernel(nc, *args)
    r = _run(nc, [arrays], core_ids=[0])
    return r.results[0]["out_0_dram"]
```

```python
from contextlib import ExitStack

import concourse.bass as bass
from concourse import mybir

ALU = mybir.AluOpType
ACT = mybir.ActivationFunctionType
AX = mybir.AxisListType
F32 = mybir.dt.float32
F16 = mybir.dt.float16
BF16 = mybir.dt.bfloat16

P = 128
B, S, D = 4, 1024, 512
I = 1024
MID = 512
TAPS, GROUPS = 4, 8
KEYS, HEADS = 64, 8
E = 8
CAP = B * S // E
EPS = 1e-5
TILE = 512
SUBS = TILE // P
HALVES = S // TILE
TILES = B * HALVES
KD = D // P
KI = I // P
HALO = TAPS - 1
BSUBS = S // P
NSUB = B * BSUBS
PAIRS = HEADS // 2
BIG = 1e30

W_SCALE = 2.0 ** 8
LN_SCALE = 2.0 ** 8
P_SCALE = 2.0 ** 6
H_SCALE = 2.0 ** 7
MID_SCALE = 2.0 ** 6
W2_SCALE = H_SCALE * W_SCALE / MID_SCALE
PROB_SCALE = 2.0 ** 12


def carry(dve, pad, *waits):
    for s, v in waits:
        at_least(dve, s, v)
    dve.memset(pad, 0.0)


def at_least(eng, sem, value):
    if isinstance(value, int) and value <= 0:
        return
    eng.wait_ge(sem, value)


def product3(pe, out, chunks, start=True, stop=True):
    last = len(chunks) - 1
    for n, (l_hi, l_lo, r_hi, r_lo) in enumerate(chunks):
        pe.matmul(out, l_hi, r_hi, start=start and n == 0, stop=False)
        pe.matmul(out, l_hi, r_lo, start=False, stop=False)
        mm = pe.matmul(out, l_lo, r_hi, start=False, stop=stop and n == last)
    return mm


def bass_decoder_kernel(
    nc, x, ctxT, mask, in_wT, conv_wT, conv_b, ln_g, ln_b, fc_wT, fc_b, cproj_w, cproj_b, out_wT,
    WqT, bq, Wk, bk, Wv, bv, Wo, bo, Wg, We, be, ident_in, tri_in, prio_in, out,
):
    x_v = x.rearrange("b (h s p) d -> b h p s d", h=HALVES, p=P)
    x1_dram = nc.dram_tensor("x1_scratch", (B * HALVES, P, SUBS, D), F32).ap()
    out_v = out.rearrange("b (s p) d -> (b s) p d", p=P)
    m_dram = nc.dram_tensor("m_scratch", (B, P, 2, KD, HEADS * KEYS), F16).ap()
    vw_dram = nc.dram_tensor("vw_scratch", (B, P, 2, PAIRS, D), F16).ap()

    top = ExitStack()
    with top:
        def sem(name):
            return top.enter_context(nc.semaphore(name))

        def sb_in(stack):
            return lambda name, shape, dt=F32: stack.enter_context(nc.sbuf_tensor(name, shape, dt))

        bank = [top.enter_context(nc.psum_tensor(f"bank{n}", [P, 512], F32)) for n in range(8)]

        sb = sb_in(top)
        ident = sb("ident", [P, P])
        hbias = sb("hbias", [P, B, HEADS * KEYS])
        masku = sb("masku", [P, NSUB, KEYS], mybir.dt.uint8)
        tri = sb("tri", [P, P], BF16)
        ones_b = sb("ones_b", [P, P], BF16)
        prio = sb("prio", [P, E])
        mhalf = sb("mhalf", [P, SUBS])
        pad_dve = sb("pad_dve", [P, 1])
        xs = sb("xs", [P, HALVES, SUBS, D])
        xn = sb("xn", [P, SUBS, D])
        xT = sb("xT", [P, 2, KD, TILE], F16)
        bn, mv = sb("bn", [P, SUBS, 6]), sb("mv", [P, SUBS, 2])
        va, rs = sb("va", [P, SUBS]), sb("rs", [P, SUBS])
        nm, nb = sb("nm", [P, SUBS]), sb("nb", [P, SUBS])
        in_w = sb("in_w", [P, 2, KD, 2 * I], F16)
        conv_fc_w = sb("conv_fc_w", [P, 2 * GROUPS * TAPS * P + 2 * KI * MID], F16)
        conv_w = conv_fc_w[:, 0:2 * GROUPS * TAPS * P].rearrange("p (t g k o) -> p t g k o", t=2, g=GROUPS, k=TAPS)
        fc_w = conv_fc_w[:, 2 * GROUPS * TAPS * P:].rearrange("p (t k n) -> p t k n", t=2, k=KI)
        m_w = in_w[:, :, :, :].rearrange("p t k n -> p (t k n)").rearrange(
            "p (b t k n) -> p b t k n", b=B, t=2, k=KD)
        vw_w = conv_fc_w[:, :].rearrange("p (b t k n) -> p b t k n", b=B, t=2, k=PAIRS)

        mid_stack = ExitStack()
        mb = sb_in(mid_stack)
        out_w = mb("out_w", [P, 2, KI, D], F16)
        w2 = mb("w2", [P, 2, KD, D], F16)
        fc_g_row = mb("fc_g_row", [P, MID])
        fc_b_row = mb("fc_b_row", [P, MID])
        out_b_row = mb("out_b_row", [P, D])
        conv_bs = mb("conv_bs", [P, GROUPS])
        ones1 = mb("ones1", [P, 1])
        zero = mb("zero", [P, TILE])

        x_landed = [sem(f"x_landed{h}") for h in range(HALVES)]
        bn_done, mv_done, va_done, rs_done = sem("bn_done"), sem("mv_done"), sem("va_done"), sem("rs_done")
        nm_done, nb_done = sem("nm_done"), sem("nb_done")
        xn_done = sem("xn_done")
        resid_done = sem("resid_done")
        xt_tr, xt_hi, xt_lo = sem("xt_tr"), sem("xt_hi"), sem("xt_lo")
        iph, ipg = sem("iph"), sem("ipg")
        p_hi_done, p_lo_done, p_halo, p_ready = sem("p_hi_done"), sem("p_lo_done"), sem("p_halo"), sem("p_ready")
        gate_done = sem("gate_done")
        conv_done = sem("conv_done")
        h_done = sem("h_done")
        h_hi, h_lo, h_sq, h_sum, q_sum = sem("h_hi"), sem("h_lo"), sem("h_sq"), sem("h_sum"), sem("q_sum")
        stats_done = sem("stats_done")
        ln2_mneg, ln2_e2, ln2_msq, ln2_v, ln2_r = (sem("ln2_mneg"), sem("ln2_e2"), sem("ln2_msq"),
                                                   sem("ln2_v"), sem("ln2_r"))
        fc_done, t_done, u_done, silu_done = sem("fc_done"), sem("t_done"), sem("u_done"), sem("silu_done")
        mt_tr, mt_hi, mt_lo = sem("mt_tr"), sem("mt_hi"), sem("mt_lo")
        h_used = sem("h_used")
        out_done, x1_done, x1_stored = sem("out_done"), sem("x1_done"), sem("x1_stored")

        m_landed, vw_landed = [sem(f"m_landed{n}") for n in range(B)], [sem(f"vw_landed{n}") for n in range(B)]

        OUT_BANK = [6, 7, 2, 3]
        FC_SQ = (H_SCALE * W_SCALE) ** 2
        XT_B, MT_B, ST_B = bank[4], bank[5], bank[7]

        def transpose_x(pe, t, s):
            pe.wait_ge(xn_done, SUBS * t + s + 1)
            at_least(pe, xt_lo, SUBS * t + s)
            for k in range(KD):
                tr = pe.transpose(XT_B[:, k * P:(k + 1) * P], xn[:, s, k * P:(k + 1) * P], ident[:, :])
            tr.then_inc(xt_tr, 1)

        def xt_hi_part(act, t, s):
            act.wait_ge(xt_tr, SUBS * t + s + 1)
            at_least(act, ipg, GROUPS * t)
            act.activation(xT[:, 0, :, s * P:(s + 1) * P],
                           XT_B[:, :].rearrange("p (k n) -> p k n", k=KD), ACT.Copy)\
               .then_inc(xt_hi, 1)

        def normalise_x(act, t, half, s):
            if s == 0:
                act.wait_ge(nb_done, t + 1)
                at_least(act, xt_tr, SUBS * t)
            act.activation(xn[:, s, :], xs[:, half, s, :], ACT.Identity, bias=nb[:, s:s + 1],
                           scale=rs[:, s:s + 1]).then_inc(xn_done, 1)

        def ln_stats(dve, t, half, s, b_use):
            if s == 0:
                dve.wait_ge(x_landed[half], 16 * (b_use + 1))
            dve.bn_stats(bn[:, s, :], xs[:, half, s, :]).then_inc(bn_done, 1)

        def ln_var(dve, t):
            carry(dve, pad_dve[:, :], (bn_done, SUBS * t + SUBS), (xn_done, SUBS * t))
            for s in range(SUBS):
                ins = dve.bn_aggr(mv[:, s, :], bn[:, s, :])
            ins.then_inc(mv_done, 1)
            dve.wait_ge(mv_done, t + 1)
            dve.tensor_scalar(nm[:, :], mv[:, :, 0], -1.0, None, ALU.mult).then_inc(nm_done, 1)
            dve.tensor_scalar(va[:, :], mv[:, :, 1], EPS, LN_SCALE ** -2, ALU.add, ALU.mult)\
               .then_inc(va_done, 1)

        def xt_lo_part(dve, t, s):
            dve.wait_ge(xt_hi, SUBS * t + s + 1)
            r = slice(s * P, (s + 1) * P)
            dve.tensor_tensor(xT[:, 1, :, r], XT_B[:, :].rearrange("p (k n) -> p k n", k=KD),
                              xT[:, 0, :, r], ALU.subtract).then_inc(xt_lo, 1)

        def ln_factors(pool, t):
            pool.wait_ge(va_done, t + 1)
            pool.wait_ge(nm_done, t + 1)
            pool.tensor_tensor(rs[:, :], va[:, :], mhalf[:, :], ALU.pow).then_inc(rs_done, 1)
            at_least(pool, rs_done, t + 1)
            pool.tensor_tensor(nb[:, :], nm[:, :], rs[:, :], ALU.mult).then_inc(nb_done, 1)

        def residual(pool, t, half):
            for s in range(SUBS):
                pool.wait_ge(xn_done, SUBS * t + s + 1)
                pool.tensor_tensor(xs[:, half, s, :], xs[:, half, s, :], out_b_row[:, :], ALU.add)\
                    .then_inc(resid_done, 1)

        prep = ExitStack()
        pb = sb_in(prep)
        raw0 = pb("raw0", [P, KD * 2 * I])
        raw1 = pb("raw1", [P, 4 * KD * D])
        kbd, vbd = [xs[:, h, :, :].rearrange("p c (b n) -> p c b n", b=B) for h in range(2)]
        ctx = xn[:, 0:2, :].rearrange("p s d -> p (s d)").rearrange("p (k n) -> p k n", k=KD)
        vw_stage = pb("vw_stage", [P, 2, 2, D], F16)
        vec_col = pb("vec_col", [P, 3 * KD])
        vec = pb("vec", [P, 4 * KI + 3 * KD])
        g256 = pb("g256", [P, KI])
        tri_f = xn[:, 2, 0:P]

        conv_bv, ln_gv, ln_bv, cproj_bv = [vec[:, n * KI:(n + 1) * KI] for n in range(4)]
        bqv, bkv, bvv = [vec[:, 4 * KI + n * KD:4 * KI + (n + 1) * KD] for n in range(3)]
        raw_in = raw0[:, :].rearrange("p (k n) -> p k n", k=KD)
        raw_conv = raw0[:, 0:GROUPS * TAPS * P]
        raw_fc = raw0[:, KD * I:2 * KD * I].rearrange("p (k n) -> p k n", k=KI)
        wk_r, wv_r, wq_r, wo_r = [raw1[:, n * KD * D:(n + 1) * KD * D].rearrange("p (k n) -> p k n", k=KD)
                                  for n in range(4)]
        m_stage = [raw1[:, n * KD * D:(n + 1) * KD * D].bitcast(F16).rearrange(
            "p (b t n) -> p b t n", b=B, t=2) for n in range(2)]
        raw_out = raw1[:, 0:KI * D].rearrange("p (k n) -> p k n", k=KI)
        raw_cproj = raw1[:, KI * D:2 * KI * D].rearrange("p (k n) -> p k n", k=KI)

        names = ["small", "ctx", "wk", "wv", "wq", "wo", "in0", "in1", "conv", "fc", "outw", "cproj"]
        landed = {n: sem(f"landed_{n}") for n in names}
        SMALL = 12
        p_const = sem("p_const")
        p_job = sem("p_job")
        p_hi = sem("p_hi")
        p_evac = sem("p_evac")
        p_whi = sem("p_whi")
        p_wlo = sem("p_wlo")
        p_vec = sem("p_vec")
        m_stored = [sem(f"m_stored{n}") for n in range(2)]
        vw_stored = [sem(f"vw_stored{n}") for n in range(2)]

        K_JOB, V_JOB, HB_JOB, M_JOB = 0, KD, 2 * KD, 2 * KD + PAIRS
        FC_COL_JOB = M_JOB + KD * PAIRS
        VW_JOB = FC_COL_JOB + 1
        FC_ROW_JOB = VW_JOB + B * PAIRS
        OUT_COL_JOB = FC_ROW_JOB + 2
        OUT_ROW_JOB = OUT_COL_JOB + 2
        W2_JOBS = [OUT_COL_JOB + 1] + [OUT_ROW_JOB + m for m in range(1, KD)]
        JOBS = W2_JOBS[-1] + 1

        def job_bank(n):
            return bank[(n - JOBS) % 8]

        IN_N, CONV_N, FC_N, OUT_N = KD, 2, KI, 2
        FC_PIECE, CONV_PIECE = 0, FC_N
        OUT_PIECE, IN_PIECE = FC_N + CONV_N, FC_N + CONV_N + OUT_N
        PIECES = IN_PIECE + IN_N

        def piece(n):
            if n < CONV_PIECE:
                k = n
                return fc_w[:, 0, k, :], fc_w[:, 1, k, :], raw_fc[:, k, :], g256[:, k:k + 1]
            if n < OUT_PIECE:
                q = n - CONV_PIECE
                hi, lo = [conv_w[:, t, 4 * q:4 * q + 4, :, :].rearrange("p g k o -> p (g k o)") for t in range(2)]
                return hi, lo, raw_conv[:, q * 2048:(q + 1) * 2048], W_SCALE
            if n < IN_PIECE:
                q = n - OUT_PIECE
                hi, lo = [out_w[:, t, 4 * q:4 * q + 4, :].rearrange("p k n -> p (k n)") for t in range(2)]
                return hi, lo, raw_out[:, 4 * q:4 * q + 4, :].rearrange("p k n -> p (k n)"), W_SCALE
            k = n - IN_PIECE
            return in_w[:, 0, k, :], in_w[:, 1, k, :], raw_in[:, k, :], W_SCALE

        def m_out(n):
            m, c = n // PAIRS, n % PAIRS
            return m_stage[m % 2][:, :, :, c * P:(c + 1) * P]

        def vw_out(n):
            return vw_stage[:, n % 2, :, :]

        def prep_over(eng):
            eng.wait_ge(p_evac, JOBS)
            eng.wait_ge(p_wlo, PIECES)
            for n in range(2):
                eng.wait_ge(vw_stored[n], 16 * B * PAIRS // 2)

        def prep_sp(sp):
            kn = "(k p) n -> p k n"
            sp.dma_start(ctx, ctxT.rearrange(kn, p=P)).then_inc(landed["ctx"], 16)
            sp.dma_start(wk_r, Wk.rearrange(kn, p=P)).then_inc(landed["wk"], 16)
            for n, v in enumerate([conv_b, ln_g, ln_b, cproj_b]):
                sp.dma_start(vec[:, n * KI:(n + 1) * KI], v).then_inc(landed["small"], 16)
            for n, v in enumerate([bq, bk, bv]):
                sp.dma_start(vec[:, 4 * KI + n * KD:4 * KI + (n + 1) * KD], v).then_inc(landed["small"], 16)
            sp.dma_start(ident[:, :], ident_in).then_inc(landed["small"], 16)
            sp.dma_start(tri_f, tri_in).then_inc(landed["small"], 16)
            sp.dma_start(prio[:, :], prio_in).then_inc(landed["small"], 16)
            sp.dma_start(masku[:, :, :], mask).then_inc(landed["small"], 16)
            sp.dma_start(fc_b_row[:, :], fc_b.partition_broadcast(P)).then_inc(landed["small"], 16)
            sp.dma_start(wv_r, Wv.rearrange(kn, p=P)).then_inc(landed["wv"], 16)
            sp.dma_start(wq_r, WqT.rearrange(kn, p=P)).then_inc(landed["wq"], 16)
            sp.dma_start(raw_fc, fc_wT.rearrange(kn, p=P)).then_inc(landed["fc"], 16)
            sp.dma_start(wo_r, Wo.rearrange(kn, p=P)).then_inc(landed["wo"], 16)
            sp.dma_start(raw_conv, conv_wT).then_inc(landed["conv"], 16)
            for m in range(KD):
                sp.wait_ge(p_evac, M_JOB + PAIRS * (m + 1))
                for b in range(B):
                    sp.dma_start(m_dram[b, :, :, m, :], m_stage[m % 2][:, b, :, :]).then_inc(m_stored[m % 2], 16)
            sp.dma_start(xs[:, 0, :, :], x_v[0, 0]).then_inc(x_landed[0], 16)
            sp.wait_ge(m_stored[0], 16 * B * KD // 2)
            sp.wait_ge(m_stored[1], 16 * B * KD // 2)
            sp.dma_start(raw_out, out_wT.rearrange(kn, p=P)).then_inc(landed["outw"], 16)
            for n in range(B * PAIRS):
                sp.wait_ge(p_evac, VW_JOB + n + 1)
                sp.dma_start(vw_dram[n // PAIRS, :, :, n % PAIRS, :], vw_out(n)).then_inc(vw_stored[n % 2], 16)
            sp.dma_start(raw_cproj, cproj_w.rearrange(kn, p=P)).then_inc(landed["cproj"], 16)
            sp.wait_ge(p_whi, OUT_PIECE)
            sp.wait_ge(p_wlo, OUT_PIECE)
            in_v = in_wT.rearrange(kn, p=P)
            for n in range(2):
                sp.dma_start(raw_in[:, 2 * n:2 * n + 2, :], in_v[:, 2 * n:2 * n + 2, :]).then_inc(landed[f"in{n}"], 16)
            sp.dma_start(xs[:, 1, :, :], x_v[0, 1]).then_inc(x_landed[1], 16)

        def prep_pool(pool):
            pool.memset(kbd, 0.0).then_inc(p_const, 1)
            pool.memset(vbd, 0.0).then_inc(p_const, 1)
            pool.memset(ones_b[:, :], 1.0).then_inc(p_const, 1)
            pool.memset(mhalf[:, :], -0.5).then_inc(p_const, 1)
            pool.memset(zero[:, :], 0.0).then_inc(p_const, 1)
            pool.wait_ge(p_const, 5)
            ln_factors(pool, 0)

        def prep_pe(pe):
            def slot(n):
                at_least(pe, p_evac, n - 7)
                return job_bank(n)

            def column_to_row(o, c0):
                for c in range(KD):
                    mm = pe.matmul(o[:, c * P:(c + 1) * P], vec_col[:, c0 + c:c0 + c + 1].to_broadcast([P, P]),
                                   ident[:, :], start=True, stop=True)
                return mm

            pe.wait_ge(landed["ctx"], 16)
            for job, name, w in ((K_JOB, "wk", wk_r), (V_JOB, "wv", wv_r)):
                pe.wait_ge(landed[name], 16)
                for m in range(KD):
                    o = slot(job + m)[:, 0:B * KEYS]
                    for k in range(KD):
                        mm = pe.matmul(o, w[:, k, m * P:(m + 1) * P], ctx[:, k, :],
                                       start=(k == 0), stop=(k == KD - 1))
                    mm.then_inc(p_job, 1)
            pe.wait_ge(p_evac, K_JOB + KD)
            for c in range(PAIRS):
                o = slot(HB_JOB + c)
                pe.matmul(o[:, :], bqv[:, c:c + 1].to_broadcast([P, P]), kbd[:, c, :, :].rearrange("p b n -> p (b n)"),
                          start=True, stop=True).then_inc(p_job, 1)
            pe.wait_ge(landed["wq"], 16)
            for m in range(KD):
                for c in range(PAIRS):
                    o = slot(M_JOB + PAIRS * m + c)
                    pe.matmul(o[:, :], wq_r[:, c, m * P:(m + 1) * P], kbd[:, c, :, :].rearrange("p b n -> p (b n)"),
                              start=True, stop=True).then_inc(p_job, 1)
            pe.wait_ge(landed["fc"], 16)
            gb = vec[:, KI:3 * KI].rearrange("p (v k) -> p k v", v=2)
            o = slot(FC_COL_JOB)
            for m in range(KD):
                for k in range(KI):
                    mm = pe.matmul(o[:, 2 * m:2 * m + 2], raw_fc[:, k, m * P:(m + 1) * P], gb[:, k, :],
                                   start=(k == 0), stop=(k == KI - 1))
            mm.then_inc(p_job, 1)
            pe.wait_ge(landed["wo"], 16)
            pe.wait_ge(p_evac, V_JOB + KD)
            for b in range(B):
                for c in range(PAIRS):
                    o = slot(VW_JOB + PAIRS * b + c)
                    pe.matmul(o[:, :], vbd[:, c, b, :], wo_r[:, c, :], start=True, stop=True).then_inc(p_job, 1)
            pe.wait_ge(p_evac, FC_COL_JOB + 1)
            for v in range(2):
                column_to_row(slot(FC_ROW_JOB + v), KD * v).then_inc(p_job, 1)
            pe.wait_ge(landed["outw"], 16)
            o = slot(OUT_COL_JOB)
            for m in range(KD):
                for k in range(KI):
                    mm = pe.matmul(o[:, m:m + 1], raw_out[:, k, m * P:(m + 1) * P], cproj_bv[:, k:k + 1],
                                   start=(k == 0), stop=(k == KI - 1))
            mm.then_inc(p_job, 1)
            pe.wait_ge(landed["cproj"], 16)
            for m in range(KD):
                o = slot(W2_JOBS[m])
                for k in range(KI):
                    if m == KD - 1 and k == KI // 2:
                        transpose_x(pe, 0, 2)
                    mm = pe.matmul(o[:, :], raw_cproj[:, k, m * P:(m + 1) * P], raw_out[:, k, :],
                                   start=(k == 0), stop=(k == KI - 1))
                mm.then_inc(p_job, 1)
                if m == 0:
                    pe.wait_ge(p_evac, OUT_COL_JOB + 1)
                    column_to_row(slot(OUT_ROW_JOB), 2 * KD).then_inc(p_job, 1)
                if m == 1:
                    pe.wait_ge(p_evac, OUT_ROW_JOB + 1)
                    transpose_x(pe, 0, 0)
                if m == 2:
                    transpose_x(pe, 0, 1)
            transpose_x(pe, 0, 3)
            pe.wait_ge(p_whi, PIECES)
            pe.wait_ge(p_wlo, PIECES)

        def prep_act(act):
            def split(n):
                hi, lo, raw, scale = piece(n)
                act.activation(hi, raw, ACT.Copy, scale=scale).then_inc(p_whi, 1)

            for m in range(KD):
                for c in range(PAIRS):
                    n = PAIRS * m + c
                    act.wait_ge(p_job, M_JOB + n + 1)
                    if m < 2:
                        act.wait_ge(p_evac, V_JOB + KD)
                    else:
                        act.wait_ge(m_stored[m % 2], 16 * B)
                    act.activation(m_out(n)[:, :, 0, :], job_bank(M_JOB + n)[:, :].rearrange("p (b n) -> p b n", b=B),
                                   ACT.Copy).then_inc(p_hi, 1)
                if m == 0:
                    act.wait_ge(landed["fc"], 16)
                    act.wait_ge(p_vec, 2)
                for k in (2 * m, 2 * m + 1):
                    split(FC_PIECE + k)
            for n in range(B * PAIRS):
                act.wait_ge(p_job, VW_JOB + n + 1)
                if n >= 2:
                    act.wait_ge(vw_stored[n % 2], 16 * (n // 2))
                act.activation(vw_out(n)[:, 0, :], job_bank(VW_JOB + n)[:, :],
                               ACT.Copy, scale=W_SCALE).then_inc(p_hi, 1)
                if n == 0:
                    act.wait_ge(landed["conv"], 16)
                if n in (0, 4):
                    split(CONV_PIECE + n // 4)
            act.wait_ge(landed["outw"], 16)
            for n in range(OUT_N):
                split(OUT_PIECE + n)
            for s in range(SUBS):
                normalise_x(act, 0, 0, s)
            for m in range(KD):
                if m >= 2:
                    xt_hi_part(act, 0, m - 2)
                if m == KD - 1:
                    act.wait_ge(landed["in1"], 16)
                    split(IN_PIECE + 2)
                    split(IN_PIECE + 3)
                    xt_hi_part(act, 0, 2)
                act.wait_ge(p_job, W2_JOBS[m] + 1)
                act.activation(w2[:, 0, m, :], job_bank(W2_JOBS[m])[:, :], ACT.Copy, scale=W2_SCALE).then_inc(p_hi, 1)
                if m == 1:
                    act.wait_ge(landed["in0"], 16)
                    split(IN_PIECE)
                    split(IN_PIECE + 1)
            xt_hi_part(act, 0, 3)

        def prep_dve(dve):
            def split(n):
                hi, lo, raw, scale = piece(n)
                dve.wait_ge(p_whi, n + 1)
                dve.scalar_tensor_tensor(lo, raw, scale, hi, ALU.mult, ALU.subtract).then_inc(p_wlo, 1)

            dve.memset(ones1[:, :], 1.0).then_inc(p_vec, 1)
            dve.wait_ge(landed["small"], 16 * SMALL)
            dve.tensor_scalar(g256[:, :], ln_gv, W_SCALE, None, ALU.mult).then_inc(p_vec, 1)
            dve.tensor_scalar(conv_bs[:, :], conv_bv, P_SCALE * W_SCALE, None, ALU.mult).then_inc(p_vec, 1)
            dve.tensor_copy(tri[:, :], tri_f).then_inc(p_vec, 1)
            for job, bd, bias, scale, const in ((K_JOB, kbd, bkv, 0.125 * W_SCALE, 1), (V_JOB, vbd, bvv, 1.0, 2)):
                dve.wait_ge(p_const, const)
                for m in range(KD):
                    dve.wait_ge(p_job, job + m + 1)
                    for q in range(2):
                        r = slice(64 * q, 64 * q + 64)
                        ins = dve.tensor_scalar(
                            bd[r, m, :, r], job_bank(job + m)[r, 0:B * KEYS].rearrange("p (b n) -> p b n", b=B),
                            bias[r, m:m + 1], scale, ALU.add, ALU.mult)
                    ins.then_inc(p_evac, 1)
            for c in range(PAIRS):
                dve.wait_ge(p_job, HB_JOB + c + 1)
                dve.tensor_scalar(hbias[:, :, c * P:(c + 1) * P],
                                  job_bank(HB_JOB + c)[:, :].rearrange("p (b n) -> p b n", b=B),
                                  1.0 / W_SCALE, None, ALU.mult).then_inc(p_evac, 1)
            for m in range(KD):
                for c in range(PAIRS):
                    n = PAIRS * m + c
                    dve.wait_ge(p_hi, n + 1)
                    dve.tensor_tensor(m_out(n)[:, :, 1, :], job_bank(M_JOB + n)[:, :].rearrange("p (b n) -> p b n", b=B),
                                      m_out(n)[:, :, 0, :], ALU.subtract).then_inc(p_evac, 1)
                for k in (2 * m, 2 * m + 1):
                    split(FC_PIECE + k)
            dve.wait_ge(p_job, FC_COL_JOB + 1)
            dve.tensor_copy(vec_col[:, 0:2 * KD].rearrange("p (v m) -> p m v", v=2),
                            job_bank(FC_COL_JOB)[:, 0:2 * KD].rearrange("p (m v) -> p m v", v=2)).then_inc(p_evac, 1)
            for n in range(B * PAIRS):
                dve.wait_ge(p_hi, KD * PAIRS + n + 1)
                dve.scalar_tensor_tensor(vw_out(n)[:, 1, :], job_bank(VW_JOB + n)[:, :], W_SCALE,
                                         vw_out(n)[:, 0, :], ALU.mult, ALU.subtract).then_inc(p_evac, 1)
                if n in (0, 4):
                    split(CONV_PIECE + n // 4)
            dve.wait_ge(p_job, FC_ROW_JOB + 1)
            dve.tensor_scalar(fc_g_row[:, :], job_bank(FC_ROW_JOB)[:, :], H_SCALE * W_SCALE, None, ALU.mult)\
               .then_inc(p_evac, 1)
            dve.wait_ge(p_job, FC_ROW_JOB + 2)
            dve.tensor_tensor(fc_b_row[:, :], job_bank(FC_ROW_JOB + 1)[:, :], fc_b_row[:, :], ALU.add)\
               .then_inc(p_evac, 1)
            for s in range(SUBS):
                ln_stats(dve, 0, 0, s, 0)
            ln_var(dve, 0)
            dve.wait_ge(p_job, OUT_COL_JOB + 1)
            dve.tensor_copy(vec_col[:, 2 * KD:3 * KD], job_bank(OUT_COL_JOB)[:, 0:KD]).then_inc(p_evac, 1)
            for n in range(OUT_N):
                split(OUT_PIECE + n)
            for m in range(KD):
                if m >= 2:
                    xt_lo_part(dve, 0, m - 2)
                if m == KD - 1:
                    split(IN_PIECE + 2)
                    split(IN_PIECE + 3)
                    xt_lo_part(dve, 0, 2)
                dve.wait_ge(p_hi, (KD + B) * PAIRS + m + 1)
                dve.scalar_tensor_tensor(w2[:, 1, m, :], job_bank(W2_JOBS[m])[:, :], W2_SCALE,
                                         w2[:, 0, m, :], ALU.mult, ALU.subtract).then_inc(p_evac, 1)
                if m == 0:
                    dve.wait_ge(p_job, OUT_ROW_JOB + 1)
                    dve.tensor_copy(out_b_row[:, :], job_bank(OUT_ROW_JOB)[:, :]).then_inc(p_evac, 1)
                if m == 1:
                    split(IN_PIECE)
                    split(IN_PIECE + 1)
            xt_lo_part(dve, 0, 3)

        prep.close()
        pha = ExitStack()
        ab = sb_in(pha)
        pp = ab("pp", [P, 2, 2, HALO + TILE + 1], F16)
        tails = ab("tails", [P, GROUPS, 2, HALO], F16)
        gate = ab("gate", [P, 2, TILE])
        hh = ab("hh", [P, 2, TILE])
        sq = ab("sq", [P, 2, TILE])
        hsum = ab("hsum", [P, TILE])
        qsum = ab("qsum", [P, TILE])
        hT = ab("hT", [P, 2, KI, TILE], F16)
        mneg = ab("mneg", [P, SUBS])
        msq = ab("msq", [P, SUBS])
        e2 = ab("e2", [P, SUBS])
        v2 = ab("v2", [P, SUBS])
        r2 = ab("r2", [P, SUBS])
        tb = ab("tb", [P, 2, MID])
        ub = ab("ub", [P, 2, MID])
        mm_s = ab("mm_s", [P, SUBS, MID])
        mT = ab("mT", [P, 2, 2, KD, P], F16)
        x1o = ab("x1o", [P, SUBS, D])




        def a_sp(sp):
            def tile(b, half, rows):
                t = HALVES * b + half
                sp.wait_ge(x1_done, SUBS * t + SUBS)
                sp.dma_start(x1_dram[t], x1o[:, :, :]).then_inc(x1_stored, 16)
                sp.dma_start(xs[:, half, :, :], rows).then_inc(x_landed[half], 16)

            for half in range(HALVES):
                tile(0, half, x_v[1, half])
            with sp.Fori(1, B - 1) as b:
                for half in range(HALVES):
                    tile(b, half, x_v[b + 1, half])
            tile(B - 1, 0, x1_dram[0])
            sp.wait_ge(ipg, TILES * GROUPS)
            sp.dma_start(m_w[:, 0], m_dram[0]).then_inc(m_landed[0], 16)
            sp.wait_ge(conv_done, TILES * GROUPS)
            for n in range(B):
                if n == B // 2:
                    sp.wait_ge(fc_done, TILES * SUBS)
                sp.dma_start(vw_w[:, n], vw_dram[n]).then_inc(vw_landed[n], 16)
                if n + 1 < B:
                    sp.dma_start(m_w[:, n + 1], m_dram[n + 1]).then_inc(m_landed[n + 1], 16)
            tile(B - 1, 1, x1_dram[1])

        def a_pe(pe):

            def in_proj(t, g, gate_half):
                o = bank[1 if gate_half else 0]
                if g == 0:
                    at_least(pe, t_done, SUBS * t)
                    if not gate_half:
                        pe.wait_ge(xt_lo, SUBS * t + SUBS)
                elif gate_half:
                    pe.wait_ge(gate_done, GROUPS * t + g)
                else:
                    pe.wait_ge(p_lo_done, GROUPS * t + g)
                c = (I if gate_half else 0) + g * P
                product3(pe, o[:, :], [(in_w[:, 0, k, c:c + P], in_w[:, 1, k, c:c + P],
                                        xT[:, 0, k, :], xT[:, 1, k, :]) for k in range(KD)])\
                    .then_inc(ipg if gate_half else iph, 1)

            def conv(t, g):
                o = bank[2 + g % 2]
                if g < 2:
                    at_least(pe, x1_done, SUBS * t)
                else:
                    pe.wait_ge(h_done, GROUPS * t + g - 1)
                pe.wait_ge(p_halo, GROUPS * t + g + 1)
                pe.wait_ge(p_ready, GROUPS * t + g + 1)
                product3(pe, o[:, :], [(conv_w[:, 0, g, k, :], conv_w[:, 1, g, k, :],
                                        pp[:, g % 2, 0, k:k + TILE], pp[:, g % 2, 1, k:k + TILE])
                                       for k in range(TAPS)]).then_inc(conv_done, 1)

            def fc(t, s):
                if s == 0:
                    pe.wait_ge(p_lo_done, GROUPS * t + GROUPS)
                elif s == 1:
                    pe.wait_ge(gate_done, GROUPS * t + GROUPS)
                else:
                    pe.wait_ge(h_done, GROUPS * t + GROUPS - 3 + s)
                r = slice(s * P, (s + 1) * P)
                for g in range(KI):
                    if s == 0:
                        pe.wait_ge(h_lo, GROUPS * t + g + 1)
                    mm = product3(pe, bank[s][:, :], [(hT[:, 0, g, r], hT[:, 1, g, r],
                                                       fc_w[:, 0, g, :], fc_w[:, 1, g, :])],
                                  start=(g == 0), stop=(g == KI - 1))
                mm.then_inc(fc_done, 1)

            def stats(t):
                pe.wait_ge(h_sum, GROUPS * t + GROUPS)
                pe.wait_ge(q_sum, GROUPS * t + GROUPS)
                for n, v in enumerate((hsum, qsum)):
                    for s in range(SUBS):
                        c = n * SUBS + s
                        mm = pe.matmul(ST_B[:, c:c + 1], v[:, s * P:(s + 1) * P], ones1[:, :],
                                       start=True, stop=True)
                mm.then_inc(stats_done, 1)

            def out_h(t, s):
                if s == 1:
                    pe.wait_ge(ln2_e2, t + 1)
                elif s >= 2:
                    pe.wait_ge(t_done, SUBS * t + s + 1)
                r = slice(s * P, (s + 1) * P)
                mm = product3(pe, bank[OUT_BANK[s]][:, :],
                              [(hT[:, 0, g, r], hT[:, 1, g, r], out_w[:, 0, g, :], out_w[:, 1, g, :])
                               for g in range(KI)], stop=False)
                if s == SUBS - 1:
                    mm.then_inc(h_used, 1)

            def transpose_m(t, s):
                pe.wait_ge(silu_done, SUBS * t + s + 1)
                pe.wait_ge(mt_lo, SUBS * t + s)
                for k in range(KD):
                    tr = pe.transpose(MT_B[:, k * P:(k + 1) * P], mm_s[:, s, k * P:(k + 1) * P], ident[:, :])
                tr.then_inc(mt_tr, 1)

            def out_m(t, s):
                pe.wait_ge(mt_lo, SUBS * t + s + 1)
                product3(pe, bank[OUT_BANK[s]][:, :],
                         [(mT[:, s % 2, 0, k, :], mT[:, s % 2, 1, k, :], w2[:, 0, k, :], w2[:, 1, k, :])
                          for k in range(KD)], start=False).then_inc(out_done, 1)

            def tile(b, half):
                t = HALVES * b + half
                for g in range(GROUPS + 1):
                    if g < GROUPS:
                        in_proj(t, g, False)
                        in_proj(t, g, True)
                    if g >= 1:
                        conv(t, g - 1)
                fc(t, 0)
                fc(t, 1)
                stats(t)
                fc(t, 2)
                fc(t, 3)
                transpose_x(pe, t + 1, 0)
                out_h(t, 0)
                transpose_m(t, 0)
                out_h(t, 1)
                transpose_x(pe, t + 1, 1)
                out_m(t, 0)
                transpose_m(t, 1)
                out_h(t, 2)
                transpose_x(pe, t + 1, 2)
                out_m(t, 1)
                transpose_m(t, 2)
                out_h(t, 3)
                out_m(t, 2)
                transpose_m(t, 3)
                transpose_x(pe, t + 1, 3)
                out_m(t, 3)

            pe.wait_ge(p_vec, 1)
            for half in range(HALVES):
                tile(0, half)
            with pe.Fori(1, B - 1) as b:
                for half in range(HALVES):
                    tile(b, half)
            for half in range(HALVES):
                tile(B - 1, half)

        def a_act(act):

            def mt_hi_part(t, s):
                act.wait_ge(mt_tr, SUBS * t + s + 1)
                at_least(act, out_done, SUBS * t + max(s - 1, 0))
                act.activation(mT[:, s % 2, 0, :, :], MT_B[:, :].rearrange("p (k n) -> p k n", k=KD),
                               ACT.Copy, scale=MID_SCALE).then_inc(mt_hi, 1)


            def silu_m(t, s):
                act.wait_ge(u_done, SUBS * t + s + 1)
                at_least(act, mt_tr, SUBS * t)
                act.activation(mm_s[:, s, :], ub[:, s % 2, :], ACT.Silu).then_inc(silu_done, 1)

            def tile(b, half):
                t = HALVES * b + half
                for g in range(GROUPS + 1):
                    if g < GROUPS:
                        before = GROUPS * t + max(g - 1, 0)
                        act.wait_ge(iph, GROUPS * t + g + 1)
                        at_least(act, conv_done, before)
                        act.activation(pp[:, g % 2, 0, HALO:HALO + TILE], bank[0][:, :], ACT.Copy,
                                       scale=P_SCALE / (W_SCALE * LN_SCALE)).then_inc(p_hi_done, 1)
                        act.wait_ge(ipg, GROUPS * t + g + 1)
                        at_least(act, h_done, before)
                        act.activation(gate[:, g % 2, :], bank[1][:, :], ACT.Silu,
                                       scale=1.0 / (W_SCALE * LN_SCALE)).then_inc(gate_done, 1)
                    if g >= 1:
                        q = g - 1
                        act.wait_ge(h_done, GROUPS * t + q + 1)
                        if q == 0:
                            at_least(act, h_used, t)
                        act.activation(hT[:, 0, q, :], hh[:, q % 2, :], ACT.Copy,
                                       scale=H_SCALE / (P_SCALE * W_SCALE)).then_inc(h_hi, 1)
                        at_least(act, q_sum, GROUPS * t + max(q - 1, 0))
                        act.activation(sq[:, q % 2, :], hh[:, q % 2, :], ACT.Square,
                                       scale=1.0 / (P_SCALE * W_SCALE)).then_inc(h_sq, 1)
                for s in range(SUBS):
                    normalise_x(act, t + 1, 1 - half, s)
                silu_m(t, 0)
                silu_m(t, 1)
                silu_m(t, 2)
                xt_hi_part(act, t + 1, 0)
                silu_m(t, 3)
                mt_hi_part(t, 0)
                xt_hi_part(act, t + 1, 1)
                mt_hi_part(t, 1)
                xt_hi_part(act, t + 1, 2)
                mt_hi_part(t, 2)
                mt_hi_part(t, 3)
                xt_hi_part(act, t + 1, 3)

            prep_over(act)
            for half in range(HALVES):
                tile(0, half)
            with act.Fori(1, B - 1) as b:
                for half in range(HALVES):
                    tile(b, half)
            for half in range(HALVES):
                tile(B - 1, half)

        def a_dve(dve):



            def p_part(t, half, g):
                n = GROUPS * t + g + 1
                sl = g % 2
                at_least(dve, conv_done, GROUPS * t + max(g - 1, 0))
                if half == 0:
                    dve.memset(pp[:, sl, :, 0:HALO], 0.0).then_inc(p_halo, 1)
                else:
                    dve.tensor_copy(pp[:, sl, :, 0:HALO], tails[:, g, :, :]).then_inc(p_halo, 1)
                dve.wait_ge(p_hi_done, n)
                dve.scalar_tensor_tensor(pp[:, sl, 1, HALO:HALO + TILE], bank[0][:, :],
                                         P_SCALE / (W_SCALE * LN_SCALE), pp[:, sl, 0, HALO:HALO + TILE],
                                         ALU.mult, ALU.subtract).then_inc(p_lo_done, 1)
                dve.wait_ge(p_lo_done, n)
                dve.wait_ge(p_halo, n)
                dve.tensor_copy(tails[:, g, :, :], pp[:, sl, :, TILE:TILE + HALO]).then_inc(p_ready, 1)

            def h_part(t, g):
                n = GROUPS * t + g + 1
                before = GROUPS * t + max(g - 1, 0)
                dve.wait_ge(conv_done, n)
                dve.wait_ge(gate_done, n)
                at_least(dve, h_hi, before)
                at_least(dve, h_sq, before)
                at_least(dve, h_sum, before)
                dve.scalar_tensor_tensor(hh[:, g % 2, :], bank[2 + g % 2][:, :], conv_bs[:, g:g + 1],
                                         gate[:, g % 2, :], ALU.add, ALU.mult).then_inc(h_done, 1)

            def h_lo_part(t, g):
                dve.wait_ge(h_hi, GROUPS * t + g + 1)
                dve.scalar_tensor_tensor(hT[:, 1, g, :], hh[:, g % 2, :], H_SCALE / (P_SCALE * W_SCALE),
                                         hT[:, 0, g, :], ALU.mult, ALU.subtract).then_inc(h_lo, 1)

            def ln2_stats(t):
                dve.wait_ge(stats_done, t + 1)
                dve.tensor_scalar(mneg[:, :], ST_B[:, 0:SUBS], -1.0 / (P_SCALE * W_SCALE * I), None, ALU.mult)\
                   .then_inc(ln2_mneg, 1)
                dve.tensor_scalar(e2[:, :], ST_B[:, SUBS:2 * SUBS], FC_SQ / I, EPS * FC_SQ, ALU.mult, ALU.add)\
                   .then_inc(ln2_e2, 1)
                dve.wait_ge(ln2_mneg, t + 1)
                dve.scalar_tensor_tensor(msq[:, :], mneg[:, :], FC_SQ, mneg[:, :], ALU.mult, ALU.mult)\
                   .then_inc(ln2_msq, 1)
                dve.wait_ge(ln2_msq, t + 1)
                dve.wait_ge(ln2_e2, t + 1)
                dve.tensor_tensor(v2[:, :], e2[:, :], msq[:, :], ALU.subtract).then_inc(ln2_v, 1)

            def tu(t, s):
                n = SUBS * t + s + 1
                dve.wait_ge(fc_done, n)
                dve.scalar_tensor_tensor(tb[:, s % 2, :], fc_g_row[:, :], mneg[:, s:s + 1], bank[s][:, :],
                                         ALU.mult, ALU.add).then_inc(t_done, 1)
                if s == 0:
                    dve.wait_ge(ln2_r, t + 1)
                dve.wait_ge(t_done, n)
                at_least(dve, silu_done, SUBS * t + max(s - 1, 0))
                dve.scalar_tensor_tensor(ub[:, s % 2, :], tb[:, s % 2, :], r2[:, s:s + 1], fc_b_row[:, :],
                                         ALU.mult, ALU.add).then_inc(u_done, 1)

            def mt_lo_part(t, s):
                dve.wait_ge(mt_hi, SUBS * t + s + 1)
                dve.scalar_tensor_tensor(mT[:, s % 2, 1, :, :], MT_B[:, :].rearrange("p (k n) -> p k n", k=KD),
                                         MID_SCALE, mT[:, s % 2, 0, :, :], ALU.mult, ALU.subtract)\
                   .then_inc(mt_lo, 1)

            def x1_part(t, half, s):
                dve.wait_ge(out_done, SUBS * t + s + 1)
                if s == 0:
                    dve.wait_ge(resid_done, SUBS * t + SUBS)
                    at_least(dve, x1_stored, 16 * t)
                dve.scalar_tensor_tensor(x1o[:, s, :], bank[OUT_BANK[s]][:, :], 1.0 / (H_SCALE * W_SCALE),
                                         xs[:, half, s, :], ALU.mult, ALU.add).then_inc(x1_done, 1)

            def tile(b, half):
                t = HALVES * b + half
                for g in range(GROUPS + 1):
                    if g < GROUPS:
                        p_part(t, half, g)
                    if 2 <= g < 2 + SUBS:
                        ln_stats(dve, t + 1, 1 - half, g - 2, b + half)
                    if g == 2 + SUBS:
                        ln_var(dve, t + 1)
                    if g >= 1:
                        h_part(t, g - 1)
                        h_lo_part(t, g - 1)
                ln2_stats(t)
                for s in range(SUBS):
                    tu(t, s)
                xt_lo_part(dve, t + 1, 0)
                mt_lo_part(t, 0)
                xt_lo_part(dve, t + 1, 1)
                x1_part(t, half, 0)
                mt_lo_part(t, 1)
                xt_lo_part(dve, t + 1, 2)
                x1_part(t, half, 1)
                mt_lo_part(t, 2)
                x1_part(t, half, 2)
                mt_lo_part(t, 3)
                xt_lo_part(dve, t + 1, 3)
                x1_part(t, half, 3)

            prep_over(dve)
            for half in range(HALVES):
                tile(0, half)
            with dve.Fori(1, B - 1) as b:
                for half in range(HALVES):
                    tile(b, half)
            for half in range(HALVES):
                tile(B - 1, half)

        def a_pool(pool):


            def tile(b, half, last=False):
                t = HALVES * b + half
                for g in range(GROUPS):
                    n = GROUPS * t + g
                    pool.wait_ge(h_done, n + 1)
                    if g == 0:
                        at_least(pool, stats_done, t)
                        pool.tensor_tensor(hsum[:, :], zero[:, :], hh[:, 0, :], ALU.add).then_inc(h_sum, 1)
                        pool.wait_ge(h_sq, n + 1)
                        pool.tensor_tensor(qsum[:, :], zero[:, :], sq[:, 0, :], ALU.add).then_inc(q_sum, 1)
                    else:
                        pool.wait_ge(h_sum, n)
                        pool.tensor_tensor(hsum[:, :], hsum[:, :], hh[:, g % 2, :], ALU.add).then_inc(h_sum, 1)
                        pool.wait_ge(h_sq, n + 1)
                        pool.wait_ge(q_sum, n)
                        pool.tensor_tensor(qsum[:, :], qsum[:, :], sq[:, g % 2, :], ALU.add).then_inc(q_sum, 1)
                    if g == GROUPS - 1:
                        ln_factors(pool, t + 1)
                pool.wait_ge(ln2_v, t + 1)
                pool.tensor_tensor(r2[:, :], v2[:, :], mhalf[:, :], ALU.pow).then_inc(ln2_r, 1)
                if not last:
                    residual(pool, t + 1, 1 - half)

            pool.wait_ge(p_evac, JOBS)
            residual(pool, 0, 0)
            prep_over(pool)
            for half in range(HALVES):
                tile(0, half)
            with pool.Fori(1, B - 1) as b:
                for half in range(HALVES):
                    tile(b, half)
            tile(B - 1, 0)
            tile(B - 1, 1, last=True)

        pha.close()
        mid_stack.close()

        phb = ExitStack()
        cb_ = sb_in(phb)
        RING = BSUBS
        xr = xs[:, :, :, :].rearrange("p h s d -> p (h s) d")
        we_w = cb_("we_w", [P, 2, KD, D], F16)
        wg_w = cb_("wg_w", [P, 2, KD, E], F16)
        we_raw = cb_("we_raw", [P, KD, D])
        wg_raw = cb_("wg_raw", [P, KD, E])
        be_raw = cb_("be_raw", [P, D])
        be_hi = cb_("be_hi", [P, D], F16)
        be_w = cb_("be_w", [P, D], F16)
        be_one = cb_("be_one", [P, P], F16)
        bo_row = cb_("bo_row", [P, D])
        maskb = cb_("maskb", [P, NSUB, KEYS])
        attends = cb_("attends", [P, NSUB])
        bn2, mv2, va2, rs2 = cb_("bn2", [P, 6]), cb_("mv2", [P, 2, 2]), cb_("va2", [P, 2]), cb_("rs2", [P, 2])
        bn3, mv3, va3, rs3 = cb_("bn3", [P, 6]), cb_("mv3", [P, 2, 2]), cb_("va3", [P, 2]), cb_("rs3", [P, 2])
        nm2, nb2 = cb_("nm2", [P, 2]), cb_("nb2", [P, 2])
        nm3, nb3 = cb_("nm3", [P, 2]), cb_("nb3", [P, 2])
        xn2, xn3 = cb_("xn2", [P, 2, D]), cb_("xn3", [P, 2, D])
        x2T, x3T = cb_("x2T", [P, 2, 2, KD, P], F16), cb_("x3T", [P, 2, 2, KD, P], F16)
        prT = cb_("prT", [P, 2, 2, PAIRS, P], F16)
        bias = cb_("bias", [P, 2, HEADS, KEYS])
        sc = cb_("sc", [P, 2, HEADS, KEYS])
        ex = cb_("ex", [P, 4, HEADS, KEYS])
        mx, su, ri, rw = (cb_("mx", [P, 2, HEADS]), cb_("su", [P, HEADS]), cb_("ri", [P, HEADS]),
                          cb_("rw", [P, 2, HEADS]))
        lm, nl, eqp, pm = cb_("lm", [P, 1]), cb_("nl", [P, 1]), cb_("eqp", [P, E]), cb_("pm", [P, 1])
        oh, seen = cb_("oh", [P, E], BF16), cb_("seen", [P, E], BF16)
        e8, den, rden = cb_("e8", [P, E]), cb_("den", [P, 1]), cb_("rden", [P, 1])
        kv, kept, gk = cb_("kv", [P, E]), cb_("kept", [P, 1]), cb_("gk", [P, 1])

        T2_B, S_B, PT_B, PV_B, T3_B, WE_B, R_B, LOC_B = bank
        S_SCALE = 1.0 / (LN_SCALE * W_SCALE)
        PV_SCALE = 1.0 / (PROB_SCALE * W_SCALE)

        w_landed = {n: sem(f"w_landed_{n}") for n in ("we", "wg", "be", "bo")}
        x1_landed = [sem(f"x1_landed{n}") for n in range(RING)]
        out_stored = [sem(f"out_stored{n}") for n in range(RING)]
        c_hi, c_lo, c_zero, c_mask = sem("c_hi"), sem("c_lo"), sem("c_zero"), sem("c_mask")
        bn2_done, mv2_done, va2_done, rs2_done, xn2_done = (sem("bn2_done"), sem("mv2_done"), sem("va2_done"),
                                                           sem("rs2_done"), sem("xn2_done"))
        bn3_done, mv3_done, va3_done, rs3_done, xn3_done = (sem("bn3_done"), sem("mv3_done"), sem("va3_done"),
                                                           sem("rs3_done"), sem("xn3_done"))
        nm2_done, nb2_done, nm3_done, nb3_done = sem("nm2_done"), sem("nb2_done"), sem("nm3_done"), sem("nb3_done")
        t2_tr, t2_hi, t2_lo = sem("t2_tr"), sem("t2_hi"), sem("t2_lo")
        pt_tr, pt_hi, pt_lo = sem("pt_tr"), sem("pt_hi"), sem("pt_lo")
        t3_tr, t3_hi, t3_lo = sem("t3_tr"), sem("t3_hi"), sem("t3_lo")
        s_done, pv_done, r_done, we_done, loc_done = (sem("s_done"), sem("pv_done"), sem("r_done"),
                                                      sem("we_done"), sem("loc_done"))
        bias_done, sc_done, mx_done, sub_done, ex_done = (sem("bias_done"), sem("sc_done"), sem("mx_done"),
                                                          sem("sub_done"), sem("ex_done"))
        su_done, ri_done, rw_done, pr_done, bo_done = (sem("su_done"), sem("ri_done"), sem("rw_done"),
                                                       sem("pr_done"), sem("bo_done"))
        x2_done, lm_done, nl_done, eqp_done, pm_done, oh_done = (sem("x2_done"), sem("lm_done"), sem("nl_done"),
                                                                 sem("eqp_done"), sem("pm_done"), sem("oh_done"))
        seen_done, den_done, rden_done, kept_done, gk_done, y_done = (sem("seen_done"), sem("den_done"),
                                                                      sem("rden_done"), sem("kept_done"),
                                                                      sem("gk_done"), sem("y_done"))

        LN2_AT, T2_AT, S_AT, PV_AT, WE_AT = 2, 3, 4, 6, 7
        STEPS_TAIL = WE_AT

        def real(j):
            return not isinstance(j, int) or 0 <= j < NSUB

        AHEAD = SUBS

        def fresh(j):
            return not isinstance(j, int) or AHEAD <= j < NSUB

        def a_over(eng):
            eng.wait_ge(x1_done, TILES * SUBS)

        def steps(eng, body, loaded=lambda eng: None):
            for k in range(BSUBS):
                body(0, k, lambda d: k - d)
            loaded(eng)
            with eng.Fori(1, B) as b:
                for k in range(BSUBS):
                    body(b, k, lambda d: b * BSUBS + (k - d))
            for k in range(STEPS_TAIL):
                body(B, k, lambda d: NSUB + k - d)

        def b_sp(sp):
            kn = "(k p) n -> p k n"
            sp.dma_start(wg_raw[:, :, :], Wg.rearrange(kn, p=P)).then_inc(w_landed["wg"], 16)
            sp.dma_start(bo_row[:, :], bo.partition_broadcast(P)).then_inc(w_landed["bo"], 16)
            sp.dma_start(be_raw[:, :], be.partition_broadcast(P)).then_inc(w_landed["be"], 16)
            sp.dma_start(we_raw[:, :, :], We.rearrange(kn, p=P)).then_inc(w_landed["we"], 16)

            def step(b, k, j):
                if not isinstance(b, int):
                    sp.wait_ge(out_stored[k], 16 * b)
                    sp.dma_start(xr[:, k, :], x1_dram[b * HALVES + k // SUBS, :, k % SUBS, :])\
                      .then_inc(x1_landed[k], 16)
                y = j(WE_AT)
                if real(y):
                    sp.wait_ge(y_done, y + 1)
                    slot = (k - WE_AT) % RING
                    yb = b if k >= WE_AT else b - 1
                    sp.dma_start(out_v[yb * BSUBS + slot], xr[:, slot, :]).then_inc(out_stored[slot], 16)

            steps(sp, step, lambda sp: sp.wait_ge(x1_stored, 16 * TILES))
            for n in range(RING):
                sp.wait_ge(out_stored[n], 16 * B)

        def b_pe(pe):
            def transpose4(dst, src, done):
                for c in range(KD):
                    tr = pe.transpose(dst[:, c * P:(c + 1) * P], src[:, c * P:(c + 1) * P], ident[:, :])
                tr.then_inc(done, 1)

            def pairs(lhs, rhs, chunks):
                return [(lhs[:, 0, c, :], lhs[:, 1, c, :], rhs[:, 0, c, :], rhs[:, 1, c, :])
                        for c in range(chunks)]

            def batch_of(w, b):
                return w[:, b] if isinstance(b, int) else w[:, bass.ds(b, 1)].rearrange("p b t k n -> p (b t) k n")

            def step(b, k, j):
                p, t, s, w = j(PV_AT), j(T2_AT), j(S_AT), j(WE_AT)
                if real(p):
                    if isinstance(b, int) and p == 0:
                        a_over(pe)
                    pe.wait_ge(pr_done, p + 1)
                    at_least(pe, pt_lo, p)
                    transpose4(PT_B, ex[:, (k - PV_AT) % 4, :, :].rearrange("p h n -> p (h n)"), pt_tr)
                if fresh(t):
                    pe.wait_ge(xn2_done, t - AHEAD + 1)
                    at_least(pe, t2_lo, t - AHEAD)
                    transpose4(T2_B, xn2[:, (k - T2_AT) % 2, :], t2_tr)
                if real(w):
                    pe.wait_ge(xn3_done, w + 1)
                    at_least(pe, t3_lo, w)
                    transpose4(T3_B, xn3[:, (k - WE_AT) % 2, :], t3_tr)
                if real(s):
                    sb_ = b if k >= S_AT else b - 1
                    if isinstance(b, int) and s == 0:
                        pe.wait_ge(m_landed[0], 16)
                    if fresh(s):
                        pe.wait_ge(t2_lo, s - AHEAD + 1)
                        rows = x2T[:, (k - S_AT) % 2]
                    else:
                        pe.wait_ge(xt_lo, TILES * SUBS + s + 1)
                        rows = xT[:, :, :, s * P:(s + 1) * P]
                    at_least(pe, sc_done, s)
                    product3(pe, S_B[:, :], pairs(rows, batch_of(m_w, sb_), KD)).then_inc(s_done, 1)
                if real(p):
                    pb_ = b if k >= PV_AT else b - 1
                    if isinstance(b, int) and p == 0:
                        pe.wait_ge(vw_landed[0], 16)
                    pe.wait_ge(pt_lo, p + 1)
                    at_least(pe, x2_done, p)
                    product3(pe, PV_B[:, :], pairs(prT[:, (k - PV_AT) % 2], batch_of(vw_w, pb_), PAIRS)).then_inc(pv_done, 1)
                if real(w):
                    x3 = x3T[:, (k - WE_AT) % 2]
                    if isinstance(b, int) and w == 0:
                        pe.wait_ge(c_lo, 3)
                    pe.wait_ge(t3_lo, w + 1)
                    at_least(pe, eqp_done, w)
                    at_least(pe, den_done, w)
                    product3(pe, R_B[:, 0:E], pairs(x3, wg_w, KD)).then_inc(r_done, 1)
                    at_least(pe, y_done, w)
                    product3(pe, WE_B[:, :], pairs(x3, we_w, KD), stop=False)
                    pe.matmul(WE_B[:, :], be_one[:, :], be_w[:, :], start=False, stop=True).then_inc(we_done, 1)
                    pe.wait_ge(oh_done, w + 1)
                    at_least(pe, kept_done, w)
                    pe.wait_ge(seen_done, w + 1)
                    pe.matmul(LOC_B[:, 0:E], tri[:, :], oh[:, :], start=True, stop=False)
                    pe.matmul(LOC_B[:, 0:E], ones_b[:, :], seen[:, :], start=False, stop=True)\
                      .then_inc(loc_done, 1)

            def all_loaded(pe):
                for n in range(1, B):
                    pe.wait_ge(m_landed[n], 16)
                    pe.wait_ge(vw_landed[n], 16)

            steps(pe, step, all_loaded)

        def b_act(act):
            def split_weights():
                act.wait_ge(w_landed["we"], 16)
                act.activation(we_w[:, 0, :, :], we_raw[:, :, :], ACT.Copy, scale=W_SCALE).then_inc(c_hi, 1)
                act.wait_ge(w_landed["wg"], 16)
                act.activation(wg_w[:, 0, :, :], wg_raw[:, :, :], ACT.Copy, scale=W_SCALE).then_inc(c_hi, 1)
                act.wait_ge(w_landed["be"], 16)
                act.activation(be_hi[:, :], be_raw[:, :], ACT.Copy, scale=W_SCALE).then_inc(c_hi, 1)

            def normalise(n, q, src, xn, rs, nb, nb_done, tr, xn_done):
                act.wait_ge(nb_done, n + 1)
                at_least(act, tr, n - 1)
                act.activation(xn[:, q, :], src, ACT.Identity, bias=nb[:, q:q + 1], scale=rs[:, q:q + 1])\
                   .then_inc(xn_done, 1)

            def hi_part(n, tr, dst, src, done, scale=1.0):
                act.wait_ge(tr, n + 1)
                act.activation(dst, src[:, :].rearrange("p (k n) -> p k n", k=KD), ACT.Copy, scale=scale)\
                   .then_inc(done, 1)

            def step(b, k, j):
                l, p, t, s, w = j(LN2_AT), j(PV_AT), j(T2_AT), j(S_AT), j(WE_AT)
                if real(p):
                    hi_part(p, pt_tr, prT[:, (k - PV_AT) % 2, 0], PT_B, pt_hi, PROB_SCALE)
                if fresh(t):
                    hi_part(t - AHEAD, t2_tr, x2T[:, (k - T2_AT) % 2, 0], T2_B, t2_hi)
                if real(w):
                    hi_part(w, t3_tr, x3T[:, (k - WE_AT) % 2, 0], T3_B, t3_hi)
                if fresh(l):
                    normalise(l - AHEAD, k % 2, xr[:, (k - LN2_AT) % RING, :], xn2, rs2, nb2, nb2_done, t2_tr, xn2_done)
                if real(s):
                    act.wait_ge(sub_done, s + 1)
                    at_least(act, pt_tr, s - 3)
                    act.activation(ex[:, (k - S_AT) % 4, :, :], sc[:, (k - S_AT) % 2, :, :], ACT.Exp)\
                       .then_inc(ex_done, 1)
                if real(p):
                    normalise(p, k % 2, xr[:, (k - PV_AT) % RING, :], xn3, rs3, nb3, nb3_done, t3_tr, xn3_done)
                if real(w):
                    act.wait_ge(r_done, w + 1)
                    act.wait_ge(nl_done, w + 1)
                    act.wait_ge(eqp_done, w + 1)
                    at_least(act, rden_done, w)
                    act.activation(e8[:, :], R_B[:, 0:E], ACT.Exp, bias=nl[:, :], scale=S_SCALE,
                                   accum_out=den[:, :]).then_inc(den_done, 1)
                if isinstance(b, int) and s == 0:
                    split_weights()

            steps(act, step)

        def b_pool(pool):
            a_over(pool)
            pool.memset(be_w[:, :], 0.0).then_inc(c_zero, 1)
            pool.memset(be_one[:, :], LN_SCALE).then_inc(c_zero, 1)

            def factors(n, q, va, nm, rs, nb, va_done, nm_done, rs_done, xn_done, nb_done):
                pool.wait_ge(va_done, n + 1)
                pool.wait_ge(nm_done, n + 1)
                at_least(pool, xn_done, n - 1)
                pool.tensor_tensor(rs[:, q:q + 1], va[:, q:q + 1], mhalf[:, 0:1], ALU.pow).then_inc(rs_done, 1)
                pool.wait_ge(rs_done, n + 1)
                pool.tensor_tensor(nb[:, q:q + 1], nm[:, q:q + 1], rs[:, q:q + 1], ALU.mult).then_inc(nb_done, 1)

            def step(b, k, j):
                l, t, s, p = j(LN2_AT), j(T2_AT), j(S_AT), j(PV_AT)
                if fresh(l):
                    factors(l - AHEAD, k % 2, va2, nm2, rs2, nb2, va2_done, nm2_done, rs2_done, xn2_done, nb2_done)
                if real(t):
                    q = (k - T2_AT) % 2
                    tb_ = b if k >= T2_AT else b - 1
                    at_least(pool, sc_done, t - 1)
                    pool.tensor_tensor(bias[:, q, :, :],
                                       hbias[:, tb_, :].rearrange("p (h n) -> p h n", h=HEADS),
                                       maskb[:, t, :].unsqueeze(1).to_broadcast([P, HEADS, KEYS]), ALU.add)\
                        .then_inc(bias_done, 1)
                if real(s):
                    q = (k - S_AT) % 2
                    pool.wait_ge(mx_done, s + 1)
                    pool.tensor_tensor(sc[:, q, :, :], sc[:, q, :, :],
                                       mx[:, q, :].unsqueeze(2).to_broadcast([P, HEADS, KEYS]),
                                       ALU.subtract).then_inc(sub_done, 1)
                if real(p):
                    factors(p, k % 2, va3, nm3, rs3, nb3, va3_done, nm3_done, rs3_done, xn3_done, nb3_done)
                if real(s):
                    q = (k - S_AT) % 4
                    pool.wait_ge(rw_done, s + 1)
                    pool.tensor_tensor(ex[:, q, :, :], ex[:, q, :, :],
                                       rw[:, (k - S_AT) % 2, :].unsqueeze(2).to_broadcast([P, HEADS, KEYS]),
                                       ALU.mult).then_inc(pr_done, 1)
                if real(l):
                    if fresh(l):
                        pool.wait_ge(xn2_done, l - AHEAD + 1)
                    else:
                        pool.wait_ge(xn_done, TILES * SUBS + l + 1)
                    r = xr[:, (k - LN2_AT) % RING, :]
                    pool.tensor_tensor(r, r, bo_row[:, :], ALU.add).then_inc(bo_done, 1)

            pool.wait_ge(c_mask, 1)
            pool.wait_ge(w_landed["bo"], 16)
            steps(pool, step)

        def b_dve(dve):
            a_over(dve)
            dve.tensor_scalar(maskb[:, :, :], masku[:, :, :], BIG, -BIG, ALU.mult, ALU.add).then_inc(c_mask, 1)
            dve.memset(seen[:, :], 0.0).then_inc(seen_done, 1)

            def split_weights():
                dve.wait_ge(c_hi, 1)
                dve.scalar_tensor_tensor(we_w[:, 1, :, :].rearrange("p k n -> p (k n)"),
                                         we_raw[:, :, :].rearrange("p k n -> p (k n)"), W_SCALE,
                                         we_w[:, 0, :, :].rearrange("p k n -> p (k n)"),
                                         ALU.mult, ALU.subtract).then_inc(c_lo, 1)
                dve.wait_ge(c_hi, 2)
                dve.scalar_tensor_tensor(wg_w[:, 1, :, :], wg_raw[:, :, :], W_SCALE, wg_w[:, 0, :, :],
                                         ALU.mult, ALU.subtract).then_inc(c_lo, 1)
                dve.wait_ge(c_hi, 3)
                dve.wait_ge(c_zero, 2)
                dve.tensor_copy(be_w[0:1, :], be_hi[0:1, :])
                dve.scalar_tensor_tensor(be_w[32:33, :], be_raw[32:33, :], W_SCALE, be_hi[32:33, :],
                                         ALU.mult, ALU.subtract).then_inc(c_lo, 1)

            def stats(n, q, src, bn_, mv, nm, va, bn_done, mv_done, nm_done, va_done, nb_done):
                dve.bn_stats(bn_[:, :], src).then_inc(bn_done, 1)
                carry(dve, pad_dve[:, :], (bn_done, n + 1))
                dve.bn_aggr(mv[:, q, :], bn_[:, :]).then_inc(mv_done, 1)
                dve.wait_ge(mv_done, n + 1)
                at_least(dve, nb_done, n - 1)
                dve.tensor_scalar(nm[:, q:q + 1], mv[:, q, 0:1], -1.0, None, ALU.mult).then_inc(nm_done, 1)
                dve.tensor_scalar(va[:, q:q + 1], mv[:, q, 1:2], EPS, LN_SCALE ** -2, ALU.add, ALU.mult)\
                   .then_inc(va_done, 1)

            def lo_part(n, hi, slot, src, done, scale=1.0):
                dve.wait_ge(hi, n + 1)
                dve.scalar_tensor_tensor(slot[:, 1], src[:, :].rearrange("p (k n) -> p k n", k=KD), scale,
                                         slot[:, 0], ALU.mult, ALU.subtract).then_inc(done, 1)

            def step(b, k, j):
                l, t, s, p, w = j(LN2_AT), j(T2_AT), j(S_AT), j(PV_AT), j(WE_AT)
                if real(p):
                    lo_part(p, pt_hi, prT[:, (k - PV_AT) % 2], PT_B, pt_lo, PROB_SCALE)
                if fresh(t):
                    lo_part(t - AHEAD, t2_hi, x2T[:, (k - T2_AT) % 2], T2_B, t2_lo)
                if real(w):
                    lo_part(w, t3_hi, x3T[:, (k - WE_AT) % 2], T3_B, t3_lo)
                if fresh(l):
                    slot = (k - LN2_AT) % RING
                    lb = b if k >= LN2_AT else b - 1
                    if isinstance(lb, int) and lb == 0:
                        dve.wait_ge(x_landed[1], 16 * (B + 1))
                    else:
                        at_least(dve, x1_landed[slot], 16 * lb)
                    stats(l - AHEAD, k % 2, xr[:, slot, :], bn2, mv2, nm2, va2, bn2_done, mv2_done, nm2_done,
                          va2_done, nb2_done)
                if real(s):
                    q = (k - S_AT) % 2
                    dve.wait_ge(s_done, s + 1)
                    dve.wait_ge(bias_done, s + 1)
                    at_least(dve, ex_done, s - 1)
                    dve.scalar_tensor_tensor(sc[:, q, :, :].rearrange("p h n -> p (h n)"), S_B[:, :], S_SCALE,
                                             bias[:, q, :, :].rearrange("p h n -> p (h n)"),
                                             ALU.mult, ALU.add).then_inc(sc_done, 1)
                if real(s):
                    q = (k - S_AT) % 2
                    dve.wait_ge(sc_done, s + 1)
                    at_least(dve, sub_done, s - 1)
                    dve.tensor_reduce(mx[:, q, :], sc[:, q, :, :], AX.X, ALU.max).then_inc(mx_done, 1)
                    if isinstance(b, int) and s == 0:
                        dve.tensor_reduce(attends[:, :], masku[:, :, :], AX.X, ALU.max).then_inc(c_mask, 1)
                if real(p):
                    r = xr[:, (k - PV_AT) % RING, :]
                    dve.wait_ge(pv_done, p + 1)
                    dve.wait_ge(bo_done, p + 1)
                    dve.scalar_tensor_tensor(r, PV_B[:, :], PV_SCALE, r, ALU.mult, ALU.add).then_inc(x2_done, 1)
                    dve.wait_ge(x2_done, p + 1)
                    stats(p, k % 2, r, bn3, mv3, nm3, va3, bn3_done, mv3_done, nm3_done, va3_done, nb3_done)
                if real(w):
                    dve.wait_ge(r_done, w + 1)
                    dve.tensor_reduce(lm[:, :], R_B[:, 0:E], AX.X, ALU.max).then_inc(lm_done, 1)
                    dve.wait_ge(lm_done, w + 1)
                    at_least(dve, den_done, w)
                    dve.tensor_scalar(nl[:, :], lm[:, :], -S_SCALE, None, ALU.mult).then_inc(nl_done, 1)
                    dve.scalar_tensor_tensor(eqp[:, :], R_B[:, 0:E], lm[:, :], prio[:, :],
                                             ALU.is_equal, ALU.mult).then_inc(eqp_done, 1)
                    dve.wait_ge(eqp_done, w + 1)
                    dve.tensor_reduce(pm[:, :], eqp[:, :], AX.X, ALU.max).then_inc(pm_done, 1)
                    dve.wait_ge(pm_done, w + 1)
                    at_least(dve, loc_done, w)
                    at_least(dve, kept_done, w)
                    dve.tensor_scalar(oh[:, :], eqp[:, :], pm[:, :], None, ALU.is_equal).then_inc(oh_done, 1)
                if real(s):
                    dve.wait_ge(ex_done, s + 1)
                    dve.tensor_reduce(su[:, :], ex[:, (k - S_AT) % 4, :, :], AX.X, ALU.add).then_inc(su_done, 1)
                    dve.wait_ge(su_done, s + 1)
                    dve.reciprocal(ri[:, :], su[:, :]).then_inc(ri_done, 1)
                    dve.wait_ge(ri_done, s + 1)
                    if isinstance(b, int) and s == 0:
                        dve.wait_ge(c_mask, 2)
                    at_least(dve, pr_done, s - 1)
                    dve.tensor_scalar(rw[:, (k - S_AT) % 2, :], ri[:, :], attends[:, bass.ds(s, 1)], None,
                                      ALU.mult).then_inc(rw_done, 1)
                if isinstance(b, int) and s == 0:
                    split_weights()
                if real(w):
                    dve.wait_ge(den_done, w + 1)
                    dve.reciprocal(rden[:, :], den[:, :]).then_inc(rden_done, 1)
                    dve.wait_ge(loc_done, w + 1)
                    dve.scalar_tensor_tensor(kv[:, :], LOC_B[:, 0:E], float(CAP), oh[:, :], ALU.is_le, ALU.mult,
                                             accum_out=kept[:, :]).then_inc(kept_done, 1)
                    dve.tensor_tensor(seen[:, :], seen[:, :], oh[:, :], ALU.add).then_inc(seen_done, 1)
                    dve.wait_ge(kept_done, w + 1)
                    dve.wait_ge(rden_done, w + 1)
                    dve.scalar_tensor_tensor(gk[:, :], kept[:, :], S_SCALE, rden[:, :], ALU.mult, ALU.mult)\
                       .then_inc(gk_done, 1)
                    dve.wait_ge(gk_done, w + 1)
                    dve.wait_ge(we_done, w + 1)
                    r = xr[:, (k - WE_AT) % RING, :]
                    dve.scalar_tensor_tensor(r, WE_B[:, :], gk[:, :], r, ALU.mult, ALU.add).then_inc(y_done, 1)

            steps(dve, step)

        with nc.Block() as block:
            @block.sync
            def _(sp):
                prep_sp(sp)
                a_sp(sp)
                b_sp(sp)

            @block.tensor
            def _(pe):
                prep_pe(pe)
                a_pe(pe)
                b_pe(pe)

            @block.scalar
            def _(act):
                prep_act(act)
                a_act(act)
                b_act(act)

            @block.vector
            def _(dve):
                prep_dve(dve)
                a_dve(dve)
                b_dve(dve)

            @block.gpsimd
            def _(pool):
                prep_pool(pool)
                a_pool(pool)
                b_pool(pool)
        phb.close()


def kernel(**inputs):
    import numpy as _np
    import concourse.bacc as _bacc
    from concourse import mybir as _mybir
    from concourse.bass_utils import run_bass_kernel_spmd as _run

    g = {n: _np.asarray(v) for n, v in inputs.items()}

    def columns(v):
        return v.reshape(-1, P).T

    conv = g["L0_attn_conv_w"].reshape(GROUPS, P, P, TAPS)
    layout = {
        "x": g["x"],
        "ctxT": g["ctx_1024"].reshape(B * KEYS, D).T,
        "mask": g["mask_BxSxS2_bk0"].reshape(NSUB, P, KEYS).transpose(1, 0, 2),
        "in_wT": g["L0_attn_in_proj_w"].T,
        "conv_wT": conv.transpose(2, 0, 3, 1).reshape(P, GROUPS * TAPS * P),
        "conv_b": columns(g["L0_attn_conv_b"]),
        "ln_g": columns(g["L0_attn_ln_g"]),
        "ln_b": columns(g["L0_attn_ln_b"]),
        "fc_wT": g["L0_attn_fc_w"].T,
        "fc_b": g["L0_attn_fc_b"],
        "cproj_w": g["L0_attn_cproj_w"],
        "cproj_b": columns(g["L0_attn_cproj_b"]),
        "out_wT": g["L0_attn_out_w"].T,
        "WqT": g["L0_xattn_Wq"].T,
        "bq": columns(g["L0_xattn_bq"]),
        "Wk": g["L0_xattn_Wk"],
        "bk": columns(g["L0_xattn_bk"]),
        "Wv": g["L0_xattn_Wv"],
        "bv": columns(g["L0_xattn_bv"]),
        "Wo": g["L0_xattn_Wo"],
        "bo": g["L0_xattn_bo"],
        "Wg": g["L0_ffn_Wg"],
        "We": g["L0_ffn_We"],
        "be": g["L0_ffn_be"],
        "ident": _np.eye(P, dtype=_np.float32),
        "tri": _np.triu(_np.ones((P, P), _np.float32)),
        "prio": _np.tile(_np.arange(E, 0, -1, dtype=_np.float32), (P, 1)),
    }
    nc = _bacc.Bacc("TRN2", target_bir_lowering=False, num_devices=1)
    arrays, args = {}, []
    for name, a in layout.items():
        a = _np.ascontiguousarray(a)
        arrays[f"in_{name}_dram"] = a
        args.append(nc.dram_tensor(f"in_{name}_dram", a.shape, _mybir.dt.from_np(a.dtype), kind="ExternalInput").ap())
    args.append(nc.dram_tensor("out_0_dram", (B, S, D), F32, kind="ExternalOutput").ap())
    bass_decoder_kernel(nc, *args)
    r = _run(nc, [arrays], core_ids=[0])
    return r.results[0]["out_0_dram"]
```

```python
from contextlib import ExitStack

import concourse.bass as bass
from concourse import mybir

ALU = mybir.AluOpType
ACT = mybir.ActivationFunctionType
AX = mybir.AxisListType
F32 = mybir.dt.float32
F16 = mybir.dt.float16
BF16 = mybir.dt.bfloat16

P = 128
B, S, D = 4, 1024, 512
I = 1024
MID = 512
TAPS, GROUPS = 4, 8
KEYS, HEADS = 64, 8
E = 8
CAP = B * S // E
EPS = 1e-5
TILE = 512
SUBS = TILE // P
HALVES = S // TILE
TILES = B * HALVES
KD = D // P
KI = I // P
HALF = TILE // 2
HALO = TAPS // 2
BSUBS = S // P
NSUB = B * BSUBS
PAIRS = HEADS // 2
BIG = 1e30

W_SCALE = 2.0 ** 8
LN_SCALE = 2.0 ** 8
P_SCALE = 2.0 ** 6
H_SCALE = 2.0 ** 7
MID_SCALE = 2.0 ** 6
W2_SCALE = H_SCALE * W_SCALE / MID_SCALE
PROB_SCALE = 2.0 ** 12


def carry(dve, pad, *waits):
    for s, v in waits:
        at_least(dve, s, v)
    dve.memset(pad, 0.0)


def at_least(eng, sem, value):
    if isinstance(value, int) and value <= 0:
        return
    eng.wait_ge(sem, value)


def product3(pe, out, chunks, start=True, stop=True):
    last = len(chunks) - 1
    for n, (l_hi, l_lo, r_hi, r_lo) in enumerate(chunks):
        pe.matmul(out, l_hi, r_hi, start=start and n == 0, stop=False)
        pe.matmul(out, l_hi, r_lo, start=False, stop=False)
        mm = pe.matmul(out, l_lo, r_hi, start=False, stop=stop and n == last)
    return mm


def bass_decoder_kernel(
    nc, x, ctxT, mask, in_wT, conv_wT, conv_b, ln_g, ln_b, fc_wT, fc_b, cproj_w, cproj_b, out_wT,
    WqT, bq, Wk, bk, Wv, bv, Wo, bo, Wg, We, be, ident_in, tri_in, prio_in, out,
):
    x_v = x.rearrange("b (h s p) d -> b h p s d", h=HALVES, p=P)
    x1_dram = nc.dram_tensor("x1_scratch", (B * HALVES, P, SUBS, D), F32).ap()
    out_v = out.rearrange("b (s p) d -> (b s) p d", p=P)
    m_dram = nc.dram_tensor("m_scratch", (B, P, 2, KD, HEADS * KEYS), F16).ap()
    vw_dram = nc.dram_tensor("vw_scratch", (B, P, 2, PAIRS, D), F16).ap()

    top = ExitStack()
    with top:
        def sem(name):
            return top.enter_context(nc.semaphore(name))

        def sb_in(stack):
            return lambda name, shape, dt=F32: stack.enter_context(nc.sbuf_tensor(name, shape, dt))

        bank = [top.enter_context(nc.psum_tensor(f"bank{n}", [P, 512], F32)) for n in range(8)]

        sb = sb_in(top)
        ident = sb("ident", [P, P])
        hbias = sb("hbias", [P, B, HEADS * KEYS])
        masku = sb("masku", [P, NSUB, KEYS], mybir.dt.uint8)
        tri = sb("tri", [P, P], BF16)
        ones_b = sb("ones_b", [P, P], BF16)
        prio = sb("prio", [P, E])
        attends = sb("attends", [P, NSUB])
        mhalf = sb("mhalf", [P, SUBS])
        pad_dve = sb("pad_dve", [P, 1])
        bo_row = sb("bo_row", [P, D])
        xs = sb("xs", [P, HALVES, SUBS, D])
        xn = sb("xn", [P, SUBS, D])
        xT = sb("xT", [P, 2, KD, TILE], F16)
        bn, mv = sb("bn", [P, SUBS, 6]), sb("mv", [P, SUBS, 2])
        va, rs = sb("va", [P, SUBS]), sb("rs", [P, SUBS])
        nm, nb = sb("nm", [P, SUBS]), sb("nb", [P, SUBS])
        in_w = sb("in_w", [P, 2, KD, 2 * I], F16)
        conv_fc_w = sb("conv_fc_w", [P, 2 * GROUPS * TAPS * P + 2 * KI * MID], F16)
        conv_w = conv_fc_w[:, 0:2 * GROUPS * TAPS * P].rearrange("p (t g k o) -> p t g k o", t=2, g=GROUPS, k=TAPS)
        fc_w = conv_fc_w[:, 2 * GROUPS * TAPS * P:].rearrange("p (t k n) -> p t k n", t=2, k=KI)
        m_w = in_w[:, :, :, :].rearrange("p t k n -> p (t k n)").rearrange(
            "p (b t k n) -> p b t k n", b=B, t=2, k=KD)
        vw_w = conv_fc_w[:, :].rearrange("p (b t k n) -> p b t k n", b=B, t=2, k=PAIRS)

        mid_stack = ExitStack()
        mb = sb_in(mid_stack)
        out_w = mb("out_w", [P, 2, KI, D], F16)
        w2 = mb("w2", [P, 2, KD, D], F16)
        fc_g = mb("fc_g", [P, KD])
        fc_bs = mb("fc_bs", [P, KD])
        out_b_row = mb("out_b_row", [P, D])
        conv_bs = mb("conv_bs", [P, GROUPS])
        conv_d = mb("conv_d", [P, 2, GROUPS, TAPS // 2, P], F16)
        ones1 = mb("ones1", [P, 1])
        zero = mb("zero", [P, TILE])

        x_landed = [sem(f"x_landed{h}") for h in range(HALVES)]
        bn_done, mv_done, va_done, rs_done = sem("bn_done"), sem("mv_done"), sem("va_done"), sem("rs_done")
        nm_done, nb_done = sem("nm_done"), sem("nb_done")
        xn_done = sem("xn_done")
        resid_done = sem("resid_done")
        xt_tr, xt_hi, xt_lo = sem("xt_tr"), sem("xt_hi"), sem("xt_lo")
        iph, ipg = sem("iph"), sem("ipg")
        p_hi_done, p_lo_done, p_halo, p_ready = sem("p_hi_done"), sem("p_lo_done"), sem("p_halo"), sem("p_ready")
        d_done, d_hi, d_lo = sem("d_done"), sem("d_hi"), sem("d_lo")
        q2_done, o_done, eo_done = sem("q2_done"), sem("o_done"), sem("eo_done")
        gate_done = sem("gate_done")
        conv_done = sem("conv_done")
        h_done = sem("h_done")
        h_hi, h_lo, h_sq, h_sum, q_sum = sem("h_hi"), sem("h_lo"), sem("h_sq"), sem("h_sum"), sem("q_sum")
        stats_done = sem("stats_done")
        ln2_mneg, ln2_e2, ln2_msq, ln2_v, ln2_r = (sem("ln2_mneg"), sem("ln2_e2"), sem("ln2_msq"),
                                                   sem("ln2_v"), sem("ln2_r"))
        fc_done, t_done, u_done, silu_done = sem("fc_done"), sem("t_done"), sem("u_done"), sem("silu_done")
        mt_hi, mt_lo = sem("mt_hi"), sem("mt_lo")
        diag_done, vd_done, r2_row = sem("diag_done"), sem("vd_done"), sem("r2_row")
        h_used = sem("h_used")
        out_done, x1_done, x1_stored = sem("out_done"), sem("x1_done"), sem("x1_stored")

        m_landed, vw_landed = [[sem(f"{n}_landed_first"), sem(f"{n}_landed_rest")] for n in ("m", "vw")]

        OUT_BANK = [6, 7, 2, 3]
        CONV_BANK = [(2, 3), (5, 6)]
        FC_SQ = (H_SCALE * W_SCALE) ** 2
        XT_B, SUM_B, SQ_B = bank[4], bank[7], bank[5]

        def transpose_x(pe, t, s):
            pe.wait_ge(xn_done, SUBS * t + s + 1)
            at_least(pe, xt_lo, SUBS * t + s)
            for k in range(KD):
                tr = pe.transpose(XT_B[:, k * P:(k + 1) * P], xn[:, s, k * P:(k + 1) * P], ident[:, :])
            tr.then_inc(xt_tr, 1)

        def xt_hi_part(act, t, s):
            act.wait_ge(xt_tr, SUBS * t + s + 1)
            at_least(act, ipg, GROUPS * t)
            act.activation(xT[:, 0, :, s * P:(s + 1) * P],
                           XT_B[:, :].rearrange("p (k n) -> p k n", k=KD), ACT.Copy)\
               .then_inc(xt_hi, 1)

        def normalise_x(act, t, half, s):
            if s == 0:
                act.wait_ge(nb_done, t + 1)
                at_least(act, xt_tr, SUBS * t)
            act.activation(xn[:, s, :], xs[:, half, s, :], ACT.Identity, bias=nb[:, s:s + 1],
                           scale=rs[:, s:s + 1]).then_inc(xn_done, 1)

        def ln_stats(dve, t, half, s, b_use):
            if s == 0:
                dve.wait_ge(x_landed[half], 16 * (b_use + 1))
            dve.bn_stats(bn[:, s, :], xs[:, half, s, :]).then_inc(bn_done, 1)

        def ln_var(dve, t):
            carry(dve, pad_dve[:, :], (bn_done, SUBS * t + SUBS), (xn_done, SUBS * t))
            for s in range(SUBS):
                ins = dve.bn_aggr(mv[:, s, :], bn[:, s, :])
            ins.then_inc(mv_done, 1)
            dve.wait_ge(mv_done, t + 1)
            dve.tensor_scalar(nm[:, :], mv[:, :, 0], -1.0, None, ALU.mult).then_inc(nm_done, 1)
            dve.tensor_scalar(va[:, :], mv[:, :, 1], EPS, LN_SCALE ** -2, ALU.add, ALU.mult)\
               .then_inc(va_done, 1)

        def xt_lo_part(dve, t, s):
            dve.wait_ge(xt_hi, SUBS * t + s + 1)
            r = slice(s * P, (s + 1) * P)
            dve.tensor_tensor(xT[:, 1, :, r], XT_B[:, :].rearrange("p (k n) -> p k n", k=KD),
                              xT[:, 0, :, r], ALU.subtract).then_inc(xt_lo, 1)

        def ln_factors(pool, t):
            pool.wait_ge(va_done, t + 1)
            pool.wait_ge(nm_done, t + 1)
            pool.tensor_tensor(rs[:, :], va[:, :], mhalf[:, :], ALU.pow).then_inc(rs_done, 1)
            at_least(pool, rs_done, t + 1)
            pool.tensor_tensor(nb[:, :], nm[:, :], rs[:, :], ALU.mult).then_inc(nb_done, 1)

        def residual(pool, t, half):
            for s in range(SUBS):
                pool.wait_ge(xn_done, SUBS * t + s + 1)
                pool.tensor_tensor(xs[:, half, s, :], xs[:, half, s, :], out_b_row[:, :], ALU.add)\
                    .then_inc(resid_done, 1)

        prep = ExitStack()
        pb = sb_in(prep)
        raw0 = pb("raw0", [P, (KD - 1) * 2 * I])
        raw1 = pb("raw1", [P, 4 * KD * D])
        kbd = xs[:, 0, :, :].rearrange("p c (b n) -> p c b n", b=B)
        vbd = w2[:, :, :, :].rearrange("p t k n -> p (t k n)").bitcast(F32).rearrange(
            "p (c b n) -> p c b n", c=PAIRS, b=B)
        raw2 = xs[:, 1, :, :].rearrange("p s d -> p (s d)")
        ctx = xn[:, 0:2, :].rearrange("p s d -> p (s d)").rearrange("p (k n) -> p k n", k=KD)
        VW_SLOTS = 4
        vw_stage = xT[:, :, :, :].rearrange("p t k n -> p (t k) n").rearrange("p (s t) n -> p s t n", s=VW_SLOTS)
        ones16 = pb("ones16", [P, P], F16)
        fc_rows = pb("fc_rows", [P, MID])
        raw_conv_d = xn[:, :, :].rearrange("p s d -> p (s d)")
        cb16 = pb("cb16", [P, 2, KI], F16)
        vec = pb("vec", [P, 4 * KI + 3 * KD])
        g256 = pb("g256", [P, KI])
        tri_f = xn[:, 2, 0:P]

        conv_bv, ln_gv, ln_bv, cproj_bv = [vec[:, n * KI:(n + 1) * KI] for n in range(4)]
        bqv, bkv, bvv = [vec[:, 4 * KI + n * KD:4 * KI + (n + 1) * KD] for n in range(3)]
        raw_in = [raw0[:, k * 2 * I:(k + 1) * 2 * I] for k in range(KD - 1)] + [raw2]
        raw_conv = raw0[:, 0:GROUPS * TAPS * P]
        raw_fc_half = [r.rearrange("p (k n) -> p k n", n=MID) for r in (raw0[:, GROUPS * TAPS * P:], raw2)]
        raw_fc = [raw_fc_half[k // (KI // 2)][:, k % (KI // 2), :] for k in range(KI)]
        wk_r, wv_r, wq_r, wo_r = [raw1[:, n * KD * D:(n + 1) * KD * D].rearrange("p (k n) -> p k n", k=KD)
                                  for n in range(4)]
        m_stage = [raw1[:, n * KD * D:(n + 1) * KD * D].bitcast(F16).rearrange(
            "p (b t n) -> p b t n", b=B, t=2) for n in range(2)]
        raw_out = raw1[:, 0:KI * D].rearrange("p (k n) -> p k n", k=KI)
        raw_cproj = raw1[:, KI * D:2 * KI * D].rearrange("p (k n) -> p k n", k=KI)
        cproj = raw1[:, 0:KI * D].bitcast(F16).rearrange("p (t k n) -> p t k n", t=2, k=KI)

        names = ["small", "k0", "k1", "wv", "wq", "wo", "in0", "in1", "conv", "fc", "outw", "cproj"]
        landed = {n: sem(f"landed_{n}") for n in names}
        SMALL = 13
        p_const = sem("p_const")
        p_job = sem("p_job")
        p_hi = sem("p_hi")
        p_evac = sem("p_evac")
        p_whi = sem("p_whi")
        p_wlo = sem("p_wlo")
        p_vec = sem("p_vec")
        p_dif = sem("p_dif")
        p_cb = sem("p_cb")
        m_stored = [sem(f"m_stored{n}") for n in range(2)]
        vw_stored = [sem(f"vw_stored{n}") for n in range(VW_SLOTS)]

        K_JOB, V_JOB, HB_JOB, M_JOB = 0, KD, 2 * KD, 2 * KD + PAIRS
        VW_JOB = M_JOB + KD * PAIRS
        FC_B_JOB, FC_B_COL_JOB, FC_G_JOB, OUT_B_JOB, FC_G_COL_JOB = [VW_JOB + B * PAIRS + n for n in range(5)]
        W2_JOB = FC_G_COL_JOB + 1
        JOBS = W2_JOB + KD

        def job_bank(n):
            return bank[(n - JOBS) % 8]

        IN_N, CONV_N, FC_N, OUT_N = KD, 2, KI, 2
        FC_PIECE, CONV_PIECE = 0, FC_N
        CONV_D_PIECE = FC_N + CONV_N
        OUT_PIECE = CONV_D_PIECE + 1
        CPROJ_PIECE = OUT_PIECE + OUT_N
        CPROJ_N = 4
        IN_PIECE = CPROJ_PIECE + CPROJ_N
        PIECES = IN_PIECE + IN_N
        CONV_PIECE_SIZE = GROUPS * TAPS * P // CONV_N

        def piece(n):
            if n < CONV_PIECE:
                k = n
                return fc_w[:, 0, k, :], fc_w[:, 1, k, :], raw_fc[k], g256[:, k:k + 1]
            if n == CONV_D_PIECE:
                hi, lo = [conv_d[:, t, :, :, :].rearrange("p g k o -> p (g k o)") for t in range(2)]
                return hi, lo, raw_conv_d, W_SCALE
            if n < OUT_PIECE:
                q = n - CONV_PIECE
                hi, lo = [conv_w[:, t, 4 * q:4 * q + 4, :, :].rearrange("p g k o -> p (g k o)") for t in range(2)]
                return hi, lo, raw_conv[:, q * CONV_PIECE_SIZE:(q + 1) * CONV_PIECE_SIZE], W_SCALE
            if CPROJ_PIECE <= n < IN_PIECE:
                q = slice((n - CPROJ_PIECE) * KI // CPROJ_N, (n - CPROJ_PIECE + 1) * KI // CPROJ_N)
                hi, lo = [cproj[:, t, q, :].rearrange("p k n -> p (k n)") for t in range(2)]
                return hi, lo, raw_cproj[:, q, :].rearrange("p k n -> p (k n)"), W_SCALE
            if n < IN_PIECE:
                q = n - OUT_PIECE
                hi, lo = [out_w[:, t, 4 * q:4 * q + 4, :].rearrange("p k n -> p (k n)") for t in range(2)]
                return hi, lo, raw_out[:, 4 * q:4 * q + 4, :].rearrange("p k n -> p (k n)"), W_SCALE
            k = n - IN_PIECE
            return in_w[:, 0, k, :], in_w[:, 1, k, :], raw_in[k], W_SCALE

        def m_out(n):
            m, c = n // PAIRS, n % PAIRS
            return m_stage[m % 2][:, :, :, c * P:(c + 1) * P]

        def vw_out(n):
            return vw_stage[:, n % VW_SLOTS, :, :]

        def prep_over(eng):
            eng.wait_ge(p_evac, JOBS)
            eng.wait_ge(p_wlo, PIECES)

        def prep_sp(sp):
            kn = "(k p) n -> p k n"
            for n in range(2):
                q = slice(2 * n, 2 * n + 2)
                sp.dma_start(ctx[:, q, :], ctxT.rearrange(kn, p=P)[:, q, :]).then_inc(landed[f"k{n}"], 16)
                sp.dma_start(wk_r[:, q, :], Wk.rearrange(kn, p=P)[:, q, :]).then_inc(landed[f"k{n}"], 16)
            for n, v in enumerate([conv_b, ln_g, ln_b, cproj_b]):
                sp.dma_start(vec[:, n * KI:(n + 1) * KI], v).then_inc(landed["small"], 16)
            for n, v in enumerate([bq, bk, bv]):
                sp.dma_start(vec[:, 4 * KI + n * KD:4 * KI + (n + 1) * KD], v).then_inc(landed["small"], 16)
            sp.dma_start(ident[:, :], ident_in).then_inc(landed["small"], 16)
            sp.dma_start(tri_f, tri_in).then_inc(landed["small"], 16)
            sp.dma_start(prio[:, :], prio_in).then_inc(landed["small"], 16)
            sp.dma_start(masku[:, :, :], mask).then_inc(landed["small"], 16)
            sp.dma_start(fc_bs[:, :], fc_b).then_inc(landed["small"], 16)
            sp.dma_start(bo_row[:, :], bo.partition_broadcast(P)).then_inc(landed["small"], 16)
            sp.dma_start(wv_r, Wv.rearrange(kn, p=P)).then_inc(landed["wv"], 16)
            sp.dma_start(wq_r, WqT.rearrange(kn, p=P)).then_inc(landed["wq"], 16)
            for h in range(2):
                q = slice(h * KI // 2, (h + 1) * KI // 2)
                sp.dma_start(raw_fc_half[h], fc_wT.rearrange(kn, p=P)[:, q, :]).then_inc(landed["fc"], 16)
            sp.dma_start(wo_r, Wo.rearrange(kn, p=P)).then_inc(landed["wo"], 16)
            sp.dma_start(raw_conv, conv_wT).then_inc(landed["conv"], 16)
            for m in range(KD):
                sp.wait_ge(p_evac, M_JOB + PAIRS * (m + 1))
                for b in range(B):
                    sp.dma_start(m_dram[b, :, :, m, :], m_stage[m % 2][:, b, :, :]).then_inc(m_stored[m % 2], 16)
            out_raw = out_wT.rearrange(kn, p=P)
            for n in range(B * PAIRS):
                sp.wait_ge(p_evac, VW_JOB + n + 1)
                sp.dma_start(vw_dram[n // PAIRS, :, :, n % PAIRS, :], vw_out(n)).then_inc(vw_stored[n % VW_SLOTS], 16)
                if n == 1:
                    sp.wait_ge(m_stored[0], 16 * B * KD // 2)
                    sp.wait_ge(m_stored[1], 16 * B * KD // 2)
                if n in (1, 7):
                    q = slice(0, KI // 2) if n == 1 else slice(KI // 2, KI)
                    sp.dma_start(raw_out[:, q, :], out_raw[:, q, :]).then_inc(landed["outw"], 16)
            sp.dma_start(raw_cproj, cproj_w.rearrange(kn, p=P)).then_inc(landed["cproj"], 16)
            sp.dma_start(xs[:, 0, :, :], x_v[0, 0]).then_inc(x_landed[0], 16)
            sp.wait_ge(p_whi, OUT_PIECE)
            sp.wait_ge(p_wlo, OUT_PIECE)
            sp.wait_ge(p_job, FC_B_JOB + 1)
            for k in range(KD):
                sp.dma_start(raw_in[k], in_wT[k * P:(k + 1) * P, :]).then_inc(landed[f"in{k // 2}"], 16)
            sp.wait_ge(p_whi, PIECES)
            sp.wait_ge(p_wlo, PIECES)
            sp.dma_start(xs[:, 1, :, :], x_v[0, 1]).then_inc(x_landed[1], 16)

        def prep_pool(pool):
            pool.memset(kbd, 0.0).then_inc(p_const, 1)
            pool.memset(vbd, 0.0).then_inc(p_const, 1)
            pool.memset(ones_b[:, :], 1.0).then_inc(p_const, 1)
            pool.memset(mhalf[:, :], -0.5).then_inc(p_const, 1)
            pool.memset(zero[:, :], 0.0).then_inc(p_const, 1)
            pool.memset(ones16[:, :], 1.0).then_inc(p_const, 1)
            pool.wait_ge(landed["conv"], 16)
            pool.wait_ge(p_job, V_JOB + KD)
            pool.wait_ge(p_vec, 4)
            taps = raw_conv.rearrange("p (g q o) -> p g q o", q=2, o=P)
            pool.tensor_tensor(raw_conv_d.rearrange("p (g o) -> p g o", o=P), taps[:, :, 0, :], taps[:, :, 1, :],
                               ALU.subtract).then_inc(p_dif, 1)
            pool.wait_ge(p_const, 6)
            ln_factors(pool, 0)

        def prep_pe(pe):
            def slot(n):
                at_least(pe, p_evac, n - 7)
                return job_bank(n)

            for k in range(KD):
                if k % 2 == 0:
                    pe.wait_ge(landed[f"k{k // 2}"], 32)
                for m in range(KD):
                    mm = pe.matmul(slot(K_JOB + m)[:, 0:B * KEYS], wk_r[:, k, m * P:(m + 1) * P], ctx[:, k, :],
                                   start=(k == 0), stop=(k == KD - 1))
                    if k == KD - 1:
                        mm.then_inc(p_job, 1)
            pe.wait_ge(landed["wv"], 16)
            for m in range(KD):
                o = slot(V_JOB + m)[:, 0:B * KEYS]
                for k in range(KD):
                    mm = pe.matmul(o, wv_r[:, k, m * P:(m + 1) * P], ctx[:, k, :], start=(k == 0), stop=(k == KD - 1))
                mm.then_inc(p_job, 1)
            pe.wait_ge(p_evac, K_JOB + KD)
            for c in range(PAIRS):
                o = slot(HB_JOB + c)
                pe.matmul(o[:, :], bqv[:, c:c + 1].to_broadcast([P, P]), kbd[:, c, :, :].rearrange("p b n -> p (b n)"),
                          start=True, stop=True).then_inc(p_job, 1)
            pe.wait_ge(landed["wq"], 16)
            for m in range(KD):
                for c in range(PAIRS):
                    o = slot(M_JOB + PAIRS * m + c)
                    pe.matmul(o[:, :], wq_r[:, c, m * P:(m + 1) * P], kbd[:, c, :, :].rearrange("p b n -> p (b n)"),
                              start=True, stop=True).then_inc(p_job, 1)
            pe.wait_ge(landed["wo"], 16)
            pe.wait_ge(p_evac, V_JOB + KD)
            for b in range(B):
                for c in range(PAIRS):
                    o = slot(VW_JOB + PAIRS * b + c)
                    pe.matmul(o[:, :], vbd[:, c, b, :], wo_r[:, c, :], start=True, stop=True).then_inc(p_job, 1)
            pe.wait_ge(landed["fc"], 32)
            o = slot(FC_B_JOB)
            for k in range(KI):
                mm = pe.matmul(o[:, :], ln_bv[:, k:k + 1].to_broadcast([P, P]), raw_fc[k],
                               start=(k == 0), stop=(k == KI - 1))
            mm.then_inc(p_job, 1)

            def to_columns(job, row_job):
                pe.wait_ge(p_evac, row_job + 1)
                o = slot(job)
                for c in range(KD):
                    tr = pe.transpose(o[:, c * P:(c + 1) * P], fc_rows[:, c * P:(c + 1) * P], ident[:, :])
                tr.then_inc(p_job, 1)

            to_columns(FC_B_COL_JOB, FC_B_JOB)
            pe.wait_ge(p_const, 6)
            pe.wait_ge(p_wlo, FC_PIECE + FC_N)
            o = slot(FC_G_JOB)
            for k in range(KI):
                for q in range(2):
                    mm = pe.matmul(o[:, :], ones16[:, :], fc_w[:, q, k, :], start=(k + q == 0),
                                   stop=(k == KI - 1 and q == 1))
            mm.then_inc(p_job, 1)
            pe.wait_ge(p_vec, 6)
            pe.wait_ge(p_wlo, OUT_PIECE + OUT_N)
            product3(pe, slot(OUT_B_JOB)[:, :],
                     [(cb16[:, 0, k:k + 1].to_broadcast([P, P]), cb16[:, 1, k:k + 1].to_broadcast([P, P]),
                       out_w[:, 0, k, :], out_w[:, 1, k, :]) for k in range(KI)]).then_inc(p_job, 1)
            to_columns(FC_G_COL_JOB, FC_G_JOB)
            for m in range(KD):
                o = slot(W2_JOB + m)
                for k in range(KI):
                    if m == KD - 1 and k == KI // 2:
                        transpose_x(pe, 0, 2)
                    if m == 0 and k % 2 == 0:
                        pe.wait_ge(p_wlo, CPROJ_PIECE + k // 2 + 1)
                    mm = product3(pe, o[:, :], [(cproj[:, 0, k, m * P:(m + 1) * P], cproj[:, 1, k, m * P:(m + 1) * P],
                                                 out_w[:, 0, k, :], out_w[:, 1, k, :])],
                                  start=(k == 0), stop=(k == KI - 1))
                mm.then_inc(p_job, 1)
                if m == 1:
                    pe.wait_ge(p_evac, W2_JOB + 1)
                    transpose_x(pe, 0, 0)
                if m == 2:
                    transpose_x(pe, 0, 1)
            transpose_x(pe, 0, 3)
            pe.wait_ge(p_whi, PIECES)
            pe.wait_ge(p_wlo, PIECES)

        def prep_act(act):
            def split(n):
                hi, lo, raw, scale = piece(n)
                if n in (IN_PIECE, IN_PIECE + 2):
                    act.wait_ge(landed[f"in{(n - IN_PIECE) // 2}"], 32)
                act.activation(hi, raw, ACT.Copy, scale=scale).then_inc(p_whi, 1)

            for m in range(KD):
                for c in range(PAIRS):
                    n = PAIRS * m + c
                    act.wait_ge(p_job, M_JOB + n + 1)
                    if m < 2:
                        act.wait_ge(p_evac, V_JOB + KD)
                    else:
                        act.wait_ge(m_stored[m % 2], 16 * B)
                    act.activation(m_out(n)[:, :, 0, :], job_bank(M_JOB + n)[:, :].rearrange("p (b n) -> p b n", b=B),
                                   ACT.Copy).then_inc(p_hi, 1)
                if m == 0:
                    act.wait_ge(landed["fc"], 32)
                    act.wait_ge(p_vec, 2)
                for k in (2 * m, 2 * m + 1):
                    split(FC_PIECE + k)
            for n in range(B * PAIRS):
                act.wait_ge(p_job, VW_JOB + n + 1)
                if n >= VW_SLOTS:
                    act.wait_ge(vw_stored[n % VW_SLOTS], 16 * (n // VW_SLOTS))
                act.activation(vw_out(n)[:, 0, :], job_bank(VW_JOB + n)[:, :],
                               ACT.Copy, scale=W_SCALE).then_inc(p_hi, 1)
                if n == 0:
                    act.wait_ge(landed["conv"], 16)
                if n in (0, 4):
                    split(CONV_PIECE + n // 4)
                if n == 8:
                    act.wait_ge(p_dif, 1)
                    split(CONV_D_PIECE)
            act.activation(cb16[:, 0, :], cproj_bv, ACT.Copy, scale=W_SCALE).then_inc(p_cb, 1)
            act.wait_ge(landed["outw"], 32)
            for n in range(OUT_N):
                split(OUT_PIECE + n)
            act.wait_ge(landed["cproj"], 16)
            act.wait_ge(p_wlo, CPROJ_PIECE)
            for n in range(CPROJ_N):
                split(CPROJ_PIECE + n)
            def w2_hi(m):
                act.wait_ge(p_job, W2_JOB + m + 1)
                act.activation(w2[:, 0, m, :], job_bank(W2_JOB + m)[:, :], ACT.Copy,
                               scale=W2_SCALE / W_SCALE ** 2).then_inc(p_hi, 1)

            w2_hi(0)
            split(IN_PIECE)
            act.wait_ge(p_wlo, OUT_PIECE)
            for s in range(SUBS):
                normalise_x(act, 0, 0, s)
            w2_hi(1)
            split(IN_PIECE + 1)
            for n in range(VW_SLOTS):
                act.wait_ge(vw_stored[n], 16 * B * PAIRS // VW_SLOTS)
            xt_hi_part(act, 0, 0)
            split(IN_PIECE + 2)
            w2_hi(2)
            xt_hi_part(act, 0, 1)
            split(IN_PIECE + 3)
            xt_hi_part(act, 0, 2)
            w2_hi(3)
            xt_hi_part(act, 0, 3)

        def prep_dve(dve):
            def split(n):
                hi, lo, raw, scale = piece(n)
                dve.wait_ge(p_whi, n + 1)
                dve.scalar_tensor_tensor(lo, raw, scale, hi, ALU.mult, ALU.subtract).then_inc(p_wlo, 1)

            dve.memset(ones1[:, :], 1.0).then_inc(p_vec, 1)
            dve.wait_ge(landed["small"], 16 * SMALL)
            dve.tensor_scalar(g256[:, :], ln_gv, W_SCALE, None, ALU.mult).then_inc(p_vec, 1)
            dve.tensor_scalar(conv_bs[:, :], conv_bv, P_SCALE * W_SCALE, None, ALU.mult).then_inc(p_vec, 1)
            dve.tensor_copy(tri[:, :], tri_f).then_inc(p_vec, 1)
            dve.tensor_reduce(attends[:, :], masku[:, :, :], AX.X, ALU.max).then_inc(p_vec, 1)
            for job, bd, bias, scale, const in ((K_JOB, kbd, bkv, 0.125 * W_SCALE, 1), (V_JOB, vbd, bvv, 1.0, 2)):
                dve.wait_ge(p_const, const)
                for m in range(KD):
                    dve.wait_ge(p_job, job + m + 1)
                    for q in range(2):
                        r = slice(64 * q, 64 * q + 64)
                        ins = dve.tensor_scalar(
                            bd[r, m, :, r], job_bank(job + m)[r, 0:B * KEYS].rearrange("p (b n) -> p b n", b=B),
                            bias[r, m:m + 1], scale, ALU.add, ALU.mult)
                    ins.then_inc(p_evac, 1)
            for c in range(PAIRS):
                dve.wait_ge(p_job, HB_JOB + c + 1)
                dve.tensor_scalar(hbias[:, :, c * P:(c + 1) * P],
                                  job_bank(HB_JOB + c)[:, :].rearrange("p (b n) -> p b n", b=B),
                                  1.0 / W_SCALE, None, ALU.mult).then_inc(p_evac, 1)
            for m in range(KD):
                for c in range(PAIRS):
                    n = PAIRS * m + c
                    dve.wait_ge(p_hi, n + 1)
                    dve.tensor_tensor(m_out(n)[:, :, 1, :],
                                      job_bank(M_JOB + n)[:, :].rearrange("p (b n) -> p b n", b=B),
                                      m_out(n)[:, :, 0, :], ALU.subtract).then_inc(p_evac, 1)
                for k in (2 * m, 2 * m + 1):
                    split(FC_PIECE + k)
            for n in range(B * PAIRS):
                dve.wait_ge(p_hi, KD * PAIRS + n + 1)
                dve.scalar_tensor_tensor(vw_out(n)[:, 1, :], job_bank(VW_JOB + n)[:, :], W_SCALE,
                                         vw_out(n)[:, 0, :], ALU.mult, ALU.subtract).then_inc(p_evac, 1)
                if n in (0, 4, 8):
                    split(CONV_PIECE + n // 4)
            dve.wait_ge(p_cb, 1)
            dve.scalar_tensor_tensor(cb16[:, 1, :], cproj_bv, W_SCALE, cb16[:, 0, :], ALU.mult, ALU.subtract)\
               .then_inc(p_vec, 1)
            def column_of(job):
                return job_bank(job)[:, :].rearrange("p (c n) -> p c n", c=KD)[:, :, 0]

            dve.wait_ge(p_job, FC_B_JOB + 1)
            dve.tensor_copy(fc_rows[:, :], job_bank(FC_B_JOB)[:, :]).then_inc(p_evac, 1)
            split(OUT_PIECE)
            dve.wait_ge(p_job, FC_B_COL_JOB + 1)
            dve.tensor_tensor(fc_bs[:, :], column_of(FC_B_COL_JOB), fc_bs[:, :], ALU.add).then_inc(p_evac, 1)
            split(OUT_PIECE + 1)
            dve.wait_ge(p_job, FC_G_JOB + 1)
            dve.tensor_scalar(fc_rows[:, :], job_bank(FC_G_JOB)[:, :], H_SCALE, None, ALU.mult).then_inc(p_evac, 1)
            for n in range(CPROJ_N):
                split(CPROJ_PIECE + n)
            for s in range(SUBS):
                ln_stats(dve, 0, 0, s, 0)
            ln_var(dve, 0)
            dve.wait_ge(p_job, OUT_B_JOB + 1)
            dve.tensor_scalar(out_b_row[:, :], job_bank(OUT_B_JOB)[:, :], 1.0 / W_SCALE ** 2, None,
                              ALU.mult).then_inc(p_evac, 1)
            dve.wait_ge(p_job, FC_G_COL_JOB + 1)
            dve.tensor_copy(fc_g[:, :], column_of(FC_G_COL_JOB)).then_inc(p_evac, 1)

            def w2_lo(m):
                dve.wait_ge(p_hi, (KD + B) * PAIRS + m + 1)
                dve.scalar_tensor_tensor(w2[:, 1, m, :], job_bank(W2_JOB + m)[:, :], W2_SCALE / W_SCALE ** 2,
                                         w2[:, 0, m, :], ALU.mult, ALU.subtract).then_inc(p_evac, 1)

            w2_lo(0)
            split(IN_PIECE)
            w2_lo(1)
            split(IN_PIECE + 1)
            xt_lo_part(dve, 0, 0)
            split(IN_PIECE + 2)
            w2_lo(2)
            xt_lo_part(dve, 0, 1)
            split(IN_PIECE + 3)
            xt_lo_part(dve, 0, 2)
            w2_lo(3)
            xt_lo_part(dve, 0, 3)

        prep.close()
        pha = ExitStack()
        ab = sb_in(pha)
        cv = ab("cv", [P, 2, 2 * 3, HALO + HALF], F16)
        tails = ab("tails", [P, GROUPS, 2 * 3, HALO], F16)
        dif = ab("dif", [P, HALF])
        q2b = ab("q2b", [P, HALF])
        gate = ab("gate", [P, 2, TILE])
        hh = ab("hh", [P, 2, TILE])
        sq = ab("sq", [P, 2, TILE])
        hsum, qsum = ab("hsum", [P, TILE]), ab("qsum", [P, TILE])
        hT = ab("hT", [P, 2, KI, TILE], F16)
        mneg, v2 = hsum, qsum
        tmp2 = ab("tmp2", [P, TILE])
        vd, r2 = ab("vd", [P, SUBS]), ab("r2", [P, SUBS])
        tb = ab("tb", [P, 2, TILE])
        mm_s = ab("mm_s", [P, 2, TILE])
        mT = ab("mT", [P, 2, KD, TILE], F16)


        def a_sp(sp):
            def tile(b, half, rows):
                t = HALVES * b + half
                sp.wait_ge(x1_done, SUBS * t + SUBS)
                sp.dma_start(x1_dram[t], xs[:, half, :, :]).then_inc(x1_stored, 16)
                sp.wait_ge(x1_stored, 16 * t + 16)
                sp.dma_start(xs[:, half, :, :], rows).then_inc(x_landed[half], 16)

            for half in range(HALVES):
                tile(0, half, x_v[1, half])
            with sp.Fori(1, B - 1) as b:
                for half in range(HALVES):
                    tile(b, half, x_v[b + 1, half])
            tile(B - 1, 0, x1_dram[0])
            sp.wait_ge(ipg, TILES * GROUPS)
            sp.dma_start(m_w[:, 0], m_dram[0]).then_inc(m_landed[0], 16)
            sp.wait_ge(conv_done, TILES * GROUPS)
            for n in range(B):
                if n == B // 2:
                    sp.wait_ge(fc_done, TILES * SUBS)
                sp.dma_start(vw_w[:, n], vw_dram[n]).then_inc(vw_landed[min(n, 1)], 16)
                if n + 1 < B:
                    sp.dma_start(m_w[:, n + 1], m_dram[n + 1]).then_inc(m_landed[1], 16)
            tile(B - 1, 1, x1_dram[1])

        def a_pe(pe):
            def in_proj(t, g, gate_half):
                o = bank[1 if gate_half else 0]
                if g == 0:
                    at_least(pe, t_done, SUBS * t)
                    if not gate_half:
                        pe.wait_ge(xt_lo, SUBS * t + SUBS)
                elif gate_half:
                    pe.wait_ge(gate_done, GROUPS * t + g)
                else:
                    pe.wait_ge(p_lo_done, GROUPS * t + g)
                    pe.wait_ge(d_done, GROUPS * t + g)
                c = (I if gate_half else 0) + g * P
                product3(pe, o[:, :], [(in_w[:, 0, k, c:c + P], in_w[:, 1, k, c:c + P],
                                        xT[:, 0, k, :], xT[:, 1, k, :]) for k in range(KD)])\
                    .then_inc(ipg if gate_half else iph, 1)

            def conv(t, g):
                q23, q1 = bank[CONV_BANK[g % 2][0]], bank[CONV_BANK[g % 2][1]]
                if g < 2:
                    at_least(pe, x1_done, SUBS * t)
                else:
                    pe.wait_ge(h_done, GROUPS * t + g - 1)
                pe.wait_ge(p_halo, GROUPS * t + g + 1)
                pe.wait_ge(p_ready, GROUPS * t + g + 1)

                def taps(w, k0, step, row, c0, n):
                    return [(w[:, 0, g, k0 + step * i, :], w[:, 1, g, k0 + step * i, :],
                             cv[:, g % 2, row, c0 + i:c0 + i + n], cv[:, g % 2, 3 + row, c0 + i:c0 + i + n])
                            for i in range(2)]

                product3(pe, q1[:, 0:HALF + 1], taps(conv_w, 0, 2, 1, 0, HALF + 1))
                product3(pe, q23[:, 0:HALF], taps(conv_w, 1, 2, 0, 1, HALF))
                product3(pe, q23[:, HALF:TILE], taps(conv_d, 0, 1, 2, 1, HALF)).then_inc(conv_done, 1)

            def fc(t, s, groups):
                if groups[0] == 0:
                    if s == 0:
                        pe.wait_ge(p_lo_done, GROUPS * t + GROUPS)
                        pe.wait_ge(d_done, GROUPS * t + GROUPS)
                    elif s == 1:
                        pe.wait_ge(gate_done, GROUPS * t + GROUPS)
                    else:
                        pe.wait_ge(h_done, GROUPS * t + GROUPS - 3 + s)
                for g in groups:
                    if s == 0:
                        pe.wait_ge(h_lo, GROUPS * t + g + 1)
                    r = slice(s * P, (s + 1) * P)
                    mm = product3(pe, bank[s][:, :], [(fc_w[:, 0, g, r], fc_w[:, 1, g, r],
                                                       hT[:, 0, g, :], hT[:, 1, g, :])],
                                  start=(g == 0), stop=(g == KI - 1))
                if groups[-1] == KI - 1:
                    mm.then_inc(fc_done, 1)

            def stats(t):
                pe.wait_ge(h_sum, GROUPS * t + GROUPS)
                pe.wait_ge(q_sum, GROUPS * t + GROUPS)
                for o, v in ((SUM_B, hsum), (SQ_B, qsum)):
                    mm = pe.matmul(o[:, :], ones1[:, :].to_broadcast([P, P]), v[:, :], start=True, stop=True)
                mm.then_inc(stats_done, 1)

            def factor_rows(t):
                pe.wait_ge(ln2_r, t + 1)
                pe.wait_ge(ln2_e2, t + 1)
                for s in range(SUBS):
                    mm = pe.matmul(SQ_B[:, s * P:(s + 1) * P], r2[:, s:s + 1].to_broadcast([P, P]), ident[:, :],
                                   start=True, stop=True)
                mm.then_inc(r2_row, 1)

            def out_h(t, s):
                if s == 1:
                    pe.wait_ge(ln2_mneg, t + 1)
                elif s >= 2:
                    pe.wait_ge(t_done, SUBS * t + s + 1)
                r = slice(s * P, (s + 1) * P)
                mm = product3(pe, bank[OUT_BANK[s]][:, :],
                              [(hT[:, 0, g, r], hT[:, 1, g, r], out_w[:, 0, g, :], out_w[:, 1, g, :])
                               for g in range(KI)], stop=False)
                if s == SUBS - 1:
                    mm.then_inc(h_used, 1)

            def out_m(t, s):
                if s == 0:
                    pe.wait_ge(mt_lo, KD * t + KD)
                r = slice(s * P, (s + 1) * P)
                product3(pe, bank[OUT_BANK[s]][:, :],
                         [(mT[:, 0, k, r], mT[:, 1, k, r], w2[:, 0, k, :], w2[:, 1, k, :])
                          for k in range(KD)], start=False).then_inc(out_done, 1)

            def tile(b, half):
                t = HALVES * b + half
                for g in range(GROUPS + 1):
                    if g < GROUPS:
                        in_proj(t, g, False)
                        in_proj(t, g, True)
                    if g >= 1:
                        conv(t, g - 1)
                for groups in (range(KI - 1), range(KI - 1, KI)):
                    fc(t, 0, groups)
                    fc(t, 1, groups)
                stats(t)
                fc(t, 2, range(KI))
                fc(t, 3, range(KI))
                factor_rows(t)
                for s in range(SUBS):
                    transpose_x(pe, t + 1, s)
                    out_h(t, s)
                for s in range(SUBS):
                    out_m(t, s)

            pe.wait_ge(p_vec, 1)
            for half in range(HALVES):
                tile(0, half)
            with pe.Fori(1, B - 1) as b:
                for half in range(HALVES):
                    tile(b, half)
            for half in range(HALVES):
                tile(B - 1, half)

        def a_act(act):
            def mid_part(t, m):
                n = KD * t + m
                act.wait_ge(u_done, n + 1)
                at_least(act, mt_lo, KD * t + max(m - 1, 0))
                act.activation(mm_s[:, m % 2, :], tb[:, m % 2, :], ACT.Silu, bias=fc_bs[:, m:m + 1], scale=1.0)\
                   .then_inc(silu_done, 1)
                act.wait_ge(silu_done, n + 1)
                at_least(act, out_done, SUBS * t)
                act.activation(mT[:, 0, m, :], mm_s[:, m % 2, :], ACT.Copy, scale=MID_SCALE).then_inc(mt_hi, 1)

            def tile(b, half):
                t = HALVES * b + half
                for g in range(GROUPS + 1):
                    if g < GROUPS:
                        before = GROUPS * t + max(g - 1, 0)
                        act.wait_ge(iph, GROUPS * t + g + 1)
                        at_least(act, conv_done, before)
                        act.activation(cv[:, g % 2, 0:2, HALO:HALO + HALF],
                                       bank[0][:, :].rearrange("p (i q) -> p q i", q=2), ACT.Copy,
                                       scale=P_SCALE / (W_SCALE * LN_SCALE))
                        at_least(act, d_lo, GROUPS * t + g)
                        act.activation(dif[:, :], bank[0][:, :].rearrange("p (i q) -> p q i", q=2)[:, 1, :],
                                       ACT.Copy).then_inc(p_hi_done, 1)
                        act.wait_ge(d_done, GROUPS * t + g + 1)
                        act.activation(cv[:, g % 2, 2, HALO:HALO + HALF], dif[:, :], ACT.Copy,
                                       scale=P_SCALE / (W_SCALE * LN_SCALE)).then_inc(d_hi, 1)
                        act.wait_ge(ipg, GROUPS * t + g + 1)
                        at_least(act, h_done, before)
                        act.activation(gate[:, g % 2, :], bank[1][:, :], ACT.Silu,
                                       scale=1.0 / (W_SCALE * LN_SCALE)).then_inc(gate_done, 1)
                    if g >= 1:
                        q = g - 1
                        act.wait_ge(conv_done, GROUPS * t + q + 1)
                        at_least(act, o_done, GROUPS * t + q)
                        act.activation(q2b[:, :], bank[CONV_BANK[q % 2][0]][:, 0:HALF], ACT.Identity,
                                       bias=conv_bs[:, q:q + 1], scale=1.0).then_inc(q2_done, 1)
                        act.wait_ge(h_done, GROUPS * t + q + 1)
                        if q == 0:
                            at_least(act, h_used, t)
                        act.activation(hT[:, 0, q, :], hh[:, q % 2, :], ACT.Copy,
                                       scale=H_SCALE / (P_SCALE * W_SCALE)).then_inc(h_hi, 1)
                        at_least(act, q_sum, GROUPS * t + max(q - 1, 0))
                        act.activation(sq[:, q % 2, :], hh[:, q % 2, :], ACT.Square,
                                       scale=1.0 / (P_SCALE * W_SCALE)).then_inc(h_sq, 1)
                for s in range(SUBS):
                    normalise_x(act, t + 1, 1 - half, s)
                mid_part(t, 0)
                xt_hi_part(act, t + 1, 0)
                mid_part(t, 1)
                xt_hi_part(act, t + 1, 1)
                mid_part(t, 2)
                xt_hi_part(act, t + 1, 2)
                mid_part(t, 3)
                xt_hi_part(act, t + 1, 3)

            prep_over(act)
            for half in range(HALVES):
                tile(0, half)
            with act.Fori(1, B - 1) as b:
                for half in range(HALVES):
                    tile(b, half)
            for half in range(HALVES):
                tile(B - 1, half)

        def a_dve(dve):
            def p_part(t, half, g):
                n = GROUPS * t + g + 1
                sl = g % 2
                at_least(dve, conv_done, GROUPS * t + max(g - 1, 0))
                if half == 0:
                    dve.memset(cv[:, sl, :, 0:HALO], 0.0).then_inc(p_halo, 1)
                else:
                    dve.tensor_copy(cv[:, sl, :, 0:HALO], tails[:, g, :, :]).then_inc(p_halo, 1)
                dve.wait_ge(p_hi_done, n)
                tokens = bank[0][:, :].rearrange("p (i q) -> p q i", q=2)
                dve.tensor_tensor(dif[:, :], tokens[:, 0, :], dif[:, :], ALU.subtract).then_inc(d_done, 1)
                for q in range(2):
                    ins = dve.scalar_tensor_tensor(cv[:, sl, 3 + q, HALO:HALO + HALF], tokens[:, q, :],
                                                   P_SCALE / (W_SCALE * LN_SCALE), cv[:, sl, q, HALO:HALO + HALF],
                                                   ALU.mult, ALU.subtract)
                ins.then_inc(p_lo_done, 1)

            def d_part(t, g):
                n = GROUPS * t + g + 1
                sl = g % 2
                dve.wait_ge(d_hi, n)
                dve.scalar_tensor_tensor(cv[:, sl, 5, HALO:HALO + HALF], dif[:, :], P_SCALE / (W_SCALE * LN_SCALE),
                                         cv[:, sl, 2, HALO:HALO + HALF], ALU.mult, ALU.subtract).then_inc(d_lo, 1)
                dve.wait_ge(d_lo, n)
                dve.wait_ge(p_lo_done, n)
                dve.wait_ge(p_halo, n)
                dve.tensor_copy(tails[:, g, :, :], cv[:, sl, :, HALF:HALF + HALO]).then_inc(p_ready, 1)

            def h_part(t, g):
                n = GROUPS * t + g + 1
                before = GROUPS * t + max(g - 1, 0)
                q23, q1 = bank[CONV_BANK[g % 2][0]], bank[CONV_BANK[g % 2][1]]
                dve.wait_ge(conv_done, n)
                dve.wait_ge(q2_done, n)
                at_least(dve, h_hi, before)
                at_least(dve, h_sq, before)
                at_least(dve, h_sum, before)
                at_least(dve, h_lo, before)
                eo = hh[:, g % 2, :].rearrange("p (i q) -> p q i", q=2)
                dve.tensor_tensor(eo[:, 0, :], q1[:, 0:HALF], q2b[:, :], ALU.add)
                dve.tensor_tensor(eo[:, 1, :], q1[:, 1:HALF + 1], q2b[:, :], ALU.add).then_inc(o_done, 1)
                dve.wait_ge(o_done, n)
                dve.tensor_tensor(eo[:, 1, :], q23[:, HALF:TILE], eo[:, 1, :], ALU.add).then_inc(eo_done, 1)
                dve.wait_ge(gate_done, n)
                dve.wait_ge(eo_done, n)
                dve.tensor_tensor(hh[:, g % 2, :], hh[:, g % 2, :], gate[:, g % 2, :], ALU.mult).then_inc(h_done, 1)

            def h_lo_part(t, g):
                dve.wait_ge(h_hi, GROUPS * t + g + 1)
                dve.scalar_tensor_tensor(hT[:, 1, g, :], hh[:, g % 2, :], H_SCALE / (P_SCALE * W_SCALE),
                                         hT[:, 0, g, :], ALU.mult, ALU.subtract).then_inc(h_lo, 1)

            def ln2_stats(t):
                dve.wait_ge(stats_done, t + 1)
                dve.tensor_scalar(mneg[:, :], SUM_B[:, :], -1.0 / (P_SCALE * W_SCALE * I), None, ALU.mult)\
                   .then_inc(ln2_mneg, 1)
                dve.tensor_scalar(v2[:, :], SQ_B[:, :], FC_SQ / I, EPS * FC_SQ, ALU.mult, ALU.add).then_inc(ln2_e2, 1)
                dve.wait_ge(ln2_mneg, t + 1)
                dve.scalar_tensor_tensor(tmp2[:, :], mneg[:, :], FC_SQ, mneg[:, :], ALU.mult, ALU.mult)\
                   .then_inc(ln2_msq, 1)
                dve.wait_ge(ln2_msq, t + 1)
                dve.wait_ge(ln2_e2, t + 1)
                dve.tensor_tensor(v2[:, :], v2[:, :], tmp2[:, :], ALU.subtract).then_inc(ln2_v, 1)
                dve.wait_ge(ln2_v, t + 1)
                by_sub = [v[:, :].rearrange("p (s n) -> p s n", s=SUBS) for v in (tmp2, v2)]
                dve.tensor_tensor(by_sub[0], by_sub[1], ident[:, :].unsqueeze(1).to_broadcast([P, SUBS, P]), ALU.mult)\
                   .then_inc(diag_done, 1)
                dve.wait_ge(diag_done, t + 1)
                dve.tensor_reduce(vd[:, :], by_sub[0], AX.X, ALU.add).then_inc(vd_done, 1)

            def tu(t, s):
                n = KD * t + s + 1
                dve.wait_ge(fc_done, n)
                at_least(dve, silu_done, KD * t + max(s - 1, 0))
                dve.scalar_tensor_tensor(tb[:, s % 2, :], mneg[:, :], fc_g[:, s:s + 1], bank[s][:, :],
                                         ALU.mult, ALU.add).then_inc(t_done, 1)
                if s == 0:
                    dve.wait_ge(r2_row, t + 1)
                dve.wait_ge(t_done, n)
                dve.tensor_tensor(tb[:, s % 2, :], tb[:, s % 2, :], SQ_B[:, :], ALU.mult).then_inc(u_done, 1)

            def mt_lo_part(t, m):
                dve.wait_ge(mt_hi, KD * t + m + 1)
                dve.scalar_tensor_tensor(mT[:, 1, m, :], mm_s[:, m % 2, :], MID_SCALE, mT[:, 0, m, :],
                                         ALU.mult, ALU.subtract).then_inc(mt_lo, 1)

            def x1_part(t, half, s):
                dve.wait_ge(out_done, SUBS * t + s + 1)
                if s == 0:
                    dve.wait_ge(resid_done, SUBS * t + SUBS)
                dve.scalar_tensor_tensor(xs[:, half, s, :], bank[OUT_BANK[s]][:, :], 1.0 / (H_SCALE * W_SCALE),
                                         xs[:, half, s, :], ALU.mult, ALU.add).then_inc(x1_done, 1)

            def tile(b, half):
                t = HALVES * b + half
                for g in range(GROUPS + 1):
                    if g < GROUPS:
                        p_part(t, half, g)
                        d_part(t, g)
                    if 2 <= g < 2 + SUBS:
                        ln_stats(dve, t + 1, 1 - half, g - 2, b + half)
                    if g == 2 + SUBS:
                        ln_var(dve, t + 1)
                    if g >= 1:
                        h_part(t, g - 1)
                        h_lo_part(t, g - 1)
                ln2_stats(t)
                tu(t, 0)
                tu(t, 1)
                mt_lo_part(t, 0)
                xt_lo_part(dve, t + 1, 0)
                tu(t, 2)
                mt_lo_part(t, 1)
                xt_lo_part(dve, t + 1, 1)
                tu(t, 3)
                mt_lo_part(t, 2)
                xt_lo_part(dve, t + 1, 2)
                mt_lo_part(t, 3)
                xt_lo_part(dve, t + 1, 3)
                for s in range(SUBS):
                    x1_part(t, half, s)

            prep_over(dve)
            for half in range(HALVES):
                tile(0, half)
            with dve.Fori(1, B - 1) as b:
                for half in range(HALVES):
                    tile(b, half)
            for half in range(HALVES):
                tile(B - 1, half)

        def a_pool(pool):
            def tile(b, half, last=False):
                t = HALVES * b + half
                for g in range(GROUPS):
                    n = GROUPS * t + g
                    pool.wait_ge(h_done, n + 1)
                    if g == 0:
                        at_least(pool, u_done, KD * t)
                        pool.tensor_tensor(hsum[:, :], zero[:, :], hh[:, 0, :], ALU.add).then_inc(h_sum, 1)
                        pool.wait_ge(h_sq, n + 1)
                        pool.tensor_tensor(qsum[:, :], zero[:, :], sq[:, 0, :], ALU.add).then_inc(q_sum, 1)
                    else:
                        pool.wait_ge(h_sum, n)
                        pool.tensor_tensor(hsum[:, :], hsum[:, :], hh[:, g % 2, :], ALU.add).then_inc(h_sum, 1)
                        pool.wait_ge(h_sq, n + 1)
                        pool.wait_ge(q_sum, n)
                        pool.tensor_tensor(qsum[:, :], qsum[:, :], sq[:, g % 2, :], ALU.add).then_inc(q_sum, 1)
                    if g == GROUPS - 1:
                        ln_factors(pool, t + 1)
                pool.wait_ge(vd_done, t + 1)
                pool.tensor_tensor(r2[:, :], vd[:, :], mhalf[:, :], ALU.pow).then_inc(ln2_r, 1)
                if not last:
                    residual(pool, t + 1, 1 - half)

            pool.wait_ge(p_evac, JOBS)
            residual(pool, 0, 0)
            prep_over(pool)
            for half in range(HALVES):
                tile(0, half)
            with pool.Fori(1, B - 1) as b:
                for half in range(HALVES):
                    tile(b, half)
            tile(B - 1, 0)
            tile(B - 1, 1, last=True)

        pha.close()
        mid_stack.close()

        phb = ExitStack()
        cb_ = sb_in(phb)
        RING = BSUBS
        xr = xs[:, :, :, :].rearrange("p h s d -> p (h s) d")
        we_w = cb_("we_w", [P, 2, KD, D], F16)
        wg_w = cb_("wg_w", [P, 2, KD, E], F16)
        we_raw = cb_("we_raw", [P, KD, D])
        wg_raw = cb_("wg_raw", [P, KD, E])
        be_row = cb_("be_row", [P, D])
        gbe = cb_("gbe", [P, D])
        maskb = cb_("maskb", [P, NSUB, KEYS])
        bn2, mv2, va2, rs2 = cb_("bn2", [P, 6]), cb_("mv2", [P, 2, 2]), cb_("va2", [P, 2]), cb_("rs2", [P, 2])
        bn3, mv3, va3, rs3 = cb_("bn3", [P, 6]), cb_("mv3", [P, 2, 2]), cb_("va3", [P, 2]), cb_("rs3", [P, 2])
        nm2, nb2 = cb_("nm2", [P, 2]), cb_("nb2", [P, 2])
        nm3, nb3 = cb_("nm3", [P, 2]), cb_("nb3", [P, 2])
        xn2, xn3 = cb_("xn2", [P, 2, D]), cb_("xn3", [P, 2, D])
        x2T, x3T = cb_("x2T", [P, 2, 2, KD, P], F16), cb_("x3T", [P, 2, 2, KD, P], F16)
        prT = cb_("prT", [P, 2, 2, PAIRS, P], F16)
        bias = cb_("bias", [P, 2, HEADS, KEYS])
        sc = cb_("sc", [P, 2, HEADS, KEYS])
        ex = cb_("ex", [P, 4, HEADS, KEYS])
        mx, su, ri, rw = (cb_("mx", [P, 2, HEADS]), cb_("su", [P, HEADS]), cb_("ri", [P, HEADS]),
                          cb_("rw", [P, 2, HEADS]))
        lm, nl, eqp, pm = cb_("lm", [P, 1]), cb_("nl", [P, 1]), cb_("eqp", [P, E]), cb_("pm", [P, 1])
        oh, seen = cb_("oh", [P, E], BF16), cb_("seen", [P, E], BF16)
        e8, den, rden = cb_("e8", [P, E]), cb_("den", [P, 1]), cb_("rden", [P, 1])
        kv, kept, gk, gf = cb_("kv", [P, E]), cb_("kept", [P, 1]), cb_("gk", [P, 1]), cb_("gf", [P, 1])

        T2_B, S_B, PT_B, PV_B, T3_B, WE_B, R_B, LOC_B = bank
        S_SCALE = 1.0 / (LN_SCALE * W_SCALE)
        PV_SCALE = 1.0 / (PROB_SCALE * W_SCALE)

        w_landed = {n: sem(f"w_landed_{n}") for n in ("we", "wg", "be")}
        x1_landed = [sem(f"x1_landed{n}") for n in range(RING)]
        out_stored = [sem(f"out_stored{n}") for n in range(RING)]
        c_hi, c_lo, c_mask = sem("c_hi"), sem("c_lo"), sem("c_mask")
        bn2_done, mv2_done, va2_done, rs2_done, xn2_done = (sem("bn2_done"), sem("mv2_done"), sem("va2_done"),
                                                           sem("rs2_done"), sem("xn2_done"))
        bn3_done, mv3_done, va3_done, rs3_done, xn3_done = (sem("bn3_done"), sem("mv3_done"), sem("va3_done"),
                                                           sem("rs3_done"), sem("xn3_done"))
        nm2_done, nb2_done, nm3_done, nb3_done = sem("nm2_done"), sem("nb2_done"), sem("nm3_done"), sem("nb3_done")
        t2_tr, t2_hi, t2_lo = sem("t2_tr"), sem("t2_hi"), sem("t2_lo")
        pt_tr, pt_hi, pt_lo = sem("pt_tr"), sem("pt_hi"), sem("pt_lo")
        t3_tr, t3_hi, t3_lo = sem("t3_tr"), sem("t3_hi"), sem("t3_lo")
        s_done, pv_done, r_done, we_done, loc_done = (sem("s_done"), sem("pv_done"), sem("r_done"),
                                                      sem("we_done"), sem("loc_done"))
        bias_done, sc_done, mx_done, sub_done, ex_done = (sem("bias_done"), sem("sc_done"), sem("mx_done"),
                                                          sem("sub_done"), sem("ex_done"))
        su_done, ri_done, rw_done, pr_done, bo_done = (sem("su_done"), sem("ri_done"), sem("rw_done"),
                                                       sem("pr_done"), sem("bo_done"))
        x2_done, lm_done, nl_done, eqp_done, pm_done, oh_done = (sem("x2_done"), sem("lm_done"), sem("nl_done"),
                                                                 sem("eqp_done"), sem("pm_done"), sem("oh_done"))
        seen_done, den_done, rden_done, kept_done = (sem("seen_done"), sem("den_done"), sem("rden_done"),
                                                     sem("kept_done"))
        gk_done, y_done, gbe_done, yb_done = sem("gk_done"), sem("y_done"), sem("gbe_done"), sem("yb_done")

        LN2_AT, T2_AT, S_AT, PV_AT, WE_AT = 2, 3, 4, 6, 7
        STEPS_TAIL = WE_AT

        def real(j):
            return not isinstance(j, int) or 0 <= j < NSUB

        AHEAD = SUBS

        def fresh(j):
            return not isinstance(j, int) or AHEAD <= j < NSUB

        def a_over(eng):
            eng.wait_ge(x1_done, TILES * SUBS)

        def steps(eng, body, loaded=lambda eng: None):
            for k in range(BSUBS):
                body(0, k, lambda d: k - d)
            loaded(eng)
            with eng.Fori(1, B) as b:
                for k in range(BSUBS):
                    body(b, k, lambda d: b * BSUBS + (k - d))
            for k in range(STEPS_TAIL):
                body(B, k, lambda d: NSUB + k - d)

        def b_sp(sp):
            kn = "(k p) n -> p k n"
            sp.dma_start(wg_raw[:, :, :], Wg.rearrange(kn, p=P)).then_inc(w_landed["wg"], 16)
            sp.dma_start(be_row[:, :], be.partition_broadcast(P)).then_inc(w_landed["be"], 16)
            sp.dma_start(we_raw[:, :, :], We.rearrange(kn, p=P)).then_inc(w_landed["we"], 16)

            def step(b, k, j):
                if not isinstance(b, int):
                    sp.wait_ge(out_stored[k], 16 * b)
                    sp.dma_start(xr[:, k, :], x1_dram[b * HALVES + k // SUBS, :, k % SUBS, :])\
                      .then_inc(x1_landed[k], 16)
                y = j(WE_AT)
                if real(y):
                    sp.wait_ge(yb_done, y + 1)
                    slot = (k - WE_AT) % RING
                    yb = b if k >= WE_AT else b - 1
                    sp.dma_start(out_v[yb * BSUBS + slot], xr[:, slot, :]).then_inc(out_stored[slot], 16)

            steps(sp, step, lambda sp: sp.wait_ge(x1_stored, 16 * TILES))
            for n in range(RING):
                sp.wait_ge(out_stored[n], 16 * B)

        def b_pe(pe):
            def transpose4(dst, src, done):
                for c in range(KD):
                    tr = pe.transpose(dst[:, c * P:(c + 1) * P], src[:, c * P:(c + 1) * P], ident[:, :])
                tr.then_inc(done, 1)

            def pairs(lhs, rhs, chunks):
                return [(lhs[:, 0, c, :], lhs[:, 1, c, :], rhs[:, 0, c, :], rhs[:, 1, c, :])
                        for c in range(chunks)]

            def batch_of(w, b):
                return w[:, b] if isinstance(b, int) else w[:, bass.ds(b, 1)].rearrange("p b t k n -> p (b t) k n")

            def step(b, k, j):
                p, t, s, w = j(PV_AT), j(T2_AT), j(S_AT), j(WE_AT)
                if real(p):
                    if isinstance(b, int) and p == 0:
                        a_over(pe)
                    pe.wait_ge(pr_done, p + 1)
                    at_least(pe, pt_lo, p)
                    transpose4(PT_B, ex[:, (k - PV_AT) % 4, :, :].rearrange("p h n -> p (h n)"), pt_tr)
                if fresh(t):
                    pe.wait_ge(xn2_done, t - AHEAD + 1)
                    at_least(pe, t2_lo, t - AHEAD)
                    transpose4(T2_B, xn2[:, (k - T2_AT) % 2, :], t2_tr)
                if real(w):
                    pe.wait_ge(xn3_done, w + 1)
                    at_least(pe, t3_lo, w)
                    transpose4(T3_B, xn3[:, (k - WE_AT) % 2, :], t3_tr)
                if real(s):
                    sb_ = b if k >= S_AT else b - 1
                    if isinstance(b, int) and s == 0:
                        pe.wait_ge(m_landed[0], 16)
                    if fresh(s):
                        pe.wait_ge(t2_lo, s - AHEAD + 1)
                        rows = x2T[:, (k - S_AT) % 2]
                    else:
                        pe.wait_ge(xt_lo, TILES * SUBS + s + 1)
                        rows = xT[:, :, :, s * P:(s + 1) * P]
                    at_least(pe, sc_done, s)
                    product3(pe, S_B[:, :], pairs(rows, batch_of(m_w, sb_), KD)).then_inc(s_done, 1)
                if real(p):
                    pb_ = b if k >= PV_AT else b - 1
                    if isinstance(b, int) and p == 0:
                        pe.wait_ge(vw_landed[0], 16)
                    pe.wait_ge(pt_lo, p + 1)
                    at_least(pe, x2_done, p)
                    product3(pe, PV_B[:, :], pairs(prT[:, (k - PV_AT) % 2], batch_of(vw_w, pb_), PAIRS))\
                        .then_inc(pv_done, 1)
                if real(w):
                    x3 = x3T[:, (k - WE_AT) % 2]
                    if isinstance(b, int) and w == 0:
                        pe.wait_ge(c_lo, 2)
                    pe.wait_ge(t3_lo, w + 1)
                    at_least(pe, eqp_done, w)
                    at_least(pe, den_done, w)
                    product3(pe, R_B[:, 0:E], pairs(x3, wg_w, KD)).then_inc(r_done, 1)
                    at_least(pe, y_done, w)
                    product3(pe, WE_B[:, :], pairs(x3, we_w, KD)).then_inc(we_done, 1)
                    pe.wait_ge(oh_done, w + 1)
                    at_least(pe, kept_done, w)
                    pe.wait_ge(seen_done, w + 1)
                    pe.matmul(LOC_B[:, 0:E], tri[:, :], oh[:, :], start=True, stop=False)
                    pe.matmul(LOC_B[:, 0:E], ones_b[:, :], seen[:, :], start=False, stop=True)\
                      .then_inc(loc_done, 1)

            def all_loaded(pe):
                pe.wait_ge(m_landed[1], 16 * (B - 1))
                pe.wait_ge(vw_landed[1], 16 * (B - 1))

            steps(pe, step, all_loaded)

        def b_act(act):
            def split_weights():
                act.wait_ge(w_landed["we"], 16)
                act.activation(we_w[:, 0, :, :], we_raw[:, :, :], ACT.Copy, scale=W_SCALE).then_inc(c_hi, 1)
                act.wait_ge(w_landed["wg"], 16)
                act.activation(wg_w[:, 0, :, :], wg_raw[:, :, :], ACT.Copy, scale=W_SCALE).then_inc(c_hi, 1)

            def normalise(n, q, src, xn, rs, nb, nb_done, tr, xn_done):
                act.wait_ge(nb_done, n + 1)
                at_least(act, tr, n - 1)
                act.activation(xn[:, q, :], src, ACT.Identity, bias=nb[:, q:q + 1], scale=rs[:, q:q + 1])\
                   .then_inc(xn_done, 1)

            def hi_part(n, tr, dst, src, done, scale=1.0):
                act.wait_ge(tr, n + 1)
                act.activation(dst, src[:, :].rearrange("p (k n) -> p k n", k=KD), ACT.Copy, scale=scale)\
                   .then_inc(done, 1)

            def step(b, k, j):
                l, p, t, s, w = j(LN2_AT), j(PV_AT), j(T2_AT), j(S_AT), j(WE_AT)
                if real(p):
                    hi_part(p, pt_tr, prT[:, (k - PV_AT) % 2, 0], PT_B, pt_hi, PROB_SCALE)
                if fresh(t):
                    hi_part(t - AHEAD, t2_tr, x2T[:, (k - T2_AT) % 2, 0], T2_B, t2_hi)
                if real(w):
                    hi_part(w, t3_tr, x3T[:, (k - WE_AT) % 2, 0], T3_B, t3_hi)
                if fresh(l):
                    normalise(l - AHEAD, k % 2, xr[:, (k - LN2_AT) % RING, :], xn2, rs2, nb2, nb2_done, t2_tr, xn2_done)
                if real(s):
                    act.wait_ge(sub_done, s + 1)
                    at_least(act, pt_tr, s - 3)
                    act.activation(ex[:, (k - S_AT) % 4, :, :], sc[:, (k - S_AT) % 2, :, :], ACT.Exp)\
                       .then_inc(ex_done, 1)
                if real(p):
                    normalise(p, k % 2, xr[:, (k - PV_AT) % RING, :], xn3, rs3, nb3, nb3_done, t3_tr, xn3_done)
                if real(w):
                    act.wait_ge(r_done, w + 1)
                    act.wait_ge(nl_done, w + 1)
                    act.wait_ge(eqp_done, w + 1)
                    at_least(act, rden_done, w)
                    act.activation(e8[:, :], R_B[:, 0:E], ACT.Exp, bias=nl[:, :], scale=S_SCALE,
                                   accum_out=den[:, :]).then_inc(den_done, 1)
                if isinstance(b, int) and s == 2:
                    split_weights()

            steps(act, step)

        def b_pool(pool):
            a_over(pool)

            def factors(n, q, va, nm, rs, nb, va_done, nm_done, rs_done, xn_done, nb_done):
                pool.wait_ge(va_done, n + 1)
                pool.wait_ge(nm_done, n + 1)
                at_least(pool, xn_done, n - 1)
                pool.tensor_tensor(rs[:, q:q + 1], va[:, q:q + 1], mhalf[:, 0:1], ALU.pow).then_inc(rs_done, 1)
                pool.wait_ge(rs_done, n + 1)
                pool.tensor_tensor(nb[:, q:q + 1], nm[:, q:q + 1], rs[:, q:q + 1], ALU.mult).then_inc(nb_done, 1)

            def step(b, k, j):
                l, t, s, p, w = j(LN2_AT), j(T2_AT), j(S_AT), j(PV_AT), j(WE_AT)
                if fresh(l):
                    factors(l - AHEAD, k % 2, va2, nm2, rs2, nb2, va2_done, nm2_done, rs2_done, xn2_done, nb2_done)
                if real(t):
                    q = (k - T2_AT) % 2
                    tb_ = b if k >= T2_AT else b - 1
                    at_least(pool, sc_done, t - 1)
                    pool.tensor_tensor(bias[:, q, :, :],
                                       hbias[:, tb_, :].rearrange("p (h n) -> p h n", h=HEADS),
                                       maskb[:, t, :].unsqueeze(1).to_broadcast([P, HEADS, KEYS]), ALU.add)\
                        .then_inc(bias_done, 1)
                if real(s):
                    q = (k - S_AT) % 2
                    pool.wait_ge(mx_done, s + 1)
                    pool.tensor_tensor(sc[:, q, :, :], sc[:, q, :, :],
                                       mx[:, q, :].unsqueeze(2).to_broadcast([P, HEADS, KEYS]),
                                       ALU.subtract).then_inc(sub_done, 1)
                if real(p):
                    factors(p, k % 2, va3, nm3, rs3, nb3, va3_done, nm3_done, rs3_done, xn3_done, nb3_done)
                if real(s):
                    q = (k - S_AT) % 4
                    pool.wait_ge(rw_done, s + 1)
                    pool.tensor_tensor(ex[:, q, :, :], ex[:, q, :, :],
                                       rw[:, (k - S_AT) % 2, :].unsqueeze(2).to_broadcast([P, HEADS, KEYS]),
                                       ALU.mult).then_inc(pr_done, 1)
                if real(l):
                    if fresh(l):
                        pool.wait_ge(xn2_done, l - AHEAD + 1)
                    else:
                        pool.wait_ge(xn_done, TILES * SUBS + l + 1)
                    r = xr[:, (k - LN2_AT) % RING, :]
                    pool.tensor_tensor(r, r, bo_row[:, :], ALU.add).then_inc(bo_done, 1)
                if real(w):
                    if isinstance(b, int) and w == 0:
                        pool.wait_ge(w_landed["be"], 16)
                    pool.wait_ge(gk_done, w + 1)
                    at_least(pool, yb_done, w)
                    pool.tensor_tensor(gbe[:, :], be_row[:, :], gf[:, :].to_broadcast([P, D]), ALU.mult)\
                        .then_inc(gbe_done, 1)
                    pool.wait_ge(gbe_done, w + 1)
                    pool.wait_ge(y_done, w + 1)
                    r = xr[:, (k - WE_AT) % RING, :]
                    pool.tensor_tensor(r, r, gbe[:, :], ALU.add).then_inc(yb_done, 1)

            pool.wait_ge(c_mask, 1)
            pool.wait_ge(landed["small"], 16 * SMALL)
            steps(pool, step)

        def b_dve(dve):
            a_over(dve)
            dve.tensor_scalar(maskb[:, :, :], masku[:, :, :], BIG, -BIG, ALU.mult, ALU.add).then_inc(c_mask, 1)
            dve.memset(seen[:, :], 0.0).then_inc(seen_done, 1)

            def split_weights():
                dve.wait_ge(c_hi, 1)
                dve.scalar_tensor_tensor(we_w[:, 1, :, :].rearrange("p k n -> p (k n)"),
                                         we_raw[:, :, :].rearrange("p k n -> p (k n)"), W_SCALE,
                                         we_w[:, 0, :, :].rearrange("p k n -> p (k n)"),
                                         ALU.mult, ALU.subtract).then_inc(c_lo, 1)
                dve.wait_ge(c_hi, 2)
                dve.scalar_tensor_tensor(wg_w[:, 1, :, :], wg_raw[:, :, :], W_SCALE, wg_w[:, 0, :, :],
                                         ALU.mult, ALU.subtract).then_inc(c_lo, 1)

            def stats(n, q, src, bn_, mv, nm, va, bn_done, mv_done, nm_done, va_done, nb_done):
                dve.bn_stats(bn_[:, :], src).then_inc(bn_done, 1)
                carry(dve, pad_dve[:, :], (bn_done, n + 1))
                dve.bn_aggr(mv[:, q, :], bn_[:, :]).then_inc(mv_done, 1)
                dve.wait_ge(mv_done, n + 1)
                at_least(dve, nb_done, n - 1)
                dve.tensor_scalar(nm[:, q:q + 1], mv[:, q, 0:1], -1.0, None, ALU.mult).then_inc(nm_done, 1)
                dve.tensor_scalar(va[:, q:q + 1], mv[:, q, 1:2], EPS, LN_SCALE ** -2, ALU.add, ALU.mult)\
                   .then_inc(va_done, 1)

            def lo_part(n, hi, slot, src, done, scale=1.0):
                dve.wait_ge(hi, n + 1)
                dve.scalar_tensor_tensor(slot[:, 1], src[:, :].rearrange("p (k n) -> p k n", k=KD), scale,
                                         slot[:, 0], ALU.mult, ALU.subtract).then_inc(done, 1)

            def step(b, k, j):
                l, t, s, p, w = j(LN2_AT), j(T2_AT), j(S_AT), j(PV_AT), j(WE_AT)
                if real(p):
                    lo_part(p, pt_hi, prT[:, (k - PV_AT) % 2], PT_B, pt_lo, PROB_SCALE)
                if fresh(t):
                    lo_part(t - AHEAD, t2_hi, x2T[:, (k - T2_AT) % 2], T2_B, t2_lo)
                if real(w):
                    lo_part(w, t3_hi, x3T[:, (k - WE_AT) % 2], T3_B, t3_lo)
                if fresh(l):
                    slot = (k - LN2_AT) % RING
                    lb = b if k >= LN2_AT else b - 1
                    if isinstance(lb, int) and lb == 0:
                        dve.wait_ge(x_landed[1], 16 * (B + 1))
                    else:
                        at_least(dve, x1_landed[slot], 16 * lb)
                    stats(l - AHEAD, k % 2, xr[:, slot, :], bn2, mv2, nm2, va2, bn2_done, mv2_done, nm2_done,
                          va2_done, nb2_done)
                if real(s):
                    q = (k - S_AT) % 2
                    dve.wait_ge(s_done, s + 1)
                    dve.wait_ge(bias_done, s + 1)
                    at_least(dve, ex_done, s - 1)
                    dve.scalar_tensor_tensor(sc[:, q, :, :].rearrange("p h n -> p (h n)"), S_B[:, :], S_SCALE,
                                             bias[:, q, :, :].rearrange("p h n -> p (h n)"),
                                             ALU.mult, ALU.add).then_inc(sc_done, 1)
                if real(s):
                    q = (k - S_AT) % 2
                    dve.wait_ge(sc_done, s + 1)
                    at_least(dve, sub_done, s - 1)
                    dve.tensor_reduce(mx[:, q, :], sc[:, q, :, :], AX.X, ALU.max).then_inc(mx_done, 1)
                if real(p):
                    r = xr[:, (k - PV_AT) % RING, :]
                    dve.wait_ge(pv_done, p + 1)
                    dve.wait_ge(bo_done, p + 1)
                    dve.scalar_tensor_tensor(r, PV_B[:, :], PV_SCALE, r, ALU.mult, ALU.add).then_inc(x2_done, 1)
                    dve.wait_ge(x2_done, p + 1)
                    stats(p, k % 2, r, bn3, mv3, nm3, va3, bn3_done, mv3_done, nm3_done, va3_done, nb3_done)
                if real(w):
                    dve.wait_ge(r_done, w + 1)
                    dve.tensor_reduce(lm[:, :], R_B[:, 0:E], AX.X, ALU.max).then_inc(lm_done, 1)
                    dve.wait_ge(lm_done, w + 1)
                    at_least(dve, den_done, w)
                    dve.tensor_scalar(nl[:, :], lm[:, :], -S_SCALE, None, ALU.mult).then_inc(nl_done, 1)
                    dve.scalar_tensor_tensor(eqp[:, :], R_B[:, 0:E], lm[:, :], prio[:, :],
                                             ALU.is_equal, ALU.mult).then_inc(eqp_done, 1)
                    dve.wait_ge(eqp_done, w + 1)
                    dve.tensor_reduce(pm[:, :], eqp[:, :], AX.X, ALU.max).then_inc(pm_done, 1)
                    dve.wait_ge(pm_done, w + 1)
                    at_least(dve, loc_done, w)
                    at_least(dve, kept_done, w)
                    dve.tensor_scalar(oh[:, :], eqp[:, :], pm[:, :], None, ALU.is_equal).then_inc(oh_done, 1)
                if real(s):
                    dve.wait_ge(ex_done, s + 1)
                    dve.tensor_reduce(su[:, :], ex[:, (k - S_AT) % 4, :, :], AX.X, ALU.add).then_inc(su_done, 1)
                    dve.wait_ge(su_done, s + 1)
                    dve.reciprocal(ri[:, :], su[:, :]).then_inc(ri_done, 1)
                    dve.wait_ge(ri_done, s + 1)
                    at_least(dve, pr_done, s - 1)
                    dve.tensor_scalar(rw[:, (k - S_AT) % 2, :], ri[:, :], attends[:, bass.ds(s, 1)], None,
                                      ALU.mult).then_inc(rw_done, 1)
                if isinstance(b, int) and s == 2:
                    split_weights()
                if real(w):
                    dve.wait_ge(den_done, w + 1)
                    dve.reciprocal(rden[:, :], den[:, :]).then_inc(rden_done, 1)
                    dve.wait_ge(loc_done, w + 1)
                    dve.scalar_tensor_tensor(kv[:, :], LOC_B[:, 0:E], float(CAP), oh[:, :], ALU.is_le, ALU.mult,
                                             accum_out=kept[:, :]).then_inc(kept_done, 1)
                    dve.tensor_tensor(seen[:, :], seen[:, :], oh[:, :], ALU.add).then_inc(seen_done, 1)
                    dve.wait_ge(kept_done, w + 1)
                    dve.wait_ge(rden_done, w + 1)
                    at_least(dve, gbe_done, w)
                    dve.tensor_tensor(gf[:, :], kept[:, :], rden[:, :], ALU.mult)
                    dve.scalar_tensor_tensor(gk[:, :], kept[:, :], S_SCALE, rden[:, :], ALU.mult, ALU.mult)\
                       .then_inc(gk_done, 1)
                    dve.wait_ge(we_done, w + 1)
                    dve.wait_ge(gk_done, w + 1)
                    r = xr[:, (k - WE_AT) % RING, :]
                    dve.scalar_tensor_tensor(r, WE_B[:, :], gk[:, :], r, ALU.mult, ALU.add).then_inc(y_done, 1)

            steps(dve, step)

        with nc.Block() as block:
            @block.sync
            def _(sp):
                prep_sp(sp)
                a_sp(sp)
                b_sp(sp)

            @block.tensor
            def _(pe):
                prep_pe(pe)
                a_pe(pe)
                b_pe(pe)

            @block.scalar
            def _(act):
                prep_act(act)
                a_act(act)
                b_act(act)

            @block.vector
            def _(dve):
                prep_dve(dve)
                a_dve(dve)
                b_dve(dve)

            @block.gpsimd
            def _(pool):
                prep_pool(pool)
                a_pool(pool)
                b_pool(pool)
        phb.close()


def kernel(**inputs):
    import numpy as _np
    import concourse.bacc as _bacc
    from concourse import mybir as _mybir
    from concourse.bass_utils import run_bass_kernel_spmd as _run

    g = {n: _np.asarray(v) for n, v in inputs.items()}

    def columns(v):
        return v.reshape(-1, P).T

    conv = g["L0_attn_conv_w"].reshape(GROUPS, P, P, TAPS)
    layout = {
        "x": g["x"],
        "ctxT": g["ctx_1024"].reshape(B * KEYS, D).T,
        "mask": g["mask_BxSxS2_bk0"].reshape(NSUB, P, KEYS).transpose(1, 0, 2),
        "in_wT": g["L0_attn_in_proj_w"].T,
        "conv_wT": conv.transpose(2, 0, 3, 1).reshape(P, GROUPS * TAPS * P),
        "conv_b": columns(g["L0_attn_conv_b"]),
        "ln_g": columns(g["L0_attn_ln_g"]),
        "ln_b": columns(g["L0_attn_ln_b"]),
        "fc_wT": g["L0_attn_fc_w"].T,
        "fc_b": columns(g["L0_attn_fc_b"]),
        "cproj_w": g["L0_attn_cproj_w"],
        "cproj_b": columns(g["L0_attn_cproj_b"]),
        "out_wT": g["L0_attn_out_w"].T,
        "WqT": g["L0_xattn_Wq"].T,
        "bq": columns(g["L0_xattn_bq"]),
        "Wk": g["L0_xattn_Wk"],
        "bk": columns(g["L0_xattn_bk"]),
        "Wv": g["L0_xattn_Wv"],
        "bv": columns(g["L0_xattn_bv"]),
        "Wo": g["L0_xattn_Wo"],
        "bo": g["L0_xattn_bo"],
        "Wg": g["L0_ffn_Wg"],
        "We": g["L0_ffn_We"],
        "be": g["L0_ffn_be"],
        "ident": _np.eye(P, dtype=_np.float32),
        "tri": _np.triu(_np.ones((P, P), _np.float32)),
        "prio": _np.tile(_np.arange(E, 0, -1, dtype=_np.float32), (P, 1)),
    }
    nc = _bacc.Bacc("TRN2", target_bir_lowering=False, num_devices=1)
    arrays, args = {}, []
    for name, a in layout.items():
        a = _np.ascontiguousarray(a)
        arrays[f"in_{name}_dram"] = a
        args.append(nc.dram_tensor(f"in_{name}_dram", a.shape, _mybir.dt.from_np(a.dtype), kind="ExternalInput").ap())
    args.append(nc.dram_tensor("out_0_dram", (B, S, D), F32, kind="ExternalOutput").ap())
    bass_decoder_kernel(nc, *args)
    r = _run(nc, [arrays], core_ids=[0])
    return r.results[0]["out_0_dram"]
```
